# Optimizing a Trainium2 kernel written in Bass

```python
import numpy as np
import jax
import jax.numpy as jnp

def _softmax(x, axis=-1):
    return jax.nn.softmax(x, axis=axis)

def _gelu(x):
    return jax.nn.gelu(x, approximate=True)

def _silu(x):
    return jax.nn.silu(x)

def _sigmoid(x):
    return jax.nn.sigmoid(x)

def _layernorm(x, axis=-1, eps=1e-05):
    m = jnp.mean(x, axis=axis, keepdims=True)
    v = jnp.var(x, axis=axis, keepdims=True)
    return (x - m) / jnp.sqrt(v + eps)

def _scatter_add(tgt, idx, src, axis=0):
    return tgt.at[idx].add(src)

def _segment_sum(src, seg, n):
    return jax.ops.segment_sum(src, seg, n)
kernel_name = 'mk_decoder_preln_d2_seqx_r8_6a805e'

def setup_inputs(seed: int=0):
    np.random.seed(seed)
    _w = jnp.asarray

    def _rec_inputs():
        import jax
        import jax.numpy as jnp
        _rk = jax.random.key(seed)
        x = 7.22e-05 + 1 * jax.random.normal(jax.random.fold_in(_rk, 1), (16, 128, 256), jnp.float32)
        _lenS = 128 - jax.random.randint(jax.random.fold_in(_rk, 7), (16,), 0, max(1, 128 // 4) + 1, jnp.int32)
        _lenS2 = 128 - jax.random.randint(jax.random.fold_in(_rk, 8), (16,), 0, max(1, 128 // 4) + 1, jnp.int32)
        _ctx_2048P = jax.random.normal(jax.random.fold_in(_rk, 11), (16, 16, 256), jnp.float32)
        _ctx_2048c = jax.random.dirichlet(jax.random.fold_in(_rk, 511), 0.3 * jnp.ones((16,), jnp.float32), (16, 128))
        _ctx_2048t = jnp.einsum('bsk,bkd->bsd', _ctx_2048c, _ctx_2048P)
        _ctx_2048t = _ctx_2048t * jax.lax.rsqrt(jnp.mean(jnp.square(_ctx_2048t)) + 1e-12) * 0.953939
        ctx_2048 = 4.13588e-05 + 0.999923 * (_ctx_2048t + 0.3 * jax.random.normal(jax.random.fold_in(_rk, 611), (16, 128, 256), jnp.float32))
        _validS = jnp.arange(128)[None, :] < _lenS[:, None]
        _validS2 = jnp.arange(128)[None, :] < _lenS2[:, None]
        _causal = jnp.tril(jnp.ones((128, 128), dtype=bool))
        mask_BxSx4224_bf0 = jnp.logical_not(jnp.ones((16, 128, 528), dtype=bool))
        return (x, ctx_2048, mask_BxSx4224_bf0)
    x, ctx_2048, mask_BxSx4224_bf0 = _rec_inputs()

    def _L0_attn_setup():
        import jax, jax.numpy as jnp
        import numpy as np
        D_MODEL = 256
        N_HEADS = 16
        D_K = 128
        EPS = 1e-05
        ROPE_BASE = 10000.0

        def rope(x):
            b, s, h, d = x.shape
            d2 = d // 2
            theta = 1.0 / ROPE_BASE ** (jnp.arange(0, d, 2, dtype=jnp.float32) / d)
            pos = jnp.arange(s, dtype=jnp.float32)
            freqs = pos[:, None] * theta[None, :]
            freqs = jnp.concatenate([freqs, freqs], axis=-1)
            cos = jnp.cos(freqs)[None, :, None, :]
            sin = jnp.sin(freqs)[None, :, None, :]
            x_rot = jnp.concatenate([-x[..., d2:], x[..., :d2]], axis=-1)
            return x * cos + x_rot * sin
        key = jax.random.key(seed)
        ks = jax.random.split(key, 10)
        hd = N_HEADS * D_K

        def xavier(k, shape):
            fan_in, fan_out = (shape[1], shape[0])
            lim = np.sqrt(6.0 / (fan_in + fan_out))
            return jax.random.uniform(k, shape, jnp.float32, -lim, lim)
        return {'h': jax.random.normal(ks[0], (2, 256, D_MODEL), jnp.float32), 'wq': xavier(ks[1], (hd, D_MODEL)), 'bq': jnp.zeros((hd,), jnp.float32), 'wk': xavier(ks[2], (hd, D_MODEL)), 'bk': jnp.zeros((hd,), jnp.float32), 'wv': xavier(ks[3], (hd, D_MODEL)), 'bv': jnp.zeros((hd,), jnp.float32), 'wo': xavier(ks[4], (D_MODEL, hd)), 'bo': jnp.zeros((D_MODEL,), jnp.float32), 'ln_g': jnp.ones((D_MODEL,), jnp.float32), 'ln_b': jnp.zeros((D_MODEL,), jnp.float32)}
    _L0_attn_all = _L0_attn_setup()
    _L0_attn_in = {k: v for k, v in _L0_attn_all.items() if k in ('wq', 'bq', 'wk', 'bk', 'wv', 'bv', 'wo', 'bo', 'ln_g', 'ln_b')}
    del _L0_attn_all

    def _L0_xattn_setup():
        import jax, jax.numpy as jnp
        import numpy as np
        B, S, DIM, HD = (4, 128, 256, 128)
        H = DIM // HD
        GN_EPS = 0.001

        def _decay_masks(n_heads, seq_len):
            gam = 1.0 - 2.0 ** (-5.0 - jnp.arange(n_heads, dtype=jnp.float32))
            idx = jnp.arange(seq_len, dtype=jnp.float32)
            expo = idx[None, :] - idx[:, None]
            D = jnp.where(expo[None, :, :] <= 0, gam[:, None, None] ** expo[None, :, :], 0.0)
            return D / jnp.sqrt(D.sum(axis=-1))[:, None, :]
        key = jax.random.key(seed)
        ks = jax.random.split(key, 8)
        x = jax.random.normal(ks[0], (B, S, DIM), dtype=jnp.float32)
        k = jax.random.normal(ks[1], (B, S, DIM), dtype=jnp.float32)
        v = jax.random.normal(ks[2], (B, S, DIM), dtype=jnp.float32)
        Wh = jax.random.normal(ks[3], (H, HD, HD), dtype=jnp.float32) / np.sqrt(HD)
        wg_w = jax.random.normal(ks[4], (DIM, DIM), dtype=jnp.float32) / np.sqrt(DIM)
        wo_w = jax.random.normal(ks[5], (DIM, DIM), dtype=jnp.float32) / np.sqrt(DIM)
        gn_gamma = jnp.ones((DIM,), dtype=jnp.float32)
        gn_beta = jnp.zeros((DIM,), dtype=jnp.float32)
        return {'x': x, 'k': k, 'v': v, 'Wh': Wh, 'wg_w': wg_w, 'wo_w': wo_w, 'gn_gamma': gn_gamma, 'gn_beta': gn_beta}
    _L0_xattn_all = _L0_xattn_setup()
    _L0_xattn_in = {k: v for k, v in _L0_xattn_all.items() if k in ('Wh', 'wg_w', 'wo_w', 'gn_gamma', 'gn_beta')}
    del _L0_xattn_all

    def _L0_ffn_setup():
        import jax, jax.numpy as jnp
        import numpy as np
        D_MODEL = 256
        NUM_TILES = 64
        D_SLICE = D_MODEL // NUM_TILES
        TILES_PER_CLUSTER = 8
        NUM_CLUSTERS = NUM_TILES // TILES_PER_CLUSTER
        GRID = 16
        LN_EPS = 1e-05
        DIMS = (np.arange(NUM_TILES)[:, None] * D_SLICE + np.arange(D_SLICE)[None, :]) % D_MODEL
        DIMS = jnp.asarray(DIMS, dtype=jnp.int32)

        def _forward(x, ln_gamma, ln_beta, spline_bases, spline_slopes, output_scale):
            B, S, D = x.shape
            N = B * S
            mu = jnp.mean(x, axis=-1, keepdims=True)
            var = jnp.mean(jnp.square(x - mu), axis=-1, keepdims=True)
            xn = (x - mu) * jax.lax.rsqrt(var + LN_EPS) * ln_gamma + ln_beta
            xf = xn.reshape(N, D)
            slope_sign = jnp.sign(jnp.mean(spline_slopes, axis=-1))
            tile_sigs = jnp.zeros((NUM_TILES, D), dtype=x.dtype)
            tile_sigs = tile_sigs.at[jnp.arange(NUM_TILES)[:, None], DIMS].set(slope_sign)
            cluster_sigs = jnp.sign(tile_sigs.reshape(NUM_CLUSTERS, TILES_PER_CLUSTER, D).mean(axis=1))
            cluster_assign = jnp.arange(NUM_TILES, dtype=jnp.int32) // TILES_PER_CLUSTER
            input_sigs = jnp.sign(xf)
            cluster_scores = input_sigs @ cluster_sigs.T
            best_cluster = jnp.argmax(cluster_scores, axis=-1)
            tile_scores = input_sigs @ tile_sigs.T
            in_cluster = cluster_assign[None, :] == best_cluster[:, None]
            tile_idx = jnp.argmax(jnp.where(in_cluster, tile_scores, -jnp.inf), axis=-1)
            tok_dims = DIMS[tile_idx]
            x_slice = jnp.take_along_axis(xf, tok_dims, axis=1)
            tok_min = x_slice.min(axis=1)
            tok_max = x_slice.max(axis=1)
            onehot = tile_idx[None, :] == jnp.arange(NUM_TILES)[:, None]
            tile_min = jnp.where(onehot, tok_min[None, :], jnp.inf).min(axis=1)
            tile_max = jnp.where(onehot, tok_max[None, :], -jnp.inf).max(axis=1)
            mn = tile_min[tile_idx][:, None]
            mx = tile_max[tile_idx][:, None]
            u = jnp.clip((x_slice - mn) / (mx - mn + 1e-08), 0.0, 1.0 - 1e-06)
            gi = jnp.clip((u * GRID).astype(jnp.int32), 0, GRID - 1)
            j = jnp.arange(D_SLICE)[None, :]
            b = spline_bases[tile_idx[:, None], j, gi]
            s = spline_slopes[tile_idx[:, None], j, gi]
            x_local = (u - gi.astype(u.dtype) / GRID) * GRID
            delta = (b + s * x_local) * output_scale[tile_idx][:, None]
            out = jnp.zeros_like(xf).at[jnp.arange(N)[:, None], tok_dims].set(delta)
            return x + out.reshape(B, S, D)
        key = jax.random.key(seed)
        k1, k2, k3, k4, k5, k6 = jax.random.split(key, 6)
        x = jax.random.normal(k1, (4, 512, D_MODEL), dtype=jnp.float32)
        ln_gamma = 1.0 + 0.1 * jax.random.normal(k2, (D_MODEL,), dtype=jnp.float32)
        ln_beta = 0.1 * jax.random.normal(k3, (D_MODEL,), dtype=jnp.float32)
        spline_bases = 0.1 * jax.random.normal(k4, (NUM_TILES, D_SLICE, GRID), dtype=jnp.float32)
        spline_slopes = 0.1 + 0.1 * jax.random.normal(k5, (NUM_TILES, D_SLICE, GRID), dtype=jnp.float32)
        output_scale = 1.0 + 0.1 * jax.random.normal(k6, (NUM_TILES,), dtype=jnp.float32)
        return {'x': x, 'ln_gamma': ln_gamma, 'ln_beta': ln_beta, 'spline_bases': spline_bases, 'spline_slopes': spline_slopes, 'output_scale': output_scale}
    _L0_ffn_all = _L0_ffn_setup()
    _L0_ffn_in = {k: v for k, v in _L0_ffn_all.items() if k in ('ln_gamma', 'ln_beta', 'spline_bases', 'spline_slopes', 'output_scale')}
    del _L0_ffn_all

    def _L1_attn_setup():
        import jax, jax.numpy as jnp
        import numpy as np
        EMBED_DIM = 256
        NUM_HEADS = 16
        HEAD_DIM = EMBED_DIM // NUM_HEADS
        WINDOW = 64

        def _sliding_window_attn(q, k, v, window):
            B, H, S, d = q.shape
            C = window
            nc = S // C
            qc = q.reshape(B, H, nc, C, d)

            def two_chunks(t):
                tc = t.reshape(B, H, nc, C, d)
                prev = jnp.pad(tc[:, :, :-1], ((0, 0), (0, 0), (1, 0), (0, 0), (0, 0)))
                return jnp.concatenate([prev, tc], axis=3)
            kc = two_chunks(k)
            vc = two_chunks(v)
            scale = 1.0 / np.sqrt(d).astype(np.float32)
            scores = jnp.einsum('bhnid,bhnjd->bhnij', qc, kc) * scale
            i = jnp.arange(C)[:, None]
            j = jnp.arange(2 * C)[None, :]
            band = (j >= i) & (j <= i + C)
            kv_global = (jnp.arange(nc)[:, None, None] - 1) * C + j[None]
            mask = band[None] & (kv_global >= 0)
            scores = jnp.where(mask[None, None], scores, jnp.finfo(scores.dtype).min)
            probs = jax.nn.softmax(scores, axis=-1)
            out = jnp.einsum('bhnij,bhnjd->bhnid', probs, vc)
            return out.reshape(B, H, S, d)
        key = jax.random.key(seed)
        k1, k2, k3 = jax.random.split(key, 3)
        B, S = (2, 512)
        x = jax.random.normal(k1, (B, S, EMBED_DIM), dtype=jnp.float32)
        w_qkv = jax.random.normal(k2, (3 * EMBED_DIM, EMBED_DIM), dtype=jnp.float32) * 0.02
        w_out = jax.random.normal(k3, (EMBED_DIM, EMBED_DIM), dtype=jnp.float32) * 0.02
        return {'x': x, 'w_qkv': w_qkv, 'w_out': w_out}
    _L1_attn_all = _L1_attn_setup()
    _L1_attn_in = {k: v for k, v in _L1_attn_all.items() if k in ('w_qkv', 'w_out')}
    del _L1_attn_all

    def _L1_xattn_setup():
        import jax, jax.numpy as jnp
        import numpy as np
        import math
        DIM = 256
        B, Q_LEN, KV_LEN = (8, 128, 512)
        key = jax.random.key(seed)
        ks = jax.random.split(key, 8)
        x = jax.random.normal(ks[0], (B, Q_LEN, DIM), dtype=jnp.float32)
        mask = jnp.zeros((B, Q_LEN, KV_LEN + Q_LEN), dtype=bool)
        k_cache = jax.random.normal(ks[1], (B, KV_LEN, DIM), dtype=jnp.float32)
        v_cache = jax.random.normal(ks[2], (B, KV_LEN, DIM), dtype=jnp.float32)
        scale = 1.0 / math.sqrt(DIM)
        wq = jax.random.normal(ks[3], (DIM, DIM), dtype=jnp.float32) * scale
        wk = jax.random.normal(ks[4], (DIM, DIM), dtype=jnp.float32) * scale
        wv = jax.random.normal(ks[5], (DIM, DIM), dtype=jnp.float32) * scale
        wo = jax.random.normal(ks[6], (DIM, DIM), dtype=jnp.float32) * scale
        return {'x': x, 'mask': mask, 'k_cache': k_cache, 'v_cache': v_cache, 'wq': wq, 'wk': wk, 'wv': wv, 'wo': wo}
    _L1_xattn_all = _L1_xattn_setup()
    _L1_xattn_in = {k: v for k, v in _L1_xattn_all.items() if k in ('wq', 'wk', 'wv', 'wo')}
    del _L1_xattn_all

    def _L1_ffn_setup():
        import jax, jax.numpy as jnp
        import numpy as np
        B, S, EMB = (4, 256, 256)
        LAT, HID = (64, 128)
        E, K = (16, 8)
        SCALE = 2.5

        def _w(key, shape, fan_in):
            return jax.random.normal(key, shape, jnp.float32) * fan_in ** (-0.5)

        def _sqrelu(x):
            return jnp.square(jax.nn.relu(x))
        key = jax.random.key(seed)
        ks = jax.random.split(key, 11)
        return {'x': jax.random.normal(ks[0], (B, S, EMB), jnp.float32), 'sw1': _w(ks[1], (HID, EMB), EMB), 'swg': _w(ks[2], (HID, EMB), EMB), 'sw2': _w(ks[3], (EMB, HID), HID), 'rw1': _w(ks[4], (E, HID, LAT), LAT), 'rwg': _w(ks[5], (E, HID, LAT), LAT), 'rw2': _w(ks[6], (E, LAT, HID), HID), 'Wg': _w(ks[7], (E, EMB), EMB), 'Wdown': _w(ks[8], (LAT, EMB), EMB), 'Wup': _w(ks[9], (EMB, LAT), LAT), 'biases': jnp.zeros((E,), jnp.float32)}
    _L1_ffn_all = _L1_ffn_setup()
    _L1_ffn_in = {k: v for k, v in _L1_ffn_all.items() if k in ('sw1', 'swg', 'sw2', 'rw1', 'rwg', 'rw2', 'Wg', 'Wdown', 'Wup', 'biases')}
    del _L1_ffn_all
    return {'x': x, 'ctx_2048': ctx_2048, 'mask_BxSx4224_bf0': mask_BxSx4224_bf0, 'L0_attn_wq': _L0_attn_in['wq'], 'L0_attn_bq': _L0_attn_in['bq'], 'L0_attn_wk': _L0_attn_in['wk'], 'L0_attn_bk': _L0_attn_in['bk'], 'L0_attn_wv': _L0_attn_in['wv'], 'L0_attn_bv': _L0_attn_in['bv'], 'L0_attn_wo': _L0_attn_in['wo'], 'L0_attn_bo': _L0_attn_in['bo'], 'L0_attn_ln_g': _L0_attn_in['ln_g'], 'L0_attn_ln_b': _L0_attn_in['ln_b'], 'L0_xattn_Wh': _L0_xattn_in['Wh'], 'L0_xattn_wg_w': _L0_xattn_in['wg_w'], 'L0_xattn_wo_w': _L0_xattn_in['wo_w'], 'L0_xattn_gn_gamma': _L0_xattn_in['gn_gamma'], 'L0_xattn_gn_beta': _L0_xattn_in['gn_beta'], 'L0_ffn_ln_gamma': _L0_ffn_in['ln_gamma'], 'L0_ffn_ln_beta': _L0_ffn_in['ln_beta'], 'L0_ffn_spline_bases': _L0_ffn_in['spline_bases'], 'L0_ffn_spline_slopes': _L0_ffn_in['spline_slopes'], 'L0_ffn_output_scale': _L0_ffn_in['output_scale'], 'L1_attn_w_qkv': _L1_attn_in['w_qkv'], 'L1_attn_w_out': _L1_attn_in['w_out'], 'L1_xattn_wq': _L1_xattn_in['wq'], 'L1_xattn_wk': _L1_xattn_in['wk'], 'L1_xattn_wv': _L1_xattn_in['wv'], 'L1_xattn_wo': _L1_xattn_in['wo'], 'L1_ffn_sw1': _L1_ffn_in['sw1'], 'L1_ffn_swg': _L1_ffn_in['swg'], 'L1_ffn_sw2': _L1_ffn_in['sw2'], 'L1_ffn_rw1': _L1_ffn_in['rw1'], 'L1_ffn_rwg': _L1_ffn_in['rwg'], 'L1_ffn_rw2': _L1_ffn_in['rw2'], 'L1_ffn_Wg': _L1_ffn_in['Wg'], 'L1_ffn_Wdown': _L1_ffn_in['Wdown'], 'L1_ffn_Wup': _L1_ffn_in['Wup'], 'L1_ffn_biases': _L1_ffn_in['biases']}

def reference(x, ctx_2048, mask_BxSx4224_bf0, L0_attn_wq, L0_attn_bq, L0_attn_wk, L0_attn_bk, L0_attn_wv, L0_attn_bv, L0_attn_wo, L0_attn_bo, L0_attn_ln_g, L0_attn_ln_b, L0_xattn_Wh, L0_xattn_wg_w, L0_xattn_wo_w, L0_xattn_gn_gamma, L0_xattn_gn_beta, L0_ffn_ln_gamma, L0_ffn_ln_beta, L0_ffn_spline_bases, L0_ffn_spline_slopes, L0_ffn_output_scale, L1_attn_w_qkv, L1_attn_w_out, L1_xattn_wq, L1_xattn_wk, L1_xattn_wv, L1_xattn_wo, L1_ffn_sw1, L1_ffn_swg, L1_ffn_sw2, L1_ffn_rw1, L1_ffn_rwg, L1_ffn_rw2, L1_ffn_Wg, L1_ffn_Wdown, L1_ffn_Wup, L1_ffn_biases):
    import jax
    import jax.numpy as jnp

    def _L0_attn_ref(h, wq, bq, wk, bk, wv, bv, wo, bo, ln_g, ln_b):
        import jax, jax.numpy as jnp
        import numpy as np
        D_MODEL = 256
        N_HEADS = 16
        D_K = 128
        EPS = 1e-05
        ROPE_BASE = 10000.0

        def rope(x):
            b, s, h, d = x.shape
            d2 = d // 2
            theta = 1.0 / ROPE_BASE ** (jnp.arange(0, d, 2, dtype=jnp.float32) / d)
            pos = jnp.arange(s, dtype=jnp.float32)
            freqs = pos[:, None] * theta[None, :]
            freqs = jnp.concatenate([freqs, freqs], axis=-1)
            cos = jnp.cos(freqs)[None, :, None, :]
            sin = jnp.sin(freqs)[None, :, None, :]
            x_rot = jnp.concatenate([-x[..., d2:], x[..., :d2]], axis=-1)
            return x * cos + x_rot * sin
        residual = h
        mu = jnp.mean(h, axis=-1, keepdims=True)
        var = jnp.mean(jnp.square(h - mu), axis=-1, keepdims=True)
        x = (h - mu) * jax.lax.rsqrt(var + EPS) * ln_g + ln_b
        b, s, _ = x.shape
        q = (x @ wq.T + bq).reshape(b, s, N_HEADS, D_K)
        k = (x @ wk.T + bk).reshape(b, s, N_HEADS, D_K)
        v = (x @ wv.T + bv).reshape(b, s, N_HEADS, D_K)
        q = rope(q)
        k = rope(k)
        scale = 1.0 / np.sqrt(D_K)
        attn = jnp.einsum('bihd,bjhd->bhij', q, k) * scale
        causal = jnp.triu(jnp.ones((s, s), dtype=bool), k=1)
        attn = jnp.where(causal[None, None], -jnp.inf, attn)
        attn = jax.nn.softmax(attn, axis=-1)
        o = jnp.einsum('bhij,bjhd->bihd', attn, v).reshape(b, s, N_HEADS * D_K)
        return o @ wo.T + bo + residual

    def _L0_xattn_ref(x, k, v, Wh, wg_w, wo_w, gn_gamma, gn_beta):
        import jax, jax.numpy as jnp
        import numpy as np
        B, S, DIM, HD = (4, 128, 256, 128)
        H = DIM // HD
        GN_EPS = 0.001

        def _decay_masks(n_heads, seq_len):
            gam = 1.0 - 2.0 ** (-5.0 - jnp.arange(n_heads, dtype=jnp.float32))
            idx = jnp.arange(seq_len, dtype=jnp.float32)
            expo = idx[None, :] - idx[:, None]
            D = jnp.where(expo[None, :, :] <= 0, gam[:, None, None] ** expo[None, :, :], 0.0)
            return D / jnp.sqrt(D.sum(axis=-1))[:, None, :]
        b, s, dim = x.shape
        h, hd, _ = Wh.shape
        xh = x.reshape(b, s, h, hd)
        kh = k.reshape(b, s, h, hd)
        vh = v.reshape(b, s, h, hd)
        Q = jnp.einsum('bshd,hde->bshe', xh, Wh)
        K = jnp.einsum('bshd,hde->bshe', kh, Wh)
        V = jnp.einsum('bshd,hde->bshe', vh, Wh)
        scores = jnp.einsum('bshe,bthe->bhst', Q, K) / jnp.sqrt(jnp.float32(hd))
        Dn = _decay_masks(h, s)
        masked = scores * Dn[None, :, :, :]
        A = jnp.maximum(jnp.abs(masked.sum(axis=0)), 1.0)
        O = jnp.einsum('hst,bthe->bshe', A, V).reshape(b, s, dim)
        mu = O.mean(axis=-1, keepdims=True)
        var = O.var(axis=-1, keepdims=True)
        Y = (O - mu) / jnp.sqrt(var + GN_EPS) * gn_gamma + gn_beta
        W = jax.nn.relu(x @ wg_w)
        return W * Y @ wo_w

    def _L0_ffn_ref(x, ln_gamma, ln_beta, spline_bases, spline_slopes, output_scale):
        import jax, jax.numpy as jnp
        import numpy as np
        D_MODEL = 256
        NUM_TILES = 64
        D_SLICE = D_MODEL // NUM_TILES
        TILES_PER_CLUSTER = 8
        NUM_CLUSTERS = NUM_TILES // TILES_PER_CLUSTER
        GRID = 16
        LN_EPS = 1e-05
        DIMS = (np.arange(NUM_TILES)[:, None] * D_SLICE + np.arange(D_SLICE)[None, :]) % D_MODEL
        DIMS = jnp.asarray(DIMS, dtype=jnp.int32)

        def _forward(x, ln_gamma, ln_beta, spline_bases, spline_slopes, output_scale):
            B, S, D = x.shape
            N = B * S
            mu = jnp.mean(x, axis=-1, keepdims=True)
            var = jnp.mean(jnp.square(x - mu), axis=-1, keepdims=True)
            xn = (x - mu) * jax.lax.rsqrt(var + LN_EPS) * ln_gamma + ln_beta
            xf = xn.reshape(N, D)
            slope_sign = jnp.sign(jnp.mean(spline_slopes, axis=-1))
            tile_sigs = jnp.zeros((NUM_TILES, D), dtype=x.dtype)
            tile_sigs = tile_sigs.at[jnp.arange(NUM_TILES)[:, None], DIMS].set(slope_sign)
            cluster_sigs = jnp.sign(tile_sigs.reshape(NUM_CLUSTERS, TILES_PER_CLUSTER, D).mean(axis=1))
            cluster_assign = jnp.arange(NUM_TILES, dtype=jnp.int32) // TILES_PER_CLUSTER
            input_sigs = jnp.sign(xf)
            cluster_scores = input_sigs @ cluster_sigs.T
            best_cluster = jnp.argmax(cluster_scores, axis=-1)
            tile_scores = input_sigs @ tile_sigs.T
            in_cluster = cluster_assign[None, :] == best_cluster[:, None]
            tile_idx = jnp.argmax(jnp.where(in_cluster, tile_scores, -jnp.inf), axis=-1)
            tok_dims = DIMS[tile_idx]
            x_slice = jnp.take_along_axis(xf, tok_dims, axis=1)
            tok_min = x_slice.min(axis=1)
            tok_max = x_slice.max(axis=1)
            onehot = tile_idx[None, :] == jnp.arange(NUM_TILES)[:, None]
            tile_min = jnp.where(onehot, tok_min[None, :], jnp.inf).min(axis=1)
            tile_max = jnp.where(onehot, tok_max[None, :], -jnp.inf).max(axis=1)
            mn = tile_min[tile_idx][:, None]
            mx = tile_max[tile_idx][:, None]
            u = jnp.clip((x_slice - mn) / (mx - mn + 1e-08), 0.0, 1.0 - 1e-06)
            gi = jnp.clip((u * GRID).astype(jnp.int32), 0, GRID - 1)
            j = jnp.arange(D_SLICE)[None, :]
            b = spline_bases[tile_idx[:, None], j, gi]
            s = spline_slopes[tile_idx[:, None], j, gi]
            x_local = (u - gi.astype(u.dtype) / GRID) * GRID
            delta = (b + s * x_local) * output_scale[tile_idx][:, None]
            out = jnp.zeros_like(xf).at[jnp.arange(N)[:, None], tok_dims].set(delta)
            return x + out.reshape(B, S, D)
        return _forward(x, ln_gamma, ln_beta, spline_bases, spline_slopes, output_scale)

    def _L1_attn_ref(x, w_qkv, w_out):
        import jax, jax.numpy as jnp
        import numpy as np
        EMBED_DIM = 256
        NUM_HEADS = 16
        HEAD_DIM = EMBED_DIM // NUM_HEADS
        WINDOW = 64

        def _sliding_window_attn(q, k, v, window):
            B, H, S, d = q.shape
            C = window
            nc = S // C
            qc = q.reshape(B, H, nc, C, d)

            def two_chunks(t):
                tc = t.reshape(B, H, nc, C, d)
                prev = jnp.pad(tc[:, :, :-1], ((0, 0), (0, 0), (1, 0), (0, 0), (0, 0)))
                return jnp.concatenate([prev, tc], axis=3)
            kc = two_chunks(k)
            vc = two_chunks(v)
            scale = 1.0 / np.sqrt(d).astype(np.float32)
            scores = jnp.einsum('bhnid,bhnjd->bhnij', qc, kc) * scale
            i = jnp.arange(C)[:, None]
            j = jnp.arange(2 * C)[None, :]
            band = (j >= i) & (j <= i + C)
            kv_global = (jnp.arange(nc)[:, None, None] - 1) * C + j[None]
            mask = band[None] & (kv_global >= 0)
            scores = jnp.where(mask[None, None], scores, jnp.finfo(scores.dtype).min)
            probs = jax.nn.softmax(scores, axis=-1)
            out = jnp.einsum('bhnij,bhnjd->bhnid', probs, vc)
            return out.reshape(B, H, S, d)
        B, S, E = x.shape
        qkv = jnp.einsum('bse,fe->bsf', x, w_qkv)
        qkv = qkv.reshape(B, S, 3, NUM_HEADS, HEAD_DIM)
        qkv = jnp.transpose(qkv, (2, 0, 3, 1, 4))
        q, k, v = (qkv[0], qkv[1], qkv[2])
        attn = _sliding_window_attn(q, k, v, WINDOW)
        attn = jnp.transpose(attn, (0, 2, 1, 3)).reshape(B, S, E)
        return jnp.einsum('bse,fe->bsf', attn, w_out)

    def _L1_xattn_ref(x, mask, k_cache, v_cache, wq, wk, wv, wo):
        import jax, jax.numpy as jnp
        import numpy as np
        import math
        DIM = 256
        B, Q_LEN, KV_LEN = (8, 128, 512)
        q = jnp.einsum('bsd,ed->bse', x, wq)
        k_new = jnp.einsum('bsd,ed->bse', x, wk)
        v_new = jnp.einsum('bsd,ed->bse', x, wv)
        k = jnp.concatenate([k_cache, k_new], axis=1)
        v = jnp.concatenate([v_cache, v_new], axis=1)
        scale = 1.0 / math.sqrt(q.shape[-1])
        scores = jnp.einsum('bqd,bkd->bqk', q, k) * scale
        attn = jax.nn.softmax(scores, axis=-1)
        out = jnp.einsum('bqk,bkd->bqd', attn, v)
        return jnp.einsum('bqd,ed->bqe', out, wo)

    def _L1_ffn_ref(x, sw1, swg, sw2, rw1, rwg, rw2, Wg, Wdown, Wup, biases):
        import jax, jax.numpy as jnp
        import numpy as np
        B, S, EMB = (4, 256, 256)
        LAT, HID = (64, 128)
        E, K = (16, 8)
        SCALE = 2.5

        def _w(key, shape, fan_in):
            return jax.random.normal(key, shape, jnp.float32) * fan_in ** (-0.5)

        def _sqrelu(x):
            return jnp.square(jax.nn.relu(x))
        b, s, d = x.shape
        x2 = x.reshape(-1, d)
        shared = x2 @ sw1.T * _sqrelu(x2 @ swg.T) @ sw2.T
        xl = x2 @ Wdown.T
        probas = jax.nn.sigmoid(x2 @ Wg.T)
        _, idx = jax.lax.top_k(probas + biases, K)
        p = jnp.take_along_axis(probas, idx, axis=-1)
        p = p / p.sum(-1, keepdims=True) * SCALE
        T = x2.shape[0]
        w_dense = jnp.zeros((T, E), x2.dtype).at[jnp.arange(T)[:, None], idx].add(p)
        acc = jnp.zeros_like(xl)
        for e in range(E):
            ye = xl @ rw1[e].T * _sqrelu(xl @ rwg[e].T) @ rw2[e].T
            acc = acc + w_dense[:, e:e + 1] * ye
        out = shared + acc @ Wup.T
        return out.reshape(b, s, d)
    x = x + _L0_attn_ref(_layernorm(x, axis=-1), L0_attn_wq, L0_attn_bq, L0_attn_wk, L0_attn_bk, L0_attn_wv, L0_attn_bv, L0_attn_wo, L0_attn_bo, L0_attn_ln_g, L0_attn_ln_b)
    x = x + _L0_xattn_ref(_layernorm(x, axis=-1), ctx_2048, ctx_2048, L0_xattn_Wh, L0_xattn_wg_w, L0_xattn_wo_w, L0_xattn_gn_gamma, L0_xattn_gn_beta)
    x = x + _L0_ffn_ref(_layernorm(x, axis=-1), L0_ffn_ln_gamma, L0_ffn_ln_beta, L0_ffn_spline_bases, L0_ffn_spline_slopes, L0_ffn_output_scale)
    x = x + _L1_attn_ref(_layernorm(x, axis=-1), L1_attn_w_qkv, L1_attn_w_out)
    x = x + _L1_xattn_ref(_layernorm(x, axis=-1), mask_BxSx4224_bf0, ctx_2048, ctx_2048, L1_xattn_wq, L1_xattn_wk, L1_xattn_wv, L1_xattn_wo)
    x = x + _L1_ffn_ref(_layernorm(x, axis=-1), L1_ffn_sw1, L1_ffn_swg, L1_ffn_sw2, L1_ffn_rw1, L1_ffn_rwg, L1_ffn_rw2, L1_ffn_Wg, L1_ffn_Wdown, L1_ffn_Wup, L1_ffn_biases)
    return x

_drawn_inputs = setup_inputs


def setup_inputs(seed=0):
    import zlib

    import numpy as np

    out = dict(_drawn_inputs(seed))
    spreads = {'L0_attn_bq': (0.0, 0.685),
     'L0_attn_bk': (0.0, 0.8),
     'L0_attn_bv': (0.0, 0.1),
     'L0_attn_bo': (0.0, 0.1),
     'L0_attn_ln_g': (1.0, 0.548),
     'L0_attn_ln_b': (0.0, 0.1),
     'L0_xattn_gn_gamma': (1.0, 0.2),
     'L0_xattn_gn_beta': (0.0, 0.1),
     'L1_ffn_biases': (0.0, 0.1)}
    factors = {'L0_ffn_ln_gamma': 5.358,
     'L0_ffn_ln_beta': 4.241,
     'L0_ffn_spline_bases': 4.472,
     'L0_ffn_spline_slopes': 6.508,
     'L0_ffn_output_scale': 8.0,
     'L1_attn_w_qkv': 2.934,
     'L1_attn_w_out': 2.801}
    for name, (base, spread) in spreads.items():
        noise = np.random.default_rng([zlib.crc32(name.encode()), seed]).standard_normal(out[name].shape)
        drawn = base * np.exp(spread * noise) if base else spread * noise
        out[name] = jnp.asarray(drawn.astype(out[name].dtype))
    for name, factor in factors.items():
        out[name] = (out[name] * factor).astype(out[name].dtype)
    return out
```

```python
import numpy as np
import concourse.bass as bass
from concourse import mybir
from concourse.alu_op_type import AluOpType as ALU
from contextlib import ExitStack

F32 = mybir.dt.float32
F32R = mybir.dt.float32r
BF16 = mybir.dt.bfloat16
ACT = mybir.ActivationFunctionType
AX = mybir.AxisListType

B, S, D = 16, 128, 256
KD = D // 128
LN_EPS = 1e-5

HEADS0, DK0 = 16, 128
QUADS = HEADS0 // 4
QW = 4 * DK0
STEPS0 = B * QUADS
MASKED = -1e30


def wait(eng, sem, value):
    if isinstance(value, int) and value <= 0:
        return
    eng.wait_ge(sem, value)


def matmul3(nc, out, lhs, rhs, first, last):
    (lh, ll), (rh, rl) = lhs, rhs
    nc.tensor.matmul(out, lh, rl, start=first, stop=False)
    nc.tensor.matmul(out, ll, rh, start=False, stop=False)
    return nc.tensor.matmul(out, lh, rh, start=False, stop=last)


def finish_stats(nc, dve, done, count, stats, mean, var_eps, tmp, eps):
    half = D // 2
    me, m2e, mo, m2o = stats[:, :, 1], stats[:, :, 2], stats[:, :, 4], stats[:, :, 5]

    def link(ins):
        nonlocal count
        count += 1
        ins.then_inc(done, 1)

    link(nc.vector.tensor_tensor(tmp[:, 0, :], me, mo, ALU.add))
    link(nc.vector.tensor_tensor(tmp[:, 1, :], me, mo, ALU.subtract))
    link(nc.vector.tensor_tensor(tmp[:, 2, :], m2e, m2o, ALU.add))
    dve.wait_ge(done, count)
    link(nc.vector.tensor_scalar(mean, tmp[:, 0, :], 0.5, None, ALU.mult))
    link(nc.vector.scalar_tensor_tensor(tmp[:, 3, :], tmp[:, 1, :], half / 2.0, tmp[:, 1, :], ALU.mult, ALU.mult))
    dve.wait_ge(done, count)
    link(nc.vector.tensor_tensor(tmp[:, 4, :], tmp[:, 3, :], tmp[:, 2, :], ALU.add))
    dve.wait_ge(done, count)
    link(nc.vector.tensor_scalar(var_eps, tmp[:, 4, :], 1.0 / D, float(eps), ALU.mult, ALU.add))
    return count


def decoder_kernel(nc, a, out):
    ctx = ExitStack()
    with ctx:
        def sb(name, shape, dt=F32, where=ctx):
            return where.enter_context(nc.sbuf_tensor(name, shape, dt))

        sems_in_use = []

        def sem(name):
            sems_in_use.append(nc.alloc_semaphore(name=name))
            return sems_in_use[-1]

        def clear_semaphores():
            nc.clear_and_free_semaphores(sems_in_use)
            nc.all_engine_barrier()
            sems_in_use.clear()

        bank = [ctx.enter_context(nc.psum_tensor(f"bank{i}", [128, 512], F32)) for i in range(8)]
        X = sb("X", [128, B, D])
        ident = sb("ident", [128, 128])
        mean = sb("mean", [128, B])
        var_eps = sb("var_eps", [128, B])
        rstd = sb("rstd", [128, B])
        minus_half = sb("minus_half", [128, B])
        stats = sb("stats", [128, B, 6])
        ln_tmp = sb("ln_tmp", [128, 5, B])

        phase_attn0(nc, a, sem, sb, bank, X, ident, mean, var_eps, rstd, minus_half, stats, ln_tmp)
        phase_rest(nc, a, sem, sb, bank, X, ident, mean, var_eps, rstd, minus_half, stats, ln_tmp, out, clear_semaphores)


def batch(tile, b):
    if isinstance(b, int):
        return tile[:, b, :]
    return tile[:, bass.ds(b, 1), :].rearrange("p a n -> p (a n)")


def one(tile, b):
    return tile[:, b:b + 1] if isinstance(b, int) else tile[:, bass.ds(b, 1)]


def phase_attn0(nc, a, sem, sb_, bank, X, ident, mean, var_eps, rstd, minus_half, stats, ln_tmp):
    local = ExitStack()
    with local:
        def sb(name, shape, dt=F32):
            return sb_(name, shape, dt, local)

        H = sb("H", [128, B, D])
        WH = sb("WH", [128, 3, KD, HEADS0 * DK0], F32R)
        WL = sb("WL", [128, 3, KD, HEADS0 * DK0], F32R)
        WO = sb("WO", [128, HEADS0, D])
        stage = sb("stage", [128, 2, KD, QW])
        qk_bias = sb("qk_bias", [128, 2 * HEADS0 * DK0], BF16)
        ones_row = sb("ones_row", [128, 128], BF16)
        bias_in = sb("bias_in", [32, DK0])
        bias_part = sb("bias_part", [32, 3, DK0], BF16)
        bias_left = sb("bias_left", [32, 2, DK0])
        cos = sb("cos", [128, DK0])
        sin = sb("sin", [128, DK0])
        mask_f = sb("mask_f", [128, 128])
        mask = sb("mask", [128, 4, 128], BF16)
        ident_b = sb("ident_b", [128, 128], BF16)
        gb = sb("gb", [128, 2, KD])
        out_bias = sb("out_bias", [128, D])
        out_const = sb("out_const", [128, D])
        bv_col = sb("bv_col", [128, HEADS0])
        mean2 = sb("mean2", [128, B])
        rstd2 = sb("rstd2", [128, B])
        xn = sb("xn", [128, D])
        xT_full = sb("xT_full", [128, KD, 128])
        xT_hi = sb("xT_hi", [128, KD, 128], F32R)
        xT_lo = sb("xT_lo", [128, KD, 128], F32R)
        roped_q = sb("roped_q", [128, 2, QW])
        roped_k = sb("roped_k", [128, 2, QW])
        sin_q = sb("sin_q", [128, QW])
        sin_k = sb("sin_k", [128, QW])
        qT = sb("qT", [128, 4, 128])
        kT = sb("kT", [128, 4, 128])
        V = sb("V", [128, 4, QW])
        P = sb("P", [128, 4, 128])
        PT = sb("PT", [128, 4, 128])
        oT = sb("oT", [128, 4, 128])
        neg_max = sb("neg_max", [128, QUADS, 4])
        exp_sum = sb("exp_sum", [128, QUADS, 4])
        inv_sum = sb("inv_sum", [128, QUADS, 4])

        x_loaded = sem("x_loaded")
        consts_loaded = sem("consts_loaded")
        wo_loaded = sem("wo_loaded")
        stage_loaded = [sem("stage0_loaded"), sem("stage1_loaded")]
        weights_rounded = sem("weights_rounded")
        weights_split = sem("weights_split")
        bias_split = sem("bias_split")
        bias_placed = sem("bias_placed")
        consts_made = sem("consts_made")
        const_projected = sem("const_projected")
        const_ready = sem("const_ready")
        ln0 = sem("ln0")
        rstd_ready = sem("rstd_ready")
        half_set = sem("half_set")
        xn_ready = sem("xn_ready")
        x_transposed = sem("x_transposed")
        xT_evacuated = sem("xT_evacuated")
        xT_split = sem("xT_split")
        q_projected = sem("q_projected")
        k_projected = sem("k_projected")
        v_projected = sem("v_projected")
        q_products = sem("q_products")
        k_products = sem("k_products")
        q_roped = sem("q_roped")
        k_roped = sem("k_roped")
        v_ready = sem("v_ready")
        q_transposed = sem("q_transposed")
        k_transposed = sem("k_transposed")
        qT_ready = sem("qT_ready")
        kT_ready = sem("kT_ready")
        scored = sem("scored")
        max_found = sem("max_found")
        exps_done = sem("exps_done")
        inv_ready = sem("inv_ready")
        probs_ready = sem("probs_ready")
        p_transposed = sem("p_transposed")
        PT_ready = sem("PT_ready")
        pv_done = sem("pv_done")
        oT_ready = sem("oT_ready")
        out_projected = sem("out_projected")
        out_added = sem("out_added")

        Q, K, V_, QT, KT, SC, PO, OUT = bank
        w_src = [a[n].rearrange("(k p) n -> p k n", p=128) for n in ("wqT", "wkT", "wvT")]
        ITEMS = [(q, w) for q in range(QUADS) for w in range(3)]

        with nc.Block() as block:
            @block.sync
            def _(sp):
                sp.dma_start(X[:], a["x"].rearrange("b p d -> p b d")).then_inc(x_loaded, 16)
                sp.dma_start(ident[:], a["ident"]).then_inc(consts_loaded, 16)
                sp.dma_start(mask_f[:], a["causal"]).then_inc(consts_loaded, 16)
                sp.dma_start(cos[:], a["cos"]).then_inc(consts_loaded, 16)
                sp.dma_start(sin[:], a["sin"]).then_inc(consts_loaded, 16)
                sp.dma_start(gb[:, 0, :], a["ln_gT"]).then_inc(consts_loaded, 16)
                sp.dma_start(gb[:, 1, :], a["ln_bT"]).then_inc(consts_loaded, 16)
                sp.dma_start(bias_in[0:16, :], a["L0_attn_bq"].rearrange("(h n) -> h n", n=DK0)).then_inc(consts_loaded, 16)
                sp.dma_start(bias_in[16:32, :], a["L0_attn_bk"].rearrange("(h n) -> h n", n=DK0)).then_inc(consts_loaded, 16)
                sp.dma_start(bv_col[:], a["bvT"]).then_inc(consts_loaded, 16)
                sp.dma_start(out_bias[:], a["L0_attn_bo"].rearrange("(a n) -> a n", a=1).broadcast_to([128, D])).then_inc(consts_loaded, 16)
                for i, (q, w) in enumerate(ITEMS):
                    wait(sp, weights_split, i - 1)
                    sp.dma_start(stage[:, i % 2, :, :], w_src[w][:, :, q * QW:(q + 1) * QW]).then_inc(stage_loaded[i % 2], 16)
                    if i == 2:
                        sp.wait_ge(bias_split, 5)
                        for part in range(3):
                            sp.dma_start(qk_bias[part:part + 1, :].rearrange("a (h n) -> a h n", n=DK0),
                                         bias_part[:, part, :]).then_inc(bias_placed, 16)
                    if i == 5:
                        sp.dma_start(WO[:], a["woT"].rearrange("(h p) n -> p h n", p=DK0)).then_inc(wo_loaded, 16)

            @block.gpsimd
            def _(pool):
                nc.gpsimd.memset(minus_half[:], -0.5).then_inc(half_set, 1)
                pool.wait_ge(half_set, 1)
                pool.wait_ge(ln0, 16 + 7)
                nc.gpsimd.tensor_tensor(rstd[:], var_eps[:], minus_half[:], ALU.pow).then_inc(rstd_ready, 1)
                pool.wait_ge(ln0, 16 + 7 + 32 + 7)
                nc.gpsimd.tensor_tensor(rstd2[:], var_eps[:], minus_half[:], ALU.pow).then_inc(rstd_ready, 1)

                def step(t, q):
                    p = q % 2
                    pool.wait_ge(q_products, 2 * t + 2)
                    nc.gpsimd.tensor_tensor(roped_q[:, p, :], roped_q[:, p, :], sin_q[:], ALU.add).then_inc(q_roped, 1)
                    pool.wait_ge(k_products, 2 * t + 2)
                    nc.gpsimd.tensor_tensor(roped_k[:, p, :], roped_k[:, p, :], sin_k[:], ALU.add).then_inc(k_roped, 1)

                with pool.Fori(0, B) as b:
                    for q in range(QUADS):
                        step(b * QUADS + q, q)

            @block.scalar
            def _(act):
                def round_weights(i):
                    q, w = ITEMS[i]
                    act.wait_ge(stage_loaded[i % 2], 16 * (i // 2 + 1))
                    nc.scalar.activation(WH[:, w, :, q * QW:(q + 1) * QW], stage[:, i % 2, :, :], ACT.Copy).then_inc(weights_rounded, 1)

                def evacuate_xT(b):
                    act.wait_ge(x_transposed, b + 1)
                    for k in range(KD):
                        wait(act, xT_split, 2 * b)
                        nc.scalar.activation(xT_full[:, k, :], V_[:, k * 128:(k + 1) * 128], ACT.Identity,
                                             bias=gb[:, 1, k:k + 1], scale=gb[:, 0, k:k + 1]).then_inc(xT_evacuated, 1)

                def step(s, q, b, first=False, last=False, drain=False):
                    u = s - 2
                    if not (isinstance(u, int) and u < 0):
                        uq = (q + 2) % 4
                        for h in range(4):
                            act.wait_ge(max_found, 1 + u)
                            wait(act, p_transposed, u)
                            ins = nc.scalar.activation(P[:, h, :], SC[:, h * 128:(h + 1) * 128], ACT.Exp,
                                                       bias=neg_max[:, uq, h:h + 1], accum_out=exp_sum[:, uq, h:h + 1])
                        ins.then_inc(exps_done, 1)
                    if not drain:
                        act.wait_ge(v_projected, s + 1)
                        wait(act, pv_done, s - 3)
                        nc.scalar.activation(V[:, q, :], V_[:], ACT.Copy).then_inc(v_ready, 1)
                        if first and q < 3:
                            for i in range(3 * q + 3, 3 * q + 6):
                                round_weights(i)
                    u = s - 1
                    if not (isinstance(u, int) and (u < 0 or u >= STEPS0)):
                        act.wait_ge(q_transposed, u + 1)
                        wait(act, scored, u)
                        nc.scalar.activation(qT[:].rearrange("p h n -> p (h n)"), QT[:], ACT.Copy, scale=1.0 / DK0 ** 0.5).then_inc(qT_ready, 1)
                        act.wait_ge(k_transposed, u + 1)
                        nc.scalar.activation(kT[:].rearrange("p h n -> p (h n)"), KT[:], ACT.Copy).then_inc(kT_ready, 1)
                    u = s - 2
                    if not (isinstance(u, int) and u < 0):
                        act.wait_ge(p_transposed, u + 1)
                        wait(act, pv_done, u)
                        nc.scalar.activation(PT[:].rearrange("p h n -> p (h n)"), PO[:], ACT.Copy).then_inc(PT_ready, 1)
                        act.wait_ge(pv_done, u + 1)
                        wait(act, out_projected, u)
                        nc.scalar.activation(oT[:].rearrange("p h n -> p (h n)"), PO[:], ACT.Copy).then_inc(oT_ready, 1)
                    if q == 2 and not last and not drain:
                        evacuate_xT(b + 1)

                for i in range(3):
                    round_weights(i)
                act.wait_ge(consts_loaded, 160)
                evacuate_xT(0)
                for q in range(QUADS):
                    step(q, q, 0, first=True)
                with act.Fori(1, B - 1) as b:
                    for q in range(QUADS):
                        step(b * QUADS + q, q, b)
                for q in range(QUADS):
                    step((B - 1) * QUADS + q, q, B - 1, last=True)
                for s in (STEPS0, STEPS0 + 1):
                    step(s, s % 4, B, drain=True)

            @block.vector
            def _(dve):
                dve.wait_ge(x_loaded, 16)
                with dve.Fori(0, B) as b:
                    nc.vector.bn_stats(batch(stats, b), batch(X, b)).then_inc(ln0, 1)
                dve.wait_ge(ln0, 16)
                n = finish_stats(nc, dve, ln0, 16, stats, mean[:], var_eps[:], ln_tmp, LN_EPS)
                dve.wait_ge(ln0, n)
                dve.wait_ge(rstd_ready, 1)
                with dve.Fori(0, B) as b:
                    nc.vector.tensor_scalar(batch(H, b), batch(X, b), one(mean, b), one(rstd, b), ALU.subtract, ALU.mult).then_inc(ln0, 1)
                    dve.wait_ge(ln0, 2 * b + n + 1)
                    nc.vector.bn_stats(batch(stats, b), batch(H, b)).then_inc(ln0, 1)
                    nc.vector.tensor_tensor(batch(X, b), batch(X, b), batch(H, b), ALU.add)
                dve.wait_ge(ln0, n + 32)
                n = finish_stats(nc, dve, ln0, n + 32, stats, mean2[:], var_eps[:], ln_tmp, LN_EPS)
                dve.wait_ge(ln0, n)

                dve.wait_ge(consts_loaded, 160)
                nc.vector.tensor_copy(ident_b[:], ident[:]).then_inc(consts_made, 1)
                for h in range(4):
                    nc.vector.tensor_copy(mask[:, h, :], mask_f[:]).then_inc(consts_made, 1)
                nc.vector.memset(ones_row[:], 0.0).then_inc(consts_made, 1)
                nc.vector.memset(qk_bias[:], 0.0).then_inc(consts_made, 1)
                dve.wait_ge(consts_made, 7)
                nc.vector.memset(ones_row[0:3, :], 1.0).then_inc(consts_made, 1)
                nc.vector.tensor_copy(bias_part[:, 0, :], bias_in[:]).then_inc(bias_split, 1)
                dve.wait_ge(bias_split, 1)
                nc.vector.tensor_tensor(bias_left[:, 0, :], bias_in[:], bias_part[:, 0, :], ALU.subtract).then_inc(bias_split, 1)
                dve.wait_ge(bias_split, 2)
                nc.vector.tensor_copy(bias_part[:, 1, :], bias_left[:, 0, :]).then_inc(bias_split, 1)
                dve.wait_ge(bias_split, 3)
                nc.vector.tensor_tensor(bias_left[:, 1, :], bias_left[:, 0, :], bias_part[:, 1, :], ALU.subtract).then_inc(bias_split, 1)
                dve.wait_ge(bias_split, 4)
                nc.vector.tensor_copy(bias_part[:, 2, :], bias_left[:, 1, :]).then_inc(bias_split, 1)

                def split_weights(i):
                    q, w = ITEMS[i]
                    dve.wait_ge(weights_rounded, i + 1)
                    cols = slice(q * QW, (q + 1) * QW)
                    nc.vector.tensor_tensor(WL[:, w, :, cols], stage[:, i % 2, :, :], WH[:, w, :, cols].bitcast(F32), ALU.subtract).then_inc(weights_split, 1)

                def normalise(b):
                    wait(dve, x_transposed, b)
                    nc.vector.tensor_scalar(xn[:], batch(H, b), one(mean2, b), one(rstd2, b), ALU.subtract, ALU.mult).then_inc(xn_ready, 1)

                def split_xT(b):
                    dve.wait_ge(xT_evacuated, 2 * b + 2)
                    wait(dve, v_projected, 4 * b)
                    nc.vector.tensor_copy(xT_hi[:], xT_full[:]).then_inc(xT_split, 1)
                    dve.wait_ge(xT_split, 2 * b + 1)
                    nc.vector.tensor_tensor(xT_lo[:], xT_full[:], xT_hi[:].bitcast(F32), ALU.subtract).then_inc(xT_split, 1)

                def rope(t, p, src, projected, products, transposed, roped_sum, roped, sin_part):
                    dve.wait_ge(projected, t + 1)
                    wait(dve, transposed, t - 1)
                    quad = lambda ap: ap.rearrange("p (h n) -> p h n", h=4)
                    nc.vector.tensor_tensor(quad(roped[:, p, :]), quad(src[:]), cos[:].rearrange("p (h n) -> p h n", h=1).broadcast_to([128, 4, DK0]), ALU.mult).then_inc(products, 1)
                    wait(dve, roped_sum, t)
                    half = lambda ap, i: quad(ap)[:, :, i * 64:(i + 1) * 64]
                    for i in range(2):
                        ins = nc.vector.tensor_tensor(half(sin_part[:], i), half(src[:], 1 - i),
                                                      sin[:, i * 64:(i + 1) * 64].rearrange("p (h n) -> p h n", h=1).broadcast_to([128, 4, 64]), ALU.mult)
                    ins.then_inc(products, 1)

                def find_max(u, uq):
                    dve.wait_ge(scored, u + 1)
                    nc.vector.tensor_reduce(neg_max[:, uq, :], SC[:].rearrange("p (h n) -> p h n", h=4), AX.X, ALU.max, negate=True).then_inc(max_found, 1)

                def step(s, q, b, first=False, last=False, drain=False):
                    u, uq = s - 2, (q + 2) % 4
                    past = not (isinstance(u, int) and u < 0)
                    if past:
                        find_max(u, uq)
                    if not drain:
                        rope(s, q % 2, Q, q_projected, q_products, q_transposed, q_roped, roped_q, sin_q)
                    if past:
                        dve.wait_ge(exps_done, u + 1)
                        nc.vector.reciprocal(inv_sum[:, uq, :], exp_sum[:, uq, :]).then_inc(inv_ready, 1)
                        dve.wait_ge(inv_ready, u + 1)
                        nc.vector.tensor_tensor(P[:], P[:], inv_sum[:, uq, :].rearrange("p (h n) -> p h n", n=1).broadcast_to([128, 4, 128]), ALU.mult).then_inc(probs_ready, 1)
                    if not drain:
                        rope(s, q % 2, K, k_projected, k_products, k_transposed, k_roped, roped_k, sin_k)
                        if first and q < 3:
                            for i in range(3 * q + 3, 3 * q + 6):
                                split_weights(i)
                        if q == 1 and not last:
                            normalise(b + 1)
                        if q == 3 and not last:
                            split_xT(b + 1)

                def add_out(b):
                    dve.wait_ge(out_projected, 4 * b + 4)
                    nc.vector.tensor_tensor(batch(X, b), OUT[:, 0:D], batch(X, b), ALU.add).then_inc(out_added, 1)
                    dve.wait_ge(out_added, 2 * b + 1)
                    nc.vector.tensor_tensor(batch(X, b), batch(X, b), out_const[:], ALU.add).then_inc(out_added, 1)

                dve.wait_ge(rstd_ready, 2)
                normalise(0)
                for i in range(3):
                    split_weights(i)
                split_xT(0)
                for q in range(QUADS):
                    step(q, q, 0, first=True)
                dve.wait_ge(const_projected, 1)
                nc.vector.tensor_tensor(out_const[:], KT[:, 0:D], out_bias[:], ALU.add).then_inc(const_ready, 1)
                dve.wait_ge(const_ready, 1)
                with dve.Fori(1, B - 1) as b:
                    for q in range(QUADS):
                        step(b * QUADS + q, q, b)
                        if q == 2:
                            add_out(b - 1)
                for q in range(QUADS):
                    step((B - 1) * QUADS + q, q, B - 1, last=True)
                    if q == 2:
                        add_out(B - 2)
                for s in (STEPS0, STEPS0 + 1):
                    step(s, s % 4, B, drain=True)
                add_out(B - 1)

            @block.tensor
            def _(pe):
                def transpose_x(b):
                    pe.wait_ge(xn_ready, b + 1)
                    wait(pe, v_ready, 4 * b - 1)
                    for k in range(KD):
                        ins = nc.tensor.transpose(V_[:, k * 128:(k + 1) * 128], xn[:, k * 128:(k + 1) * 128], ident[:])
                    ins.then_inc(x_transposed, 1)

                def project(t, q, b):
                    if q == 0:
                        pe.wait_ge(xT_split, 2 * b + 2)
                    cols = slice(q * QW, (q + 1) * QW)
                    for w, (dst, done, free, n_free) in enumerate((
                            (Q, q_projected, q_products, 2 * t),
                            (K, k_projected, k_products, 2 * t),
                            (V_, v_projected, v_ready, t))):
                        wait(pe, free, n_free)
                        if isinstance(t, int) and t < QUADS:
                            pe.wait_ge(weights_split, 3 * q + w + 1)
                            if t == 0 and w == 0:
                                pe.wait_ge(consts_made, 8)
                                pe.wait_ge(bias_placed, 48)
                        if w == 2 and q == 3:
                            wait(pe, xT_evacuated, 4 + 2 * b) if not (isinstance(b, int) and b == B - 1) else None
                        if w < 2:
                            nc.tensor.matmul(dst[:], ones_row[:], qk_bias[:, w * HEADS0 * DK0 + q * QW:w * HEADS0 * DK0 + (q + 1) * QW], start=True, stop=False)
                        for k in range(KD):
                            ins = matmul3(nc, dst[:], (xT_hi[:, k, :], xT_lo[:, k, :]), (WH[:, w, k, cols], WL[:, w, k, cols]),
                                          first=(w == 2 and k == 0), last=(k == KD - 1))
                        ins.then_inc(done, 1)

                def transpose_qk(u, uq):
                    for src, ready, dst, done, free in ((roped_q, q_roped, QT, q_transposed, qT_ready), (roped_k, k_roped, KT, k_transposed, kT_ready)):
                        pe.wait_ge(ready, u + 1)
                        wait(pe, free, u)
                        for h in range(4):
                            ins = nc.tensor.transpose(dst[:, h * 128:(h + 1) * 128], src[:, uq % 2, h * 128:(h + 1) * 128], ident[:])
                        ins.then_inc(done, 1)

                def transpose_p(u):
                    pe.wait_ge(probs_ready, u + 1)
                    wait(pe, oT_ready, u)
                    for h in range(4):
                        ins = nc.tensor.transpose(PO[:, h * 128:(h + 1) * 128], P[:, h, :], ident[:])
                    ins.then_inc(p_transposed, 1)

                def out_project(u, uq):
                    pe.wait_ge(oT_ready, u + 1)
                    if uq == 0:
                        wait(pe, out_added, u // 4 * 2 if isinstance(u, int) else None) if isinstance(u, int) else pe.wait_ge(out_added, out_count[0])
                    for h in range(4):
                        ins = nc.tensor.matmul(OUT[:, 0:D], oT[:, h, :], WO[:, 4 * uq + h, :], start=(uq == 0 and h == 0), stop=(uq == 3 and h == 3))
                    ins.then_inc(out_projected, 1)

                def score(u):
                    pe.wait_ge(qT_ready, u + 1)
                    pe.wait_ge(kT_ready, u + 1)
                    wait(pe, exps_done, u)
                    nc.tensor.matmul(SC[:], ident_b[:], mask[:].rearrange("p h n -> p (h n)"), start=True, stop=True)
                    for h in range(4):
                        ins = nc.tensor.matmul(SC[:, h * 128:(h + 1) * 128], qT[:, h, :], kT[:, h, :], start=False, stop=True, skip_group_check=True)
                    ins.then_inc(scored, 1)

                def weigh(u, uq):
                    pe.wait_ge(PT_ready, u + 1)
                    for h in range(4):
                        ins = nc.tensor.matmul(PO[:, h * 128:(h + 1) * 128], V[:, uq, h * 128:(h + 1) * 128], PT[:, h, :], start=True, stop=True)
                    ins.then_inc(pv_done, 1)

                out_count = [0]

                def step(s, q, b, last=False):
                    live = lambda u: not isinstance(u, int) or 0 <= u < STEPS0
                    if live(s):
                        project(s, q, b)
                    if live(s - 1):
                        transpose_qk(s - 1, (q + 3) % 4)
                    if live(s - 2):
                        transpose_p(s - 2)
                    if live(s - 3):
                        if not isinstance(b, int):
                            out_count[0] = 2 * b
                        out_project(s - 3, (q + 1) % 4)
                    if live(s - 1):
                        score(s - 1)
                    if live(s - 2):
                        weigh(s - 2, (q + 2) % 4)
                    if q == 2 and not last:
                        transpose_x(b + 1)

                pe.wait_ge(consts_loaded, 160)
                transpose_x(0)
                for q in range(QUADS):
                    step(q, q, 0)
                pe.wait_ge(wo_loaded, 16)
                pe.wait_ge(kT_ready, 3)
                for h in range(HEADS0):
                    ins = nc.tensor.matmul(KT[:, 0:D], bv_col[:, h:h + 1].broadcast_to([128, 128]), WO[:, h, :], start=(h == 0), stop=(h == HEADS0 - 1))
                ins.then_inc(const_projected, 1)
                pe.wait_ge(const_ready, 1)
                with pe.Fori(1, B - 1) as b:
                    for q in range(QUADS):
                        step(b * QUADS + q, q, b)
                for q in range(QUADS):
                    step((B - 1) * QUADS + q, q, B - 1, last=True)
                for s in range(STEPS0, STEPS0 + 3):
                    step(s, s % 4, B, last=True)

def live(u, n=B):
    return not isinstance(u, int) or 0 <= u < n


def run_pairs(eng, step, extra, peeled=1):
    for s in range(2 * peeled):
        step(s, s % 2)
    with eng.Fori(peeled, B // 2 - 1) as i:
        for j in range(2):
            step(i * 2 + j, j)
    for s in range(B - 2, B + extra):
        step(s, s % 2)


def phase_retention(nc, a, sem, sb_, bank, X, ident, mean, var_eps, rstd, minus_half, stats, ln_tmp):
    local = ExitStack()
    with local:
        def sb(name, shape, dt=F32):
            return sb_(name, shape, dt, local)

        H_ = 2
        V = sb("ret_V", [128, H_, B, 128])
        gate = sb("ret_gate", [128, B, D])
        O = sb("ret_O", [128, B, D])
        AT = sb("ret_AT", [128, H_, 128])
        decay = sb("ret_decay", [128, H_, 128])
        Wh = sb("ret_Wh", [128, H_, 128])
        WhT = sb("ret_WhT", [128, H_, 128])
        G = sb("ret_G", [128, H_, 128])
        w_in = sb("ret_w_in", [128, 2, KD, D])
        w_hi = sb("ret_w_hi", [128, 2, KD, D], F32R)
        w_lo = sb("ret_w_lo", [128, 2, KD, D], F32R)
        gn = sb("ret_gn", [128, 2, D])
        ctxT = sb("ret_ctxT", [128, 2, H_, 128])
        xn = sb("ret_xn", [128, 2, D])
        xT_full = sb("ret_xT_full", [128, 2, KD, 128])
        xT_hi = sb("ret_xT_hi", [128, 2, KD, 128], F32R)
        xT_lo = sb("ret_xT_lo", [128, 2, KD, 128], F32R)
        TT = sb("ret_TT", [128, 2, H_, 128])
        zeros = sb("ret_zeros", [128, D], BF16)

        consts = sem("ret_consts")
        ctx_loaded = [sem("ret_ctx0"), sem("ret_ctx1")]
        w_rounded = sem("ret_w_rounded")
        w_split = sem("ret_w_split")
        zeroed = sem("ret_zeroed")
        gram_done = sem("ret_gram_done")
        G_ready = sem("ret_G_ready")
        ln = sem("ret_ln")
        rstd_ready = sem("ret_rstd")
        xn_ready = sem("ret_xn_ready")
        transposed = sem("ret_transposed")
        full_ready = sem("ret_full_ready")
        hi_ready = sem("ret_hi_ready")
        lo_ready = sem("ret_lo_ready")
        T_done = sem("ret_T_done")
        gate_done = sem("ret_gate_done")
        TT_ready = sem("ret_TT_ready")
        V_ready = sem("ret_V_ready")
        gate_ready = sem("ret_gate_ready")
        scored = sem("ret_scored")
        AT_ready = sem("ret_AT_ready")

        with nc.Block() as block:
            @block.sync
            def _(sp):
                for dst, src in ((WhT[:], a["WhT"]), (Wh[:], a["L0_xattn_Wh"].rearrange("h e d -> e h d")),
                                 (w_in[:, 0], a["L0_xattn_wg_w"].rearrange("(k p) n -> p k n", p=128)),
                                 (w_in[:, 1], a["L0_xattn_wo_w"].rearrange("(k p) n -> p k n", p=128)),
                                 (decay[:], a["decayT"]),
                                 (gn[:, 0, :], a["L0_xattn_gn_gamma"].rearrange("(a n) -> a n", a=1).broadcast_to([128, D])),
                                 (gn[:, 1, :], a["L0_xattn_gn_beta"].rearrange("(a n) -> a n", a=1).broadcast_to([128, D]))):
                    sp.dma_start(dst, src).then_inc(consts, 16)

                def step(s, j):
                    if live(s):
                        wait(sp, scored, s - 1)
                        sp.dma_start(ctxT[:, j], ctx_columns(a, s)).then_inc(ctx_loaded[j], 16)
                run_pairs(sp, step, 0)

            @block.gpsimd
            def _(pool):
                pool.wait_ge(ln, B + 7)
                nc.gpsimd.tensor_tensor(rstd[:], var_eps[:], minus_half[:], ALU.pow).then_inc(rstd_ready, 1)

            @block.scalar
            def _(act):
                act.wait_ge(consts, 112)
                nc.scalar.activation(w_hi[:], w_in[:], ACT.Copy).then_inc(w_rounded, 1)
                act.wait_ge(gram_done, 1)
                nc.scalar.activation(G[:].rearrange("p h n -> p (h n)"), bank[7][:, 0:256], ACT.Copy).then_inc(G_ready, 1)

                def step(s, j):
                    if live(s):
                        act.wait_ge(transposed, s + 1)
                        wait(act, gate_done, s - 1)
                        nc.scalar.activation(flat(xT_full[:, j]), bank[j][:, 0:256], ACT.Copy).then_inc(full_ready, 1)
                        nc.scalar.activation(flat(xT_hi[:, j]), bank[j][:, 0:256], ACT.Copy).then_inc(hi_ready, 1)
                    if live(s - 1):
                        act.wait_ge(T_done, s)
                        wait(act, scored, s - 2)
                        nc.scalar.activation(flat(TT[:, 1 - j]), bank[3 - j][:, 0:256], ACT.Copy).then_inc(TT_ready, 1)
                run_pairs(act, step, 1)

            @block.vector
            def _(dve):
                with dve.Fori(0, B) as b:
                    nc.vector.bn_stats(batch(stats, b), batch(X, b)).then_inc(ln, 1)
                dve.wait_ge(ln, B)
                n = finish_stats(nc, dve, ln, B, stats, mean[:], var_eps[:], ln_tmp, LN_EPS)
                nc.vector.memset(zeros[:], 0.0).then_inc(zeroed, 1)
                dve.wait_ge(w_rounded, 1)
                nc.vector.tensor_tensor(w_lo[:], w_in[:], w_hi[:].bitcast(F32), ALU.subtract).then_inc(w_split, 1)
                dve.wait_ge(rstd_ready, 1)
                dve.wait_ge(ln, n)

                def normalise(b, j):
                    wait(dve, transposed, b - 1)
                    nc.vector.tensor_scalar(xn[:, j, :], batch(X, b), one(mean, b), one(rstd, b), ALU.subtract, ALU.mult).then_inc(xn_ready, 1)

                normalise(0, 0)

                def step(s, j):
                    if live(s + 1):
                        normalise(s + 1, 1 - j)
                    if live(s):
                        dve.wait_ge(hi_ready, s + 1)
                        nc.vector.tensor_tensor(flat(xT_lo[:, j]), flat(xT_full[:, j]), flat(xT_hi[:, j]).bitcast(F32), ALU.subtract).then_inc(lo_ready, 1)
                    if live(s - 1):
                        dve.wait_ge(gate_done, s)
                        v_out = V[:, :, s - 1, :] if isinstance(s, int) else V[:, :, bass.ds(s - 1, 1), :].rearrange("p h a n -> p h (a n)")
                        nc.vector.tensor_scalar(v_out, bank[5 - j][:, 256:512].rearrange("p (h n) -> p h n", h=H_), 1.0, None, ALU.mult).then_inc(V_ready, 1)
                        nc.vector.tensor_scalar(batch(gate, s - 1), bank[5 - j][:, 0:D], 0.0, None, ALU.max).then_inc(gate_ready, 1)
                run_pairs(dve, step, 1)
                dve.wait_ge(scored, B)
                nc.vector.tensor_tensor(flat(AT[:]), bank[6][:, 0:256], flat(decay[:]), ALU.mult).then_inc(AT_ready, 1)
                dve.wait_ge(AT_ready, 1)
                nc.vector.scalar_tensor_tensor(flat(AT[:]), flat(AT[:]), -1.0, flat(AT[:]), ALU.mult, ALU.max).then_inc(AT_ready, 1)
                dve.wait_ge(AT_ready, 2)
                nc.vector.tensor_scalar(flat(AT[:]), flat(AT[:]), 1.0, None, ALU.max).then_inc(AT_ready, 1)

            @block.tensor
            def _(pe):
                pe.wait_ge(consts, 112)
                for h in range(H_):
                    ins = nc.tensor.matmul(bank[7][:, h * 128:(h + 1) * 128], WhT[:, h, :], WhT[:, h, :], start=True, stop=True)
                ins.then_inc(gram_done, 1)
                pe.wait_ge(zeroed, 1)
                nc.tensor.matmul(bank[6][:, 0:256], zeros[:, 0:128], zeros[:], start=True, stop=True)
                pe.wait_ge(G_ready, 1)
                pe.wait_ge(w_split, 1)

                def step(s, j):
                    if live(s):
                        pe.wait_ge(xn_ready, s + 1)
                        wait(pe, hi_ready, s - 1)
                        for k in range(KD):
                            ins = nc.tensor.transpose(bank[j][:, k * 128:(k + 1) * 128], xn[:, j, k * 128:(k + 1) * 128], ident[:])
                        ins.then_inc(transposed, 1)
                    u, i = s - 1, 1 - j
                    if live(u):
                        pe.wait_ge(full_ready, u + 1)
                        pe.wait_ge(ctx_loaded[i], 16 * (u // 2 + 1) if isinstance(u, int) else pair_count(s, j, i))
                        wait(pe, TT_ready, u - 1)
                        for h in range(H_):
                            ins = nc.tensor.matmul(bank[2 + i][:, h * 128:(h + 1) * 128], G[:, h, :], xT_full[:, i, h, :], start=True, stop=True)
                        ins.then_inc(T_done, 1)
                        wait(pe, gate_ready, u - 1)
                        for h in range(H_):
                            nc.tensor.matmul(bank[4 + i][:, 256 + h * 128:256 + (h + 1) * 128], ctxT[:, i, h, :], Wh[:, h, :], start=True, stop=True)
                        pe.wait_ge(lo_ready, u + 1)
                        for k in range(KD):
                            ins = matmul3(nc, bank[4 + i][:, 0:D], (xT_hi[:, i, k, :], xT_lo[:, i, k, :]), (w_hi[:, 0, k, :], w_lo[:, 0, k, :]),
                                          first=(k == 0), last=(k == KD - 1))
                        ins.then_inc(gate_done, 1)
                    u = s - 2
                    if live(u):
                        pe.wait_ge(TT_ready, u + 1)
                        for h in range(H_):
                            ins = nc.tensor.matmul(bank[6][:, h * 128:(h + 1) * 128], ctxT[:, j, h, :], TT[:, j, h, :], start=False, stop=True, skip_group_check=True)
                        ins.then_inc(scored, 1)
                run_pairs(pe, step, 2)

        vproj = sem("ret_av_done")
        O_ready = sem("ret_O_ready")
        ln2 = sem("ret_ln2")
        rstd2_ready = sem("ret_rstd2")
        shaped = sem("ret_shaped")
        wy_ready = sem("ret_wy_ready")
        wy_transposed = sem("ret_wy_transposed")
        wyT_full_ready = sem("ret_wyT_full")
        wyT_ready = sem("ret_wyT_hi")
        wyT_lo_ready = sem("ret_wyT_lo")
        wo_done = sem("ret_wo_done")
        added = sem("ret_added")
        y = sb("ret_y", [128, 2, D])
        GROUP = 4
        with nc.Block() as block:
            @block.gpsimd
            def _(pool):
                pool.wait_ge(ln2, B + 7)
                nc.gpsimd.tensor_tensor(rstd[:], var_eps[:], minus_half[:], ALU.pow).then_inc(rstd2_ready, 1)

            @block.tensor
            def _(pe):
                for g in range(B // GROUP):
                    for h in range(H_):
                        wait(pe, O_ready, 2 * (g - 1) + h - 1)
                        nc.tensor.matmul(bank[2 * (g % 2) + h][:], AT[:, h, :], V[:, h, g * GROUP:(g + 1) * GROUP, :].rearrange("p b n -> p (b n)"),
                                         start=True, stop=True).then_inc(vproj, 1)

                def step(s, j):
                    if live(s):
                        pe.wait_ge(wy_ready, s + 1)
                        wait(pe, wyT_ready, s - 1)
                        for k in range(KD):
                            ins = nc.tensor.transpose(bank[4 + j][:, k * 128:(k + 1) * 128], xn[:, j, k * 128:(k + 1) * 128], ident[:])
                        ins.then_inc(wy_transposed, 1)
                    u, i = s - 1, 1 - j
                    if live(u):
                        pe.wait_ge(wyT_lo_ready, u + 1)
                        wait(pe, added, u - 1)
                        for k in range(KD):
                            ins = matmul3(nc, bank[6 + i][:, 0:D], (xT_hi[:, i, k, :], xT_lo[:, i, k, :]), (w_hi[:, 1, k, :], w_lo[:, 1, k, :]),
                                          first=(k == 0), last=(k == KD - 1))
                        ins.then_inc(wo_done, 1)
                run_pairs(pe, step, 1)

            @block.scalar
            def _(act):
                def step(s, j):
                    if live(s):
                        act.wait_ge(wy_transposed, s + 1)
                        wait(act, wo_done, s - 1)
                        nc.scalar.activation(flat(xT_full[:, j]), bank[4 + j][:, 0:256], ACT.Copy).then_inc(wyT_full_ready, 1)
                        nc.scalar.activation(flat(xT_hi[:, j]), bank[4 + j][:, 0:256], ACT.Copy).then_inc(wyT_ready, 1)
                run_pairs(act, step, 0)

            @block.vector
            def _(dve):
                for g in range(B // GROUP):
                    for h in range(H_):
                        dve.wait_ge(vproj, 2 * g + h + 1)
                        nc.vector.tensor_copy(O[:, g * GROUP:(g + 1) * GROUP, h * 128:(h + 1) * 128],
                                              bank[2 * (g % 2) + h][:].rearrange("p (b n) -> p b n", b=GROUP)).then_inc(O_ready, 1)
                dve.wait_ge(O_ready, 2 * B // GROUP)
                with dve.Fori(0, B) as b:
                    nc.vector.bn_stats(batch(stats, b), batch(O, b)).then_inc(ln2, 1)
                dve.wait_ge(ln2, B)
                n = finish_stats(nc, dve, ln2, B, stats, mean[:], var_eps[:], ln_tmp, 1e-3)
                dve.wait_ge(rstd2_ready, 1)
                dve.wait_ge(ln2, n)

                def shape_y(b, j):
                    nc.vector.tensor_scalar(y[:, j, :], batch(O, b), one(mean, b), one(rstd, b), ALU.subtract, ALU.mult).then_inc(shaped, 1)
                    dve.wait_ge(shaped, b * 3 + 1)
                    nc.vector.tensor_tensor(y[:, j, :], y[:, j, :], gn[:, 0, :], ALU.mult).then_inc(shaped, 1)
                    dve.wait_ge(shaped, b * 3 + 2)
                    nc.vector.tensor_tensor(y[:, j, :], y[:, j, :], gn[:, 1, :], ALU.add).then_inc(shaped, 1)
                    dve.wait_ge(shaped, b * 3 + 3)
                    wait(dve, wy_transposed, b - 1)
                    nc.vector.tensor_tensor(xn[:, j, :], y[:, j, :], batch(gate, b), ALU.mult).then_inc(wy_ready, 1)

                shape_y(0, 0)

                def step(s, j):
                    if live(s + 1):
                        shape_y(s + 1, 1 - j)
                    if live(s):
                        dve.wait_ge(wyT_ready, s + 1)
                        nc.vector.tensor_tensor(flat(xT_lo[:, j]), flat(xT_full[:, j]), flat(xT_hi[:, j]).bitcast(F32), ALU.subtract).then_inc(wyT_lo_ready, 1)
                    if live(s - 1):
                        dve.wait_ge(wo_done, s)
                        nc.vector.tensor_tensor(batch(X, s - 1), bank[7 - j][:, 0:D], batch(X, s - 1), ALU.add).then_inc(added, 1)
                run_pairs(dve, step, 1)


def flat(ap):
    return ap.rearrange("p h n -> p (h n)")


def pair_count(s, j, i, ahead=-1):
    if ahead < 0:
        return (s - j) * 8 + (16 if i < j else 0)
    return (s - j) * 8 + (16 if j < i else 32)


def ctx_columns(a, b):
    view = a["ctxT"].rearrange("(k p) n -> p k n", p=128)
    return view[:, :, b * S:(b + 1) * S] if isinstance(b, int) else view[:, :, bass.ds(b * S, S)]

def phase_spline(nc, a, sem, sb_, bank, X, ident, mean, var_eps, rstd, minus_half, stats, ln_tmp):
    local = ExitStack()
    with local:
        def sb(name, shape, dt=F32):
            return sb_(name, shape, dt, local)

        NT, W, GRID, NC_ = 64, 4, 16, 8
        BIG = 1e30
        TABW = 2 * W * GRID + 3
        H = sb("sp_H", [128, B, D])
        XF = sb("sp_XF", [128, B, D])
        sign = sb("sp_sign", [128, B, D])
        wide = sb("sp_wide", [128, B, D])
        gb = sb("sp_gb", [128, 2, D])
        slopes_in = sb("sp_slopes_in", [128, D, GRID])
        slope_sum = sb("sp_slope_sum", [128, D])
        slope_neg = sb("sp_slope_neg", [128, D])
        slope_sign = sb("sp_slope_sign", [128, D])
        tile_score = sb("sp_tile_score", [128, B, NT])
        cluster_score = sb("sp_cluster_score", [128, B, NC_])
        rank = sb("sp_rank", [128, NT + NC_ + GRID + 1])
        best = sb("sp_best", [128, 2, B])
        cluster_hot = sb("sp_cluster_hot", [128, B, NC_])
        hot = sb("sp_hot", [128, B, NT])
        xs = sb("sp_xs", [128, B, W])
        lo_hi = sb("sp_lo_hi", [128, 2, B])
        off = sb("sp_off", [128, B, NT])
        extreme = sb("sp_extreme", [128, 2, B, NT])
        tile_ext = sb("sp_tile_ext", [128, 2, NT])
        table = sb("sp_table", [NT, TABW])
        hot_b = sb("sp_hot_b", [128, 2, 128])
        hotT = sb("sp_hotT", [NT, 2, 128])
        found = sb("sp_found", [128, B, TABW])
        span = sb("sp_span", [128, 2, B])
        u = sb("sp_u", [128, B, W])
        ge = sb("sp_ge", [128, B * W, GRID + 1])
        cell = sb("sp_cell", [128, B, W, GRID])
        picked = sb("sp_picked", [128, 2, B, W, GRID])
        coef = sb("sp_coef", [128, 4, B, W])

        loaded = sem("sp_loaded")
        stat = sem("sp_stat")
        rstd_ready = sem("sp_rstd_ready")
        ext_ready = sem("sp_ext_ready")
        ext_transposed = sem("sp_ext_transposed")
        table_ready = sem("sp_table_ready")
        hot_copied = sem("sp_hot_copied")
        hot_transposed = sem("sp_hot_transposed")
        hotT_ready = sem("sp_hotT_ready")
        looked_up = sem("sp_looked_up")
        found_ready = sem("sp_found_ready")
        chain = sem("sp_chain")

        def row(name):
            return a[name].rearrange("(a n) -> a n", a=1).broadcast_to([128, D])

        with nc.Block() as block:
            @block.sync
            def _(sp):
                for dst, src in ((gb[:, 0, :], row("L0_ffn_ln_gamma")), (gb[:, 1, :], row("L0_ffn_ln_beta")),
                                 (slopes_in[:].rearrange("p d g -> p (d g)"),
                                  a["L0_ffn_spline_slopes"].rearrange("(a t) j g -> a (t j g)", a=1).broadcast_to([128, D * GRID])),
                                 (rank[:], a["rank"]),
                                 (table[:, 0:64], a["L0_ffn_spline_bases"].rearrange("t j g -> t (j g)")),
                                 (table[:, 64:128], a["L0_ffn_spline_slopes"].rearrange("t j g -> t (j g)")),
                                 (table[:, 128:129], a["L0_ffn_output_scale"].rearrange("(t a) -> t a", a=1))):
                    sp.dma_start(dst, src).then_inc(loaded, 16)

            @block.gpsimd
            def _(pool):
                pool.wait_ge(stat, B + 7)
                nc.gpsimd.tensor_tensor(rstd[:], var_eps[:], minus_half[:], ALU.pow).then_inc(rstd_ready, 1)
                pool.wait_ge(stat, 3 * B + 14)
                nc.gpsimd.tensor_tensor(rstd[:], var_eps[:], minus_half[:], ALU.pow).then_inc(rstd_ready, 1)

            @block.vector
            def _(dve):
                count = [0]

                def link(ins):
                    count[0] += 1
                    ins.then_inc(chain, 1)
                    dve.wait_ge(chain, count[0])

                TT, TS, STT = nc.vector.tensor_tensor, nc.vector.tensor_scalar, nc.vector.scalar_tensor_tensor
                with dve.Fori(0, B) as b:
                    nc.vector.bn_stats(batch(stats, b), batch(X, b)).then_inc(stat, 1)
                dve.wait_ge(stat, B)
                n = finish_stats(nc, dve, stat, B, stats, mean[:], var_eps[:], ln_tmp, LN_EPS)
                link(nc.vector.memset(hot_b[:], 0.0))
                dve.wait_ge(loaded, 112)
                link(nc.vector.tensor_reduce(slope_sum[:], slopes_in[:], AX.X, ALU.add))
                link(TS(slope_neg[:], slope_sum[:], 0.0, None, ALU.is_lt))
                link(STT(slope_sign[:], slope_sum[:], 0.0, slope_neg[:], ALU.is_gt, ALU.subtract))
                dve.wait_ge(stat, n)
                dve.wait_ge(rstd_ready, 1)
                with dve.Fori(0, B) as b:
                    TS(batch(H, b), batch(X, b), one(mean, b), one(rstd, b), ALU.subtract, ALU.mult).then_inc(stat, 1)
                    dve.wait_ge(stat, n + 1 + 2 * b)
                    nc.vector.bn_stats(batch(stats, b), batch(H, b)).then_inc(stat, 1)
                dve.wait_ge(stat, n + 2 * B)
                n = finish_stats(nc, dve, stat, n + 2 * B, stats, mean[:], var_eps[:], ln_tmp, LN_EPS)
                dve.wait_ge(stat, n)
                dve.wait_ge(rstd_ready, 2)
                with dve.Fori(0, B) as b:
                    TS(batch(XF, b), batch(H, b), one(mean, b), one(rstd, b), ALU.subtract, ALU.mult).then_inc(stat, 1)
                    TT(batch(X, b), batch(X, b), batch(H, b), ALU.add).then_inc(stat, 1)
                dve.wait_ge(stat, n + 2 * B)

                rows = lambda ap: ap.rearrange("p (a n) -> p a n", a=1).broadcast_to([128, B, D])
                link(TT(XF[:], XF[:], rows(gb[:, 0, :]), ALU.mult))
                link(TT(XF[:], XF[:], rows(gb[:, 1, :]), ALU.add))
                link(TS(wide[:], XF[:], 0.0, None, ALU.is_lt))
                link(STT(sign[:], XF[:], 0.0, wide[:], ALU.is_gt, ALU.subtract))
                link(TT(sign[:], sign[:], rows(slope_sign[:]), ALU.mult))
                link(nc.vector.tensor_reduce(tile_score[:], sign[:].rearrange("p b (t j) -> p b t j", j=W), AX.X, ALU.add))
                link(nc.vector.tensor_reduce(cluster_score[:], tile_score[:].rearrange("p b (c t) -> p b c t", t=8), AX.X, ALU.add))
                col = lambda lo, m: rank[:, lo:lo + m].rearrange("p (a n) -> p a n", a=1).broadcast_to([128, B, m])
                over = lambda ap, m: ap.rearrange("p (b n) -> p b n", n=1).broadcast_to([128, B, m])
                link(STT(cluster_score[:], cluster_score[:], float(NC_), col(NT, NC_), ALU.mult, ALU.add))
                link(nc.vector.tensor_reduce(best[:, 0, :], cluster_score[:], AX.X, ALU.max))
                link(TT(cluster_hot[:], cluster_score[:], over(best[:, 0, :], NC_), ALU.is_equal))
                link(STT(tile_score[:], tile_score[:], float(NT), col(0, NT), ALU.mult, ALU.add))
                link(TS(cluster_hot[:], cluster_hot[:], 4096.0, None, ALU.mult))
                link(TT(tile_score[:].rearrange("p b (c t) -> p (b c) t", t=8), tile_score[:].rearrange("p b (c t) -> p (b c) t", t=8),
                        cluster_hot[:].rearrange("p b (c a) -> p (b c) a", a=1).broadcast_to([128, B * NC_, 8]), ALU.add))
                link(nc.vector.tensor_reduce(best[:, 1, :], tile_score[:], AX.X, ALU.max))
                link(TT(hot[:], tile_score[:], over(best[:, 1, :], NT), ALU.is_equal))
                per_tile = lambda t: t[:].rearrange("p b (t j) -> p (b t) j", j=W)
                hot_wide = hot[:].rearrange("p b (t a) -> p (b t) a", a=1).broadcast_to([128, B * NT, W])
                link(TT(per_tile(wide), per_tile(XF), hot_wide, ALU.mult))
                link(nc.vector.tensor_reduce(xs[:], wide[:].rearrange("p b (t j) -> p b j t", j=W), AX.X, ALU.add))
                link(nc.vector.tensor_reduce(lo_hi[:, 0, :], xs[:], AX.X, ALU.min))
                link(nc.vector.tensor_reduce(lo_hi[:, 1, :], xs[:], AX.X, ALU.max))
                link(TS(off[:], hot[:], -BIG, BIG, ALU.mult, ALU.add))
                for i, sgn in ((0, ALU.add), (1, ALU.subtract)):
                    link(TT(extreme[:, i], hot[:], over(lo_hi[:, i, :], NT), ALU.mult))
                    link(TT(extreme[:, i], extreme[:, i], off[:], sgn))
                    link(nc.vector.tensor_reduce(tile_ext[:, i, :], extreme[:, i].rearrange("p b t -> p t b"), AX.X, (ALU.min, ALU.max)[i]))
                nc.vector.tensor_copy(tile_ext[:, 0, 0:1], tile_ext[:, 0, 0:1]).then_inc(ext_ready, 1)
                dve.wait_ge(ext_transposed, 1)
                for i in range(2):
                    nc.vector.tensor_reduce(table[:, 129 + i:130 + i], bank[0][0:NT, i * 128:(i + 1) * 128], AX.X, (ALU.min, ALU.max)[i]).then_inc(table_ready, 1)

                def step(s, j):
                    if live(s):
                        wait(dve, hot_transposed, s - 1)
                        TS(hot_b[:, j, 0:NT], batch(hot, s), 1.0, None, ALU.mult).then_inc(hot_copied, 1)
                    if live(s - 1):
                        dve.wait_ge(looked_up, s)
                        TS(batch(found, s - 1), bank[5 - j][:, 0:TABW], 1.0, None, ALU.mult).then_inc(found_ready, 1)
                run_pairs(dve, step, 1)
                dve.wait_ge(found_ready, B)

                link(TT(span[:, 0, :], found[:, :, 130], found[:, :, 129], ALU.subtract))
                link(TS(span[:, 0, :], span[:, 0, :], 1e-8, None, ALU.add))
                link(nc.vector.reciprocal(span[:, 1, :], span[:, 0, :]))
                link(TT(u[:], xs[:], over(found[:, :, 129], W), ALU.subtract))
                link(TT(u[:], u[:], over(span[:, 1, :], W), ALU.mult))
                link(TS(u[:], u[:], 0.0, float(np.float32(1.0 - 1e-6)), ALU.max, ALU.min))
                link(TS(u[:], u[:], float(GRID), None, ALU.mult))
                u_flat = u[:].rearrange("p b w -> p (b w)")
                link(TT(ge[:], u_flat.rearrange("p (n a) -> p n a", a=1).broadcast_to([128, B * W, GRID + 1]),
                        rank[:, NT + NC_:].rearrange("p (a g) -> p a g", a=1).broadcast_to([128, B * W, GRID + 1]), ALU.is_ge))
                cells = lambda ap: ap.rearrange("p b w g -> p (b w) g")
                link(TT(cells(cell[:]), ge[:, :, 0:GRID], ge[:, :, 1:GRID + 1], ALU.subtract))
                for i in range(2):
                    link(TT(picked[:, i], cell[:], found[:, :, 64 * i:64 * (i + 1)].rearrange("p b (w g) -> p b w g", w=W), ALU.mult))
                    link(nc.vector.tensor_reduce(coef[:, i], picked[:, i], AX.X, ALU.add))
                link(nc.vector.tensor_reduce(coef[:, 2].rearrange("p b w -> p (b w)"), ge[:, :, 1:GRID + 1], AX.X, ALU.add))
                link(TT(coef[:, 2], u[:], coef[:, 2], ALU.subtract))
                link(TT(coef[:, 2], coef[:, 2], coef[:, 1], ALU.mult))
                link(TT(coef[:, 2], coef[:, 2], coef[:, 0], ALU.add))
                link(TT(coef[:, 3], coef[:, 2], over(found[:, :, 128], W), ALU.mult))
                for j in range(W):
                    link(TT(wide[:].rearrange("p b (t j) -> p b t j", j=W)[:, :, :, j], hot[:], over(coef[:, 3, :, j], NT), ALU.mult))
                link(TT(X[:], X[:], wide[:], ALU.add))

            @block.tensor
            def _(pe):
                pe.wait_ge(ext_ready, 1)
                for i in range(2):
                    ins = nc.tensor.transpose(bank[0][0:NT, i * 128:(i + 1) * 128], tile_ext[:, i, :], ident[:])
                ins.then_inc(ext_transposed, 1)
                pe.wait_ge(table_ready, 2)

                def step(s, j):
                    if live(s):
                        pe.wait_ge(hot_copied, s + 1)
                        wait(pe, hotT_ready, s - 1)
                        nc.tensor.transpose(bank[2 + j][:, 0:128], hot_b[:, j, :], ident[:]).then_inc(hot_transposed, 1)
                    if live(s - 1):
                        pe.wait_ge(hotT_ready, s)
                        wait(pe, found_ready, s - 2)
                        nc.tensor.matmul(bank[5 - j][:, 0:TABW], hotT[:, 1 - j, :], table[:], start=True, stop=True).then_inc(looked_up, 1)
                run_pairs(pe, step, 1)

            @block.scalar
            def _(act):
                def step(s, j):
                    if live(s):
                        act.wait_ge(hot_transposed, s + 1)
                        wait(act, looked_up, s - 1)
                        nc.scalar.activation(hotT[:, j, :], bank[2 + j][0:NT, 0:128], ACT.Copy).then_inc(hotT_ready, 1)
                run_pairs(act, step, 0)

def phase_window(nc, a, sem, sb_, bank, X, ident, mean, var_eps, rstd, minus_half, stats, ln_tmp):
    local = ExitStack()
    with local:
        def sb(name, shape, dt=F32):
            return sb_(name, shape, dt, local)

        NH, DH, VW = 16, 16, 17
        wqk = sb("win_wqk", [128, KD, 2 * D])
        w_in = sb("win_w_in", [128, 2, KD, D])
        w_hi = sb("win_w_hi", [128, 2, KD, D], F32R)
        w_lo = sb("win_w_lo", [128, 2, KD, D], F32R)
        band_f = sb("win_band_f", [128, 128])
        band = sb("win_band", [128, 4, 128], BF16)
        ident_b = sb("win_ident_b", [128, 128], BF16)
        parity = sb("win_parity", [128, 2])
        xn = sb("win_xn", [128, 2, D])
        xT_full = sb("win_xT_full", [128, KD, 128])
        xT_hi = sb("win_xT_hi", [128, KD, 128], F32R)
        xT_lo = sb("win_xT_lo", [128, KD, 128], F32R)
        qT = sb("win_qT", [128, 2, KD, 128])
        k_of = sb("win_k_of", [128, 2, KD, 2, 128])
        V = sb("win_V", [128, 2, NH, VW])
        P = sb("win_P", [128, 2, 4, 128])
        PT = sb("win_PT", [128, 2, 4, 128])
        neg_max = sb("win_neg_max", [128, 4, 4])
        inv = sb("win_inv", [128, 2, NH])
        o = sb("win_o", [128, 2, D])
        oT_hi = sb("win_oT_hi", [128, KD, 128], F32R)
        oT_lo = sb("win_oT_lo", [128, KD, 128], F32R)
        oT_full = sb("win_oT_full", [128, KD, 128])

        consts = sem("win_consts")
        made = sem("win_made")
        w_rounded = sem("win_w_rounded")
        ln = sem("win_ln")
        rstd_ready = sem("win_rstd_ready")
        xn_ready = sem("win_xn_ready")
        x_transposed = sem("win_x_transposed")
        xT_full_ready = sem("win_xT_full_ready")
        xT_hi_ready = sem("win_xT_hi_ready")
        xT_lo_ready = sem("win_xT_lo_ready")
        qk_projected = sem("win_qk_projected")
        v_projected = sem("win_v_projected")
        qk_ready = sem("win_qk_ready")
        V_ready = sem("win_V_ready")
        scored = sem("win_scored")
        max_found = sem("win_max_found")
        exps_done = sem("win_exps_done")
        p_transposed = sem("win_p_transposed")
        PT_ready = sem("win_PT_ready")
        weighed = sem("win_weighed")
        inv_ready = sem("win_inv_ready")
        o_ready = sem("win_o_ready")
        o_transposed = sem("win_o_transposed")
        oT_full_ready = sem("win_oT_full_ready")
        oT_hi_ready = sem("win_oT_hi_ready")
        oT_lo_ready = sem("win_oT_lo_ready")
        out_projected = sem("win_out_projected")
        added = sem("win_added")

        QK, SC, PTB, OB, VB, MISC = bank[0], (bank[1], bank[2]), (bank[3], bank[4]), bank[5], bank[6], bank[7]
        STEPS = B * 4

        with nc.Block() as block:
            @block.sync
            def _(sp):
                wT = a["w_qkvT"].rearrange("(k p) n -> p k n", p=128)
                for dst, src in ((wqk[:], wT[:, :, 0:2 * D]), (w_in[:, 0], wT[:, :, 2 * D:3 * D]),
                                 (w_in[:, 1], a["w_outT"].rearrange("(k p) n -> p k n", p=128)),
                                 (band_f[:], a["band"]), (parity[:], a["parity"])):
                    sp.dma_start(dst, src).then_inc(consts, 16)

            @block.gpsimd
            def _(pool):
                pool.wait_ge(ln, B + 7)
                nc.gpsimd.tensor_tensor(rstd[:], var_eps[:], minus_half[:], ALU.pow).then_inc(rstd_ready, 1)

            def run(eng, step, extra, first=None):
                for q in range(4):
                    step(q, q, 0, 0)
                for q in range(4):
                    step(4 + q, q, 1, 1)
                with eng.Fori(1, B // 2 - 1) as i:
                    for j in range(2):
                        for q in range(4):
                            step(i * 8 + 4 * j + q, q, i * 2 + j, j)
                for b in (B - 2, B - 1):
                    for q in range(4):
                        step(4 * b + q, q, b, b % 2)
                for q in range(extra):
                    step(STEPS + q, q, B, 0)

            @block.scalar
            def _(act):
                act.wait_ge(consts, 80)
                nc.scalar.activation(w_hi[:], w_in[:], ACT.Copy).then_inc(w_rounded, 1)

                def take_xT(b):
                    act.wait_ge(x_transposed, b + 1)
                    wait(act, v_projected, b)
                    nc.scalar.activation(flat(xT_full[:]), MISC[:, 0:D], ACT.Copy).then_inc(xT_full_ready, 1)
                    nc.scalar.activation(flat(xT_hi[:]), MISC[:, 0:D], ACT.Copy).then_inc(xT_hi_ready, 1)

                def take_qk(b, j):
                    act.wait_ge(qk_projected, b + 1)
                    wait(act, scored, 4 * b - 4)
                    nc.scalar.activation(flat(qT[:, j]), QK[:, 0:D], ACT.Copy, scale=1.0 / DH ** 0.5).then_inc(qk_ready, 1)
                    for par in range(2):
                        nc.scalar.activation(k_of[:, j, :, par, :], QK[:, D:2 * D].rearrange("p (k n) -> p k n", k=KD), ACT.Copy,
                                             scale=parity[:, par:par + 1]).then_inc(qk_ready, 1)

                def take_v(b, j):
                    act.wait_ge(v_projected, b + 1)
                    wait(act, weighed, 4 * b - 4)
                    nc.scalar.activation(V[:, j, :, 0:DH], VB[:, 0:D].rearrange("p (h n) -> p h n", h=NH), ACT.Copy).then_inc(V_ready, 1)

                def exps(t, q):
                    act.wait_ge(max_found, t + 1)
                    wait(act, p_transposed, t - 1)
                    for h in range(4):
                        ins = nc.scalar.activation(P[:, q % 2, h, :], SC[q % 2][:, h * 128:(h + 1) * 128], ACT.Exp, bias=neg_max[:, q, h:h + 1])
                    ins.then_inc(exps_done, 1)

                def take_oT(b):
                    act.wait_ge(o_transposed, b + 1)
                    wait(act, out_projected, b)
                    nc.scalar.activation(flat(oT_full[:]), MISC[:, D:2 * D], ACT.Copy).then_inc(oT_full_ready, 1)
                    nc.scalar.activation(flat(oT_hi[:]), MISC[:, D:2 * D], ACT.Copy).then_inc(oT_hi_ready, 1)

                take_xT(0)
                take_qk(0, 0)
                take_v(0, 0)

                def step(t, q, b, j):
                    if live(t, STEPS):
                        exps(t, q)
                    if q == 1 and live(b + 1):
                        take_xT(b + 1)
                    if q == 2:
                        if live(b + 1):
                            take_qk(b + 1, 1 - j)
                        if live(b - 1):
                            take_oT(b - 1)
                    if q == 3 and live(b + 1):
                        take_v(b + 1, 1 - j)
                run(act, step, 3)

            @block.vector
            def _(dve):
                with dve.Fori(0, B) as b:
                    nc.vector.bn_stats(batch(stats, b), batch(X, b)).then_inc(ln, 1)
                dve.wait_ge(ln, B)
                n = finish_stats(nc, dve, ln, B, stats, mean[:], var_eps[:], ln_tmp, LN_EPS)
                dve.wait_ge(consts, 80)
                for h in range(4):
                    nc.vector.tensor_copy(band[:, h, :], band_f[:]).then_inc(made, 1)
                nc.vector.tensor_copy(ident_b[:], ident[:]).then_inc(made, 1)
                nc.vector.memset(V[:], 1.0).then_inc(made, 1)
                dve.wait_ge(w_rounded, 1)
                nc.vector.tensor_tensor(w_lo[:], w_in[:], w_hi[:].bitcast(F32), ALU.subtract).then_inc(made, 1)
                dve.wait_ge(ln, n)
                dve.wait_ge(rstd_ready, 1)

                def normalise(b, j):
                    wait(dve, x_transposed, b - 1)
                    nc.vector.tensor_scalar(xn[:, j, :], batch(X, b), one(mean, b), one(rstd, b), ALU.subtract, ALU.mult).then_inc(xn_ready, 1)

                def split_xT(b):
                    dve.wait_ge(xT_hi_ready, b + 1)
                    nc.vector.tensor_tensor(flat(xT_lo[:]), flat(xT_full[:]), flat(xT_hi[:]).bitcast(F32), ALU.subtract).then_inc(xT_lo_ready, 1)

                def find_max(t, q):
                    dve.wait_ge(scored, t + 1)
                    nc.vector.tensor_reduce(neg_max[:, q, :], SC[q % 2][:].rearrange("p (h n) -> p h n", h=4), AX.X, ALU.max, negate=True).then_inc(max_found, 1)

                def take_PT(t, q):
                    dve.wait_ge(p_transposed, t + 1)
                    wait(dve, weighed, t - 1)
                    nc.vector.tensor_copy(flat(PT[:, q % 2]), PTB[q % 2][:]).then_inc(PT_ready, 1)

                def norm_out(b, j):
                    dve.wait_ge(weighed, 4 * b + 4)
                    heads = OB[:, 0:NH * VW].rearrange("p (h n) -> p h n", h=NH)
                    nc.vector.reciprocal(inv[:, j, :], heads[:, :, DH]).then_inc(inv_ready, 1)
                    dve.wait_ge(inv_ready, b + 1)
                    wait(dve, o_transposed, b - 1)
                    nc.vector.tensor_tensor(o[:, j, :].rearrange("p (h n) -> p h n", h=NH), heads[:, :, 0:DH],
                                            inv[:, j, :].rearrange("p (h n) -> p h n", n=1).broadcast_to([128, NH, DH]), ALU.mult).then_inc(o_ready, 1)

                def split_oT(b):
                    dve.wait_ge(oT_hi_ready, b + 1)
                    nc.vector.tensor_tensor(flat(oT_lo[:]), flat(oT_full[:]), flat(oT_hi[:]).bitcast(F32), ALU.subtract).then_inc(oT_lo_ready, 1)

                def add_out(b):
                    dve.wait_ge(out_projected, b + 1)
                    nc.vector.tensor_tensor(batch(X, b), MISC[:, 0:D], batch(X, b), ALU.add).then_inc(added, 1)

                normalise(0, 0)
                split_xT(0)
                normalise(1, 1)

                def step(t, q, b, j):
                    if live(t, STEPS):
                        find_max(t, q)
                    if q == 1 and live(b - 1):
                        norm_out(b - 1, 1 - j)
                    if q == 2:
                        if live(b + 1):
                            split_xT(b + 1)
                        if live(b + 2):
                            normalise(b + 2, j)
                        if live(b - 1):
                            split_oT(b - 1)
                    if live(t - 1, STEPS):
                        take_PT(t - 1, (q + 3) % 4)
                    if q == 3 and live(b - 1):
                        add_out(b - 1)
                run(dve, step, 4)

            @block.tensor
            def _(pe):
                def transpose_x(b, j):
                    pe.wait_ge(xn_ready, b + 1)
                    wait(pe, xT_hi_ready, b)
                    wait(pe, added, b - 2)
                    for k in range(KD):
                        ins = nc.tensor.transpose(MISC[:, k * 128:(k + 1) * 128], xn[:, j, k * 128:(k + 1) * 128], ident[:])
                    ins.then_inc(x_transposed, 1)

                def project_qk(b):
                    pe.wait_ge(xT_full_ready, b + 1)
                    wait(pe, qk_ready, 3 * b)
                    for c in range(4):
                        for k in range(KD):
                            ins = nc.tensor.matmul(QK[:, c * 128:(c + 1) * 128], wqk[:, k, c * 128:(c + 1) * 128], xT_full[:, k, :],
                                                   start=(k == 0), stop=(k == KD - 1))
                    ins.then_inc(qk_projected, 1)

                def project_v(b):
                    pe.wait_ge(xT_lo_ready, b + 1)
                    wait(pe, V_ready, b)
                    for k in range(KD):
                        ins = matmul3(nc, VB[:, 0:D], (xT_hi[:, k, :], xT_lo[:, k, :]), (w_hi[:, 0, k, :], w_lo[:, 0, k, :]),
                                      first=(k == 0), last=(k == KD - 1))
                    ins.then_inc(v_projected, 1)

                def score(t, q, b, j):
                    if q == 0:
                        pe.wait_ge(qk_ready, 3 * b + 3)
                    wait(pe, exps_done, t - 1)
                    dst = SC[q % 2]
                    nc.tensor.matmul(dst[:], ident_b[:], flat(band[:]), start=True, stop=True)
                    for pair in range(2):
                        rows = slice(32 * q, 32 * q + 32)
                        ins = nc.tensor.matmul(dst[:, pair * 256:(pair + 1) * 256], qT[rows, j, pair, :], k_of[rows, j, pair, :, :].rearrange("p a n -> p (a n)"),
                                               start=False, stop=True, skip_group_check=True)
                    ins.then_inc(scored, 1)

                def transpose_p(t, q):
                    pe.wait_ge(exps_done, t + 1)
                    wait(pe, PT_ready, t - 1)
                    for h in range(4):
                        ins = nc.tensor.transpose(PTB[q % 2][:, h * 128:(h + 1) * 128], P[:, q % 2, h, :], ident[:])
                    ins.then_inc(p_transposed, 1)

                def weigh(t, q, b, j):
                    pe.wait_ge(PT_ready, t + 1)
                    if q == 0:
                        pe.wait_ge(V_ready, b + 1)
                        wait(pe, o_ready, b)
                    for h in range(4):
                        head = 8 * (h // 2) + 2 * q + h % 2
                        ins = nc.tensor.matmul(OB[:, head * VW:(head + 1) * VW], PT[:, q % 2, h, :], V[:, j, head, :], start=True, stop=True)
                    ins.then_inc(weighed, 1)

                def transpose_o(b, j):
                    pe.wait_ge(o_ready, b + 1)
                    wait(pe, oT_hi_ready, b)
                    wait(pe, added, b)
                    wait(pe, xT_hi_ready, min(b + 3, B) if isinstance(b, int) else b + 3)
                    for k in range(KD):
                        ins = nc.tensor.transpose(MISC[:, D + k * 128:D + (k + 1) * 128], o[:, j, k * 128:(k + 1) * 128], ident[:])
                    ins.then_inc(o_transposed, 1)

                def project_out(b):
                    pe.wait_ge(oT_lo_ready, b + 1)
                    for k in range(KD):
                        ins = matmul3(nc, MISC[:, 0:D], (oT_hi[:, k, :], oT_lo[:, k, :]), (w_hi[:, 1, k, :], w_lo[:, 1, k, :]),
                                      first=(k == 0), last=(k == KD - 1))
                    ins.then_inc(out_projected, 1)

                pe.wait_ge(consts, 80)
                transpose_x(0, 0)
                project_qk(0)
                pe.wait_ge(made, 7)
                project_v(0)

                def step(t, q, b, j):
                    if live(t, STEPS):
                        score(t, q, b, j)
                    if q == 0 and live(b + 1):
                        transpose_x(b + 1, 1 - j)
                    if live(t - 1, STEPS):
                        transpose_p(t - 1, (q + 3) % 4)
                    if q == 1:
                        if live(b + 1):
                            project_qk(b + 1)
                    if q == 2:
                        if live(b - 1):
                            transpose_o(b - 1, 1 - j)
                        if live(b + 1):
                            project_v(b + 1)
                    if q == 3 and live(b - 1):
                        project_out(b - 1)
                    if live(t - 2, STEPS):
                        weigh(t - 2, (q + 2) % 4, b if q >= 2 else b - 1, j if q >= 2 else 1 - j)
                run(pe, step, 4)

def phase_cross(nc, a, sem, sb_, bank, X, ident, mean, var_eps, rstd, minus_half, stats, ln_tmp):
    local = ExitStack()
    with local:
        def sb(name, shape, dt=F32):
            return sb_(name, shape, dt, local)

        wqk = sb("cr_wqk", [128, 2, KD, D])
        w_in = sb("cr_w_in", [128, 2, KD, D])
        w_hi = sb("cr_w_hi", [128, 2, KD, D], F32R)
        w_lo = sb("cr_w_lo", [128, 2, KD, D], F32R)
        xn = sb("cr_xn", [128, 2, D])
        xT_full = sb("cr_xT_full", [128, 2, KD, 128])
        xT_hi = sb("cr_xT_hi", [128, 2, KD, 128], F32R)
        xT_lo = sb("cr_xT_lo", [128, 2, KD, 128], F32R)
        qT = sb("cr_qT", [128, KD, 128])
        kT = sb("cr_kT", [128, 2, KD, 2, 128])
        V = sb("cr_V", [128, 2, 2, D])
        P = sb("cr_P", [128, 2, 128])
        PT = sb("cr_PT", [128, 2, 128])
        oT_full = sb("cr_oT_full", [128, KD, 128])
        oT_hi = sb("cr_oT_hi", [128, KD, 128], F32R)
        oT_lo = sb("cr_oT_lo", [128, KD, 128], F32R)
        neg_max = sb("cr_neg_max", [128, 2])
        exp_sum = sb("cr_exp_sum", [128, 2])
        inv_sum = sb("cr_inv_sum", [128, 2])

        consts = sem("cr_consts")
        ctx_loaded = [sem("cr_ctx0"), sem("cr_ctx1")]
        w_rounded = sem("cr_w_rounded")
        w_split = sem("cr_w_split")
        ln = sem("cr_ln")
        rstd_ready = sem("cr_rstd_ready")
        xn_ready = sem("cr_xn_ready")
        x_transposed = sem("cr_x_transposed")
        xT_full_ready = sem("cr_xT_full_ready")
        xT_hi_ready = sem("cr_xT_hi_ready")
        xT_lo_ready = sem("cr_xT_lo_ready")
        qk_projected = sem("cr_qk_projected")
        qk_ready = sem("cr_qk_ready")
        v_projected = sem("cr_v_projected")
        V_ready = sem("cr_V_ready")
        scored = sem("cr_scored")
        max_found = sem("cr_max_found")
        exps_done = sem("cr_exps_done")
        inv_ready = sem("cr_inv_ready")
        probs_ready = sem("cr_probs_ready")
        p_transposed = sem("cr_p_transposed")
        PT_ready = sem("cr_PT_ready")
        weighed = sem("cr_weighed")
        oT_full_ready = sem("cr_oT_full_ready")
        oT_hi_ready = sem("cr_oT_hi_ready")
        oT_lo_ready = sem("cr_oT_lo_ready")
        out_projected = sem("cr_out_projected")
        added = sem("cr_added")
        XB, QKB, VB, PB, OB, SB_, OUT, _ = bank

        with nc.Block() as block:
            @block.sync
            def _(sp):
                for dst, name in ((wqk[:, 0], "x_wqT"), (wqk[:, 1], "x_wkT"), (w_in[:, 0], "x_wvT"), (w_in[:, 1], "x_woT")):
                    sp.dma_start(dst, a[name].rearrange("(k p) n -> p k n", p=128)).then_inc(consts, 16)

                def step(s, j):
                    if live(s):
                        wait(sp, weighed, s - 1)
                        sp.dma_start(kT[:, j, :, 0, :], ctx_columns(a, s)).then_inc(ctx_loaded[j], 16)
                        rows = a["ctx_2048"][s] if isinstance(s, int) else a["ctx_2048"][bass.ds(s, 1)].rearrange("a t d -> (a t) d")
                        sp.dma_start(V[:, j, 0, :], rows).then_inc(ctx_loaded[j], 16)
                run_pairs(sp, step, 0)

            @block.gpsimd
            def _(pool):
                pool.wait_ge(ln, B + 7)
                nc.gpsimd.tensor_tensor(rstd[:], var_eps[:], minus_half[:], ALU.pow).then_inc(rstd_ready, 1)

            @block.scalar
            def _(act):
                act.wait_ge(consts, 64)
                nc.scalar.activation(w_hi[:], w_in[:], ACT.Copy).then_inc(w_rounded, 1)

                def step(s, j):
                    u = s - 2
                    if live(u):
                        act.wait_ge(max_found, u + 1)
                        wait(act, p_transposed, u)
                        nc.scalar.activation(flat(P[:]), SB_[:, 0:2 * 128], ACT.Exp, bias=neg_max[:, j:j + 1], accum_out=exp_sum[:, j:j + 1]).then_inc(exps_done, 1)
                    if live(s):
                        act.wait_ge(x_transposed, s + 1)
                        wait(act, v_projected, s - 1)
                        nc.scalar.activation(flat(xT_full[:, j]), XB[:, 0:D], ACT.Copy).then_inc(xT_full_ready, 1)
                        nc.scalar.activation(flat(xT_hi[:, j]), XB[:, 0:D], ACT.Copy).then_inc(xT_hi_ready, 1)
                    u, i = s - 1, 1 - j
                    if live(u):
                        act.wait_ge(qk_projected, u + 1)
                        wait(act, scored, u)
                        nc.scalar.activation(flat(qT[:]), QKB[:, 0:D], ACT.Copy, scale=1.0 / D ** 0.5).then_inc(qk_ready, 1)
                        nc.scalar.activation(kT[:, i, :, 1, :], QKB[:, D:2 * D].rearrange("p (k n) -> p k n", k=KD), ACT.Copy).then_inc(qk_ready, 1)
                    u = s - 2
                    if live(u):
                        act.wait_ge(p_transposed, u + 1)
                        wait(act, weighed, u)
                        nc.scalar.activation(flat(PT[:]), PB[:, 0:2 * 128], ACT.Copy).then_inc(PT_ready, 1)
                    u, i = s - 1, 1 - j
                    if live(u):
                        act.wait_ge(v_projected, u + 1)
                        wait(act, weighed, u - 1)
                        nc.scalar.activation(V[:, i, 1, :], VB[:, 0:D], ACT.Copy).then_inc(V_ready, 1)
                    u = s - 2
                    if live(u):
                        act.wait_ge(weighed, u + 1)
                        wait(act, out_projected, u)
                        nc.scalar.activation(flat(oT_full[:]), OB[:, 0:D], ACT.Copy).then_inc(oT_full_ready, 1)
                        nc.scalar.activation(flat(oT_hi[:]), OB[:, 0:D], ACT.Copy).then_inc(oT_hi_ready, 1)
                run_pairs(act, step, 2)

            @block.vector
            def _(dve):
                with dve.Fori(0, B) as b:
                    nc.vector.bn_stats(batch(stats, b), batch(X, b)).then_inc(ln, 1)
                dve.wait_ge(ln, B)
                n = finish_stats(nc, dve, ln, B, stats, mean[:], var_eps[:], ln_tmp, LN_EPS)
                dve.wait_ge(w_rounded, 1)
                nc.vector.tensor_tensor(w_lo[:], w_in[:], w_hi[:].bitcast(F32), ALU.subtract).then_inc(w_split, 1)
                dve.wait_ge(ln, n)
                dve.wait_ge(rstd_ready, 1)

                def normalise(b, j):
                    wait(dve, x_transposed, b - 1)
                    nc.vector.tensor_scalar(xn[:, j, :], batch(X, b), one(mean, b), one(rstd, b), ALU.subtract, ALU.mult).then_inc(xn_ready, 1)

                normalise(0, 0)

                def step(s, j):
                    u = s - 2
                    if live(u):
                        dve.wait_ge(scored, u + 1)
                        nc.vector.tensor_reduce(neg_max[:, j:j + 1], SB_[:, 0:2 * 128], AX.X, ALU.max, negate=True).then_inc(max_found, 1)
                        dve.wait_ge(exps_done, u + 1)
                        nc.vector.reciprocal(inv_sum[:, j:j + 1], exp_sum[:, j:j + 1]).then_inc(inv_ready, 1)
                        dve.wait_ge(inv_ready, u + 1)
                        nc.vector.tensor_scalar(flat(P[:]), flat(P[:]), inv_sum[:, j:j + 1], None, ALU.mult).then_inc(probs_ready, 1)
                    if live(s):
                        dve.wait_ge(xT_hi_ready, s + 1)
                        nc.vector.tensor_tensor(flat(xT_lo[:, j]), flat(xT_full[:, j]), flat(xT_hi[:, j]).bitcast(F32), ALU.subtract).then_inc(xT_lo_ready, 1)
                    u = s - 3
                    if live(u):
                        dve.wait_ge(out_projected, u + 1)
                        nc.vector.tensor_tensor(batch(X, u), OUT[:, 0:D], batch(X, u), ALU.add).then_inc(added, 1)
                    u = s - 2
                    if live(u):
                        dve.wait_ge(oT_hi_ready, u + 1)
                        nc.vector.tensor_tensor(flat(oT_lo[:]), flat(oT_full[:]), flat(oT_hi[:]).bitcast(F32), ALU.subtract).then_inc(oT_lo_ready, 1)
                    if live(s + 1):
                        normalise(s + 1, 1 - j)
                run_pairs(dve, step, 3, peeled=2)

            @block.tensor
            def _(pe):
                pe.wait_ge(consts, 64)

                def step(s, j):
                    if live(s):
                        pe.wait_ge(xn_ready, s + 1)
                        wait(pe, xT_hi_ready, s)
                        for k in range(KD):
                            ins = nc.tensor.transpose(XB[:, k * 128:(k + 1) * 128], xn[:, j, k * 128:(k + 1) * 128], ident[:])
                        ins.then_inc(x_transposed, 1)
                    u, i = s - 1, 1 - j
                    if live(u):
                        pe.wait_ge(xT_full_ready, u + 1)
                        wait(pe, qk_ready, 2 * u)
                        for w in range(2):
                            for c in range(KD):
                                for k in range(KD):
                                    ins = nc.tensor.matmul(QKB[:, (2 * w + c) * 128:(2 * w + c + 1) * 128], wqk[:, w, k, c * 128:(c + 1) * 128], xT_full[:, i, k, :],
                                                           start=(k == 0), stop=(k == KD - 1))
                        ins.then_inc(qk_projected, 1)
                    u = s - 3
                    if live(u):
                        pe.wait_ge(oT_lo_ready, u + 1)
                        wait(pe, added, u)
                        for k in range(KD):
                            ins = matmul3(nc, OUT[:, 0:D], (oT_hi[:, k, :], oT_lo[:, k, :]), (w_hi[:, 1, k, :], w_lo[:, 1, k, :]),
                                          first=(k == 0), last=(k == KD - 1))
                        ins.then_inc(out_projected, 1)
                    u = s - 2
                    if live(u):
                        pe.wait_ge(probs_ready, u + 1)
                        wait(pe, PT_ready, u)
                        for c in range(2):
                            ins = nc.tensor.transpose(PB[:, c * 128:(c + 1) * 128], P[:, c, :], ident[:])
                        ins.then_inc(p_transposed, 1)
                    u, i = s - 1, 1 - j
                    if live(u):
                        if isinstance(u, int) and u == 0:
                            pe.wait_ge(w_split, 1)
                        pe.wait_ge(xT_lo_ready, u + 1)
                        wait(pe, V_ready, u)
                        for k in range(KD):
                            ins = matmul3(nc, VB[:, 0:D], (xT_hi[:, i, k, :], xT_lo[:, i, k, :]), (w_hi[:, 0, k, :], w_lo[:, 0, k, :]),
                                          first=(k == 0), last=(k == KD - 1))
                        ins.then_inc(v_projected, 1)
                    u = s - 2
                    if live(u):
                        pe.wait_ge(PT_ready, u + 1)
                        pe.wait_ge(V_ready, u + 1)
                        wait(pe, oT_hi_ready, u)
                        for c in range(KD):
                            for k in range(2):
                                ins = nc.tensor.matmul(OB[:, c * 128:(c + 1) * 128], V[:, j, k, c * 128:(c + 1) * 128], PT[:, k, :],
                                                       start=(k == 0), stop=(k == 1))
                        ins.then_inc(weighed, 1)
                    u, i = s - 1, 1 - j
                    if live(u):
                        pe.wait_ge(qk_ready, 2 * u + 2)
                        pe.wait_ge(ctx_loaded[i], 32 * (u // 2 + 1) if isinstance(u, int) else pair_count(s, j, i) * 2)
                        wait(pe, exps_done, u)
                        for c in range(KD):
                            ins = nc.tensor.matmul(SB_[:, 0:2 * 128], qT[:, c, :], kT[:, i, c, :, :].rearrange("p a n -> p (a n)"),
                                                   start=(c == 0), stop=(c == KD - 1))
                        ins.then_inc(scored, 1)
                run_pairs(pe, step, 3, peeled=2)


def phase_moe(nc, a, sem, sb_, bank, X, ident, mean, var_eps, rstd, minus_half, stats, ln_tmp, out):
    local = ExitStack()
    with local:
        def sb(name, shape, dt=F32):
            return sb_(name, shape, dt, local)

        E_, LAT, HID, GROUP = 16, 64, 128, 4
        GW = GROUP * S
        NG = B // GROUP
        XT_hi = sb("moe_XT_hi", [128, KD, B * S], F32R)
        XT_lo = sb("moe_XT_lo", [128, KD, B * S], F32R)
        XL = sb("moe_XL", [128, B * S], F32R)
        logits = sb("moe_logits", [128, B, E_])
        gates = sb("moe_gates", [128, B, E_])
        ranked = sb("moe_ranked", [128, B, E_])
        cut = sb("moe_cut", [128, B, E_])
        top = sb("moe_top", [128, B, 8])
        gate_sum = sb("moe_gate_sum", [128, 2, B])
        route_bias = sb("moe_route_bias", [128, E_])
        wg = sb("moe_wg", [128, KD, E_])
        w_in = sb("moe_w_in", [128, 3, KD, 128])
        w_hi = sb("moe_w_hi", [128, 3, KD, 128], F32R)
        w_lo = sb("moe_w_lo", [128, 3, KD, 128], F32R)
        sw2_in = sb("moe_sw2_in", [128, D])
        sw2_hi = sb("moe_sw2_hi", [128, D], F32R)
        sw2_lo = sb("moe_sw2_lo", [128, D], F32R)
        wup = sb("moe_wup", [LAT, D])
        low_rows = sb("moe_low_rows", [128, 1])
        xn = sb("moe_xn", [128, 2, D])
        xT = sb("moe_xT", [128, 2, KD, 128])
        lat_hi = sb("moe_lat_hi", [128, GW], F32R)
        acc = sb("moe_acc", [128, B, LAT])
        relu = sb("moe_relu", [128, 2, GW])
        prod = sb("moe_prod", [128, 2, GW])
        hidden = sb("moe_hidden", [128, 2, GW])
        y_hi = sb("moe_y_hi", [128, GW], F32R)
        y_lo = sb("moe_y_lo", [128, GW], F32R)

        consts = sem("moe_consts")
        w_rounded = sem("moe_w_rounded")
        w_split = sem("moe_w_split")
        ln = sem("moe_ln")
        rstd_ready = sem("moe_rstd_ready")
        xn_ready = sem("moe_xn_ready")
        x_transposed = sem("moe_x_transposed")
        xT_ready = sem("moe_xT_ready")
        XT_split = sem("moe_XT_split")
        routed = sem("moe_routed")
        logits_ready = sem("moe_logits_ready")
        chain = sem("moe_chain")
        exp_ready = sem("moe_exp_ready")
        lat_projected = sem("moe_lat_projected")
        lat_rounded = sem("moe_lat_rounded")
        XL_ready = sem("moe_XL_ready")
        up_done = sem("moe_up_done")
        sh_relu = sem("moe_sh_relu")
        sh_prod = sem("moe_sh_prod")
        y_rounded = sem("moe_y_rounded")
        y_split = sem("moe_y_split")
        sh_out = sem("moe_sh_out")
        sh_added = sem("moe_sh_added")

        with nc.Block() as block:
            @block.sync
            def _(sp):
                cols = lambda name: a[name].rearrange("(k p) n -> p k n", p=128)
                for dst, src in ((wg[:], cols("WgT")), (w_in[:, 0, :, 0:LAT], cols("WdownT")), (w_in[:, 0, :, LAT:], cols("WdownT")),
                                 (w_in[:, 1], cols("sw1T")), (w_in[:, 2], cols("swgT")), (sw2_in[:], a["sw2T"]), (wup[:], a["WupT"]),
                                 (route_bias[:], a["L1_ffn_biases"].rearrange("(a n) -> a n", a=1).broadcast_to([128, E_])),
                                 (low_rows[:], a["low_rows"])):
                    sp.dma_start(dst, src).then_inc(consts, 16)

            @block.gpsimd
            def _(pool):
                pool.wait_ge(ln, B + 7)
                nc.gpsimd.tensor_tensor(rstd[:], var_eps[:], minus_half[:], ALU.pow).then_inc(rstd_ready, 1)
                nc.gpsimd.memset(acc[:], 0.0)

            @block.scalar
            def _(act):
                act.wait_ge(consts, 144)
                nc.scalar.activation(w_hi[:], w_in[:], ACT.Copy).then_inc(w_rounded, 1)
                nc.scalar.activation(sw2_hi[:], sw2_in[:], ACT.Copy).then_inc(w_rounded, 1)

                def step(s, j):
                    if live(s):
                        act.wait_ge(x_transposed, s + 1)
                        wait(act, routed, s - 1)
                        wait(act, XT_split, 2 * s - 2)
                        nc.scalar.activation(flat(xT[:, j]), bank[j][:, 0:D], ACT.Copy).then_inc(xT_ready, 1)
                run_pairs(act, step, 0)
                act.wait_ge(logits_ready, B)
                nc.scalar.activation(flat(gates[:]), flat(logits[:]), ACT.Exp, scale=-1.0).then_inc(exp_ready, 1)
                with act.Fori(0, NG) as g:
                    act.wait_ge(lat_projected, g + 1)
                    act.wait_ge(XL_ready, g)
                    nc.scalar.activation(lat_hi[:], bank[0][:], ACT.Copy).then_inc(lat_rounded, 1)
                    act.wait_ge(up_done, g + 1)
                    act.wait_ge(sh_prod, 2 * g)
                    nc.scalar.activation(relu[:, 0, :], bank[2][:], ACT.Relu).then_inc(sh_relu, 1)
                    act.wait_ge(sh_prod, 2 * g + 2)
                    act.wait_ge(sh_out, g)
                    nc.scalar.activation(y_hi[:], hidden[:, 0, :], ACT.Copy).then_inc(y_rounded, 1)

            @block.vector
            def _(dve):
                count = [0]

                def link(ins):
                    count[0] += 1
                    ins.then_inc(chain, 1)
                    dve.wait_ge(chain, count[0])

                TT, TS = nc.vector.tensor_tensor, nc.vector.tensor_scalar
                with dve.Fori(0, B) as b:
                    nc.vector.bn_stats(batch(stats, b), batch(X, b)).then_inc(ln, 1)
                dve.wait_ge(ln, B)
                n = finish_stats(nc, dve, ln, B, stats, mean[:], var_eps[:], ln_tmp, LN_EPS)
                dve.wait_ge(w_rounded, 2)
                TT(w_lo[:], w_in[:], w_hi[:].bitcast(F32), ALU.subtract).then_inc(w_split, 1)
                TT(sw2_lo[:], sw2_in[:], sw2_hi[:].bitcast(F32), ALU.subtract).then_inc(w_split, 1)
                dve.wait_ge(ln, n)
                dve.wait_ge(rstd_ready, 1)

                def normalise(b, j):
                    wait(dve, x_transposed, b - 1)
                    TS(xn[:, j, :], batch(X, b), one(mean, b), one(rstd, b), ALU.subtract, ALU.mult).then_inc(xn_ready, 1)

                normalise(0, 0)

                def step(s, j):
                    if live(s + 1):
                        normalise(s + 1, 1 - j)
                    if live(s):
                        dve.wait_ge(xT_ready, s + 1)
                        at = slice(s * S, (s + 1) * S) if isinstance(s, int) else bass.ds(s * S, S)
                        TS(XT_hi[:, :, at], xT[:, j], 1.0, None, ALU.mult).then_inc(XT_split, 1)
                        dve.wait_ge(XT_split, 2 * s + 1)
                        TT(XT_lo[:, :, at], xT[:, j], XT_hi[:, :, at].bitcast(F32), ALU.subtract).then_inc(XT_split, 1)
                    if live(s - 1):
                        dve.wait_ge(routed, s)
                        TS(batch(logits, s - 1), bank[3 - j][:, 0:E_], 1.0, None, ALU.mult).then_inc(logits_ready, 1)
                run_pairs(dve, step, 1)

                with dve.Fori(0, NG) as g:
                    dve.wait_ge(lat_rounded, g + 1)
                    nc.vector.scalar_tensor_tensor(XL[:, bass.ds(g * GW, GW)], lat_hi[:].bitcast(F32), low_rows[:, 0:1], bank[0][:],
                                                   ALU.mult, ALU.add).then_inc(XL_ready, 1)
                    dve.wait_ge(sh_relu, g + 1)
                    TT(prod[:, 0, :], bank[1][:], relu[:, 0, :], ALU.mult).then_inc(sh_prod, 1)
                    dve.wait_ge(sh_prod, 2 * g + 1)
                    dve.wait_ge(y_split, g)
                    TT(hidden[:, 0, :], prod[:, 0, :], relu[:, 0, :], ALU.mult).then_inc(sh_prod, 1)
                    dve.wait_ge(y_rounded, g + 1)
                    TT(y_lo[:], hidden[:, 0, :], y_hi[:].bitcast(F32), ALU.subtract).then_inc(y_split, 1)
                    dve.wait_ge(sh_out, g + 1)
                    for i in range(2):
                        rows = X[:, bass.ds(g * GROUP + 2 * i, 2), :].rearrange("p b n -> p (b n)")
                        TT(rows, bank[4 + i][:], rows, ALU.add).then_inc(sh_added, 1)

                dve.wait_ge(exp_ready, 1)
                link(TS(gates[:], gates[:], 1.0, None, ALU.add))
                link(nc.vector.reciprocal(gates[:], gates[:]))
                link(TT(ranked[:], gates[:], route_bias[:].rearrange("p (a n) -> p a n", a=1).broadcast_to([128, B, E_]), ALU.add))
                for b in range(B):
                    ins = nc.vector.max(top[:, b, :], ranked[:, b, :])
                link(ins)
                for b in range(B):
                    ins = nc.vector.match_replace(cut[:, b, :], top[:, b, :], ranked[:, b, :], -1e30)
                link(ins)
                link(TT(cut[:], cut[:], ranked[:], ALU.not_equal))
                link(TT(gates[:], gates[:], cut[:], ALU.mult))
                link(nc.vector.tensor_reduce(gate_sum[:, 0, :], gates[:], AX.X, ALU.add))
                link(nc.vector.reciprocal(gate_sum[:, 1, :], gate_sum[:, 0, :]))
                link(TS(gate_sum[:, 1, :], gate_sum[:, 1, :], 2.5, None, ALU.mult))
                link(TT(gates[:], gates[:], gate_sum[:, 1, :].rearrange("p (b n) -> p b n", n=1).broadcast_to([128, B, E_]), ALU.mult))

            @block.tensor
            def _(pe):
                pe.wait_ge(consts, 144)

                def step(s, j):
                    if live(s):
                        pe.wait_ge(xn_ready, s + 1)
                        wait(pe, xT_ready, s - 1)
                        for k in range(KD):
                            ins = nc.tensor.transpose(bank[j][:, k * 128:(k + 1) * 128], xn[:, j, k * 128:(k + 1) * 128], ident[:])
                        ins.then_inc(x_transposed, 1)
                    u, i = s - 1, 1 - j
                    if live(u):
                        pe.wait_ge(xT_ready, u + 1)
                        wait(pe, logits_ready, u - 1)
                        for k in range(KD):
                            ins = nc.tensor.matmul(bank[2 + i][:, 0:E_], xT[:, i, k, :], wg[:, k, :], start=(k == 0), stop=(k == KD - 1))
                        ins.then_inc(routed, 1)
                run_pairs(pe, step, 1)

                pe.wait_ge(w_split, 2)
                pe.wait_ge(XT_split, 2 * B)
                pe.wait_ge(logits_ready, B)
                with pe.Fori(0, NG) as g:
                    at = bass.ds(g * GW, GW)

                    def up(dst, w):
                        for k in range(KD):
                            ins = matmul3(nc, dst[:], (w_hi[:, w, k, :], w_lo[:, w, k, :]), (XT_hi[:, k, at], XT_lo[:, k, at]),
                                          first=(k == 0), last=(k == KD - 1))
                        return ins

                    pe.wait_ge(XL_ready, g)
                    up(bank[0], 0).then_inc(lat_projected, 1)
                    pe.wait_ge(sh_prod, 2 * g)
                    up(bank[2], 2)
                    up(bank[1], 1).then_inc(up_done, 1)
                    pe.wait_ge(y_split, g + 1)
                    pe.wait_ge(sh_added, 2 * g)
                    for i in range(GROUP):
                        tok = slice(i * S, (i + 1) * S)
                        ins = matmul3(nc, bank[4 + i // 2][:, (i % 2) * D:(i % 2 + 1) * D], (y_hi[:, tok], y_lo[:, tok]), (sw2_hi[:], sw2_lo[:]), True, True)
                    ins.then_inc(sh_out, 1)

        we_in = sb("moe_we_in", [128, 2, 2, HID])
        we_hi = sb("moe_we_hi", [128, 2, 2, HID], F32R)
        we_lo = sb("moe_we_lo", [128, 2, 2, HID], F32R)
        we2 = sb("moe_we2", [128, 2, LAT])
        gate_of = sb("moe_gate_of", [128, 2, B])
        we_loaded = [sem("moe_we0"), sem("moe_we1")]
        we_rounded = sem("moe_we_rounded")
        we_split = sem("moe_we_split")
        gate_copied = sem("moe_gate_copied")
        ups_done = sem("moe_ups_done")
        relu_done = sem("moe_relu_done")
        prod_done = sem("moe_prod_done")
        hidden_done = sem("moe_hidden_done")
        downs_done = sem("moe_downs_done")
        acc_added = sem("moe_acc_added")
        STEPS = E_ * NG

        def run(eng, step, extra):
            for e in range(2):
                for g in range(NG):
                    step(e * NG + g, g, e, e)
            with eng.Fori(1, E_ // 2 - 1) as i:
                for j in range(2):
                    for g in range(NG):
                        step(i * 8 + 4 * j + g, g, i * 2 + j, j)
            for e in range(E_ - 2, E_):
                for g in range(NG):
                    step(e * NG + g, g, e, e % 2)
            for g in range(extra):
                step(STEPS + g, g, E_, 0)

        with nc.Block() as block:
            @block.sync
            def _(sp):
                def load(e, j):
                    wait(sp, downs_done, 4 * (e - 1))
                    for w, name in enumerate(("rw1T", "rwgT")):
                        src = a[name][e] if isinstance(e, int) else a[name][bass.ds(e, 1)].rearrange("a l n -> (a l) n")
                        for half in range(2):
                            sp.dma_start(we_in[half * LAT:(half + 1) * LAT, j, w, :], src).then_inc(we_loaded[j], 16)
                    src = a["rw2T"][e] if isinstance(e, int) else a["rw2T"][bass.ds(e, 1)].rearrange("a l n -> (a l) n")
                    sp.dma_start(we2[:, j, :], src).then_inc(we_loaded[j], 16)
                for e in range(2):
                    load(e, e)
                with sp.Fori(1, E_ // 2) as i:
                    for j in range(2):
                        load(i * 2 + j, j)

            @block.scalar
            def _(act):
                def round_weights(e, j, n):
                    act.wait_ge(we_loaded[j], n)
                    wait(act, ups_done, 4 * (e - 1))
                    nc.scalar.activation(we_hi[:, j], we_in[:, j], ACT.Copy).then_inc(we_rounded, 1)

                round_weights(0, 0, 80)

                def step(t, g, e, j):
                    if live(t, STEPS):
                        act.wait_ge(ups_done, t + 1)
                        wait(act, hidden_done, t - 1)
                        nc.scalar.activation(relu[:, g % 2, :], bank[2 + g % 2][:], ACT.Relu).then_inc(relu_done, 1)
                    if g == 1 and live(e + 1, E_):
                        round_weights(e + 1, 1 - j, 80 * ((e + 1) // 2 + 1) if isinstance(e, int) else pair_count(e, j, 1 - j, 1) * 5)
                run(act, step, 0)

            @block.gpsimd
            def _(pool):
                def step(t, g, e, j):
                    pool.wait_ge(prod_done, t + 1)
                    wait(pool, downs_done, t - 1)
                    nc.gpsimd.tensor_tensor(hidden[:, g % 2, :], prod[:, g % 2, :], relu[:, g % 2, :], ALU.mult).then_inc(hidden_done, 1)
                run(pool, step, 0)

            @block.vector
            def _(dve):
                def split_weights(e, j):
                    dve.wait_ge(we_rounded, e + 1)
                    wait(dve, ups_done, 4 * (e - 1))
                    nc.vector.tensor_tensor(we_lo[:, j], we_in[:, j], we_hi[:, j].bitcast(F32), ALU.subtract).then_inc(we_split, 1)
                    src = gates[:, :, e:e + 1] if isinstance(e, int) else gates[:, :, bass.ds(e, 1)]
                    wait(dve, acc_added, 4 * (e - 1))
                    nc.vector.tensor_scalar(gate_of[:, j, :], src.rearrange("p b a -> p (b a)"), 1.0, None, ALU.mult).then_inc(gate_copied, 1)

                split_weights(0, 0)

                def step(t, g, e, j):
                    if live(t, STEPS):
                        dve.wait_ge(relu_done, t + 1)
                        wait(dve, hidden_done, t - 1)
                        nc.vector.tensor_tensor(prod[:, g % 2, :], bank[g % 2][:], relu[:, g % 2, :], ALU.mult).then_inc(prod_done, 1)
                    u, ug = t - 2, (g + 2) % 4
                    if live(u, STEPS):
                        uj = j if g >= 2 else 1 - j
                        dve.wait_ge(downs_done, u + 1)
                        if ug == 0:
                            dve.wait_ge(gate_copied, e + 1)
                        wait(dve, acc_added, u - 3)
                        for i in range(GROUP):
                            b = ug * GROUP + i
                            ins = nc.vector.scalar_tensor_tensor(acc[:, b, :], bank[4 + g % 2][:, i * LAT:(i + 1) * LAT], gate_of[:, uj, b:b + 1], acc[:, b, :],
                                                                 ALU.mult, ALU.add)
                        ins.then_inc(acc_added, 1)
                    if g == 2 and live(e + 1, E_):
                        split_weights(e + 1, 1 - j)
                run(dve, step, 2)

            @block.tensor
            def _(pe):
                def step(t, g, e, j):
                    if live(t, STEPS):
                        if g == 0:
                            pe.wait_ge(we_split, e + 1)
                        wait(pe, prod_done, t - 1)
                        wait(pe, relu_done, t - 1)
                        toks = XL[:, g * GW:(g + 1) * GW]
                        for w in (1, 0):
                            nc.tensor.matmul(bank[2 * w + g % 2][:], we_hi[:, j, w, :], toks, start=True, stop=False)
                            ins = nc.tensor.matmul(bank[2 * w + g % 2][:], we_lo[:, j, w, :], toks, start=False, stop=True)
                        ins.then_inc(ups_done, 1)
                    u, ug = t - 1, (g + 3) % 4
                    if live(u, STEPS):
                        uj = j if g >= 1 else 1 - j
                        pe.wait_ge(hidden_done, u + 1)
                        wait(pe, acc_added, u - 1)
                        for i in range(GROUP):
                            ins = nc.tensor.matmul(bank[4 + ug % 2][:, i * LAT:(i + 1) * LAT], hidden[:, ug % 2, i * S:(i + 1) * S], we2[:, uj, :], start=True, stop=True)
                        ins.then_inc(downs_done, 1)
                run(pe, step, 1)

        acc_b = sb("moe_acc_b", [128, 2, 128])
        accT = sb("moe_accT", [128, 2, 128])
        padded = sem("moe_padded")
        acc_copied = sem("moe_acc_copied")
        acc_transposed = sem("moe_acc_transposed")
        accT_ready = sem("moe_accT_ready")
        upped = sem("moe_upped")
        result_ready = sem("moe_result_ready")
        stored = sem("moe_stored")
        with nc.Block() as block:
            @block.vector
            def _(dve):
                nc.vector.memset(acc_b[:], 0.0).then_inc(padded, 1)
                dve.wait_ge(padded, 1)

                def step(s, j):
                    if live(s):
                        wait(dve, acc_transposed, s - 1)
                        nc.vector.tensor_scalar(acc_b[:, j, 0:LAT], batch(acc, s), 1.0, None, ALU.mult).then_inc(acc_copied, 1)
                    if live(s - 2):
                        dve.wait_ge(upped, s - 1)
                        nc.vector.tensor_tensor(batch(X, s - 2), bank[2 + j][:, 0:D], batch(X, s - 2), ALU.add).then_inc(result_ready, 1)
                run_pairs(dve, step, 2)

            @block.tensor
            def _(pe):
                def step(s, j):
                    if live(s):
                        pe.wait_ge(acc_copied, s + 1)
                        wait(pe, accT_ready, s - 1)
                        nc.tensor.transpose(bank[j][:, 0:128], acc_b[:, j, :], ident[:]).then_inc(acc_transposed, 1)
                    u, i = s - 1, 1 - j
                    if live(u):
                        pe.wait_ge(accT_ready, u + 1)
                        wait(pe, result_ready, u - 1)
                        nc.tensor.matmul(bank[2 + i][:, 0:D], accT[0:LAT, i, :], wup[:], start=True, stop=True).then_inc(upped, 1)
                run_pairs(pe, step, 1)

            @block.scalar
            def _(act):
                def step(s, j):
                    if live(s):
                        act.wait_ge(acc_transposed, s + 1)
                        wait(act, upped, s - 1)
                        nc.scalar.activation(accT[:, j, :], bank[j][:, 0:128], ACT.Copy).then_inc(accT_ready, 1)
                run_pairs(act, step, 0)

            @block.sync
            def _(sp):
                for g in range(NG):
                    done = slice(g * GROUP, (g + 1) * GROUP)
                    sp.wait_ge(result_ready, (g + 1) * GROUP)
                    sp.dma_start(out[done].rearrange("b p d -> p b d"), X[:, done, :]).then_inc(stored, 16)
                sp.wait_ge(stored, 16 * NG)


def phase_rest(nc, a, sem, sb, bank, X, ident, mean, var_eps, rstd, minus_half, stats, ln_tmp, out, clear_semaphores):
    t = (nc, a, sem, sb, bank, X, ident, mean, var_eps, rstd, minus_half, stats, ln_tmp)
    phase_retention(*t)
    phase_spline(*t)
    phase_window(*t)
    phase_cross(*t)
    clear_semaphores()
    phase_moe(*t, out)


INPUTS = ["x", "L0_attn_bq", "L0_attn_bk", "L0_attn_bo", "L0_xattn_Wh", "L0_xattn_wg_w", "L0_xattn_wo_w",
          "L0_xattn_gn_gamma", "L0_xattn_gn_beta", "L0_ffn_ln_gamma", "L0_ffn_ln_beta", "L0_ffn_spline_bases",
          "L0_ffn_spline_slopes", "L0_ffn_output_scale", "ctx_2048", "L1_ffn_biases"]


def kernel(**inputs):
    import concourse.bacc as bacc
    from concourse.bass_utils import run_bass_kernel_spmd

    f32 = np.float32
    arrays = {n: np.ascontiguousarray(inputs[n]) for n in INPUTS}
    for name, src in (("wqT", "L0_attn_wq"), ("wkT", "L0_attn_wk"), ("wvT", "L0_attn_wv"), ("woT", "L0_attn_wo")):
        arrays[name] = np.ascontiguousarray(np.asarray(inputs[src]).T)
    for name, src in (("ln_gT", "L0_attn_ln_g"), ("ln_bT", "L0_attn_ln_b"), ("bvT", "L0_attn_bv")):
        arrays[name] = np.ascontiguousarray(np.asarray(inputs[src]).reshape(-1, 128).T)
    arrays["ctxT"] = np.ascontiguousarray(np.asarray(inputs["ctx_2048"]).reshape(B * S, D).T)
    arrays["w_qkvT"] = np.ascontiguousarray(np.asarray(inputs["L1_attn_w_qkv"]).T)
    arrays["w_outT"] = np.ascontiguousarray(np.asarray(inputs["L1_attn_w_out"]).T)
    for name, src in (("x_wqT", "L1_xattn_wq"), ("x_wkT", "L1_xattn_wk"), ("x_wvT", "L1_xattn_wv"), ("x_woT", "L1_xattn_wo"),
                      ("WgT", "L1_ffn_Wg"), ("WdownT", "L1_ffn_Wdown"), ("sw1T", "L1_ffn_sw1"), ("swgT", "L1_ffn_swg"),
                      ("sw2T", "L1_ffn_sw2"), ("WupT", "L1_ffn_Wup")):
        arrays[name] = np.ascontiguousarray(np.asarray(inputs[src]).T)
    for name, src in (("rw1T", "L1_ffn_rw1"), ("rwgT", "L1_ffn_rwg"), ("rw2T", "L1_ffn_rw2")):
        arrays[name] = np.ascontiguousarray(np.asarray(inputs[src]).transpose(0, 2, 1))
    arrays["WhT"] = np.ascontiguousarray(np.asarray(inputs["L0_xattn_Wh"]).transpose(2, 0, 1))
    theta = (f32(1.0) / np.power(f32(10000.0), np.arange(0, DK0, 2, dtype=f32) / f32(DK0))).astype(f32)
    freqs = np.arange(S, dtype=f32)[:, None] * theta[None, :]
    cos, sin = np.cos(freqs).astype(f32), np.sin(freqs).astype(f32)
    arrays["cos"] = np.concatenate([cos, cos], axis=1)
    arrays["sin"] = np.concatenate([-sin, sin], axis=1)
    arrays["ident"] = np.eye(128, dtype=f32)
    row, col = np.arange(128)[:, None], np.arange(128)[None, :]
    arrays["causal"] = np.where(col <= row, f32(0), f32(MASKED)).astype(f32)
    gamma = (f32(1.0) - f32(2.0) ** (f32(-5.0) - np.arange(2, dtype=f32))).astype(f32)
    expo = np.arange(S, dtype=f32)[None, :] - np.arange(S, dtype=f32)[:, None]
    with np.errstate(over="ignore"):
        dec = np.where(expo[None] <= 0, gamma[:, None, None] ** expo[None], f32(0)).astype(f32)
    dec = dec / np.sqrt(dec.sum(axis=-1, dtype=f32))[:, None, :]
    arrays["decayT"] = np.ascontiguousarray((dec / np.sqrt(f32(128.0))).astype(f32).transpose(2, 0, 1))
    arrays["band"] = np.where((col <= row) & (col >= row - 64), f32(0), f32(MASKED)).astype(f32)
    head = np.arange(128) // 16
    arrays["parity"] = np.stack([head % 2 == 0, head % 2 == 1], axis=1).astype(f32)
    arrays["low_rows"] = np.where(np.arange(128)[:, None] < 64, f32(0), f32(-1)).astype(f32)
    ranks = np.concatenate([np.arange(63, -1, -1), np.arange(7, -1, -1), np.arange(17)]).astype(f32)
    arrays["rank"] = np.tile(ranks, (128, 1))
    nc = bacc.Bacc("TRN2", target_bir_lowering=False, num_devices=1)
    aps = {n: nc.dram_tensor(f"in_{n}", v.shape, mybir.dt.from_np(v.dtype), kind="ExternalInput").ap() for n, v in arrays.items()}
    out = nc.dram_tensor("out", (B, S, D), F32, kind="ExternalOutput").ap()
    decoder_kernel(nc, aps, out)
    result = run_bass_kernel_spmd(nc, [{f"in_{n}": v for n, v in arrays.items()}], core_ids=[0])
    return result.results[0]["out"]
```

```python
import numpy as np
import concourse.bass as bass
from concourse import mybir
from concourse.alu_op_type import AluOpType as ALU
from contextlib import ExitStack

F32 = mybir.dt.float32
F32R = mybir.dt.float32r
BF16 = mybir.dt.bfloat16
ACT = mybir.ActivationFunctionType
AX = mybir.AxisListType

B, S, D = 16, 128, 256
KD = D // 128
LN_EPS = 1e-5

HEADS0, DK0 = 16, 128
QUADS = HEADS0 // 4
QW = 4 * DK0
STEPS0 = B * QUADS
MASKED = -1e30


def wait(eng, sem, value):
    if isinstance(value, int) and value <= 0:
        return
    eng.wait_ge(sem, value)


def matmul3(nc, out, lhs, rhs, first, last):
    (lh, ll), (rh, rl) = lhs, rhs
    nc.tensor.matmul(out, lh, rl, start=first, stop=False)
    nc.tensor.matmul(out, ll, rh, start=False, stop=False)
    return nc.tensor.matmul(out, lh, rh, start=False, stop=last)


def finish_stats(nc, dve, done, count, stats, mean, var_eps, tmp, eps):
    half = D // 2
    me, m2e, mo, m2o = stats[:, :, 1], stats[:, :, 2], stats[:, :, 4], stats[:, :, 5]

    def link(ins):
        nonlocal count
        count += 1
        ins.then_inc(done, 1)

    link(nc.vector.tensor_tensor(tmp[:, 0, :], me, mo, ALU.add))
    link(nc.vector.tensor_tensor(tmp[:, 1, :], me, mo, ALU.subtract))
    link(nc.vector.tensor_tensor(tmp[:, 2, :], m2e, m2o, ALU.add))
    dve.wait_ge(done, count)
    link(nc.vector.tensor_scalar(mean, tmp[:, 0, :], 0.5, None, ALU.mult))
    link(nc.vector.scalar_tensor_tensor(tmp[:, 3, :], tmp[:, 1, :], half / 2.0, tmp[:, 1, :], ALU.mult, ALU.mult))
    dve.wait_ge(done, count)
    link(nc.vector.tensor_tensor(tmp[:, 4, :], tmp[:, 3, :], tmp[:, 2, :], ALU.add))
    dve.wait_ge(done, count)
    link(nc.vector.tensor_scalar(var_eps, tmp[:, 4, :], 1.0 / D, float(eps), ALU.mult, ALU.add))
    return count


def decoder_kernel(nc, a, out):
    ctx = ExitStack()
    with ctx:
        def sb(name, shape, dt=F32, where=ctx):
            return where.enter_context(nc.sbuf_tensor(name, shape, dt))

        sems_in_use = []

        def sem(name):
            sems_in_use.append(nc.alloc_semaphore(name=name))
            return sems_in_use[-1]

        def clear_semaphores():
            nc.clear_and_free_semaphores(sems_in_use)
            nc.all_engine_barrier()
            sems_in_use.clear()

        bank = [ctx.enter_context(nc.psum_tensor(f"bank{i}", [128, 512], F32)) for i in range(8)]
        X = sb("X", [128, B, D])
        ident = sb("ident", [128, 128])
        mean = sb("mean", [128, B])
        var_eps = sb("var_eps", [128, B])
        rstd = sb("rstd", [128, B])
        minus_half = sb("minus_half", [128, B])
        stats = sb("stats", [128, B, 6])
        ln_tmp = sb("ln_tmp", [128, 5, B])

        phase_attn0(nc, a, sem, sb, bank, X, ident, mean, var_eps, rstd, minus_half, stats, ln_tmp)
        phase_rest(nc, a, sem, sb, bank, X, ident, mean, var_eps, rstd, minus_half, stats, ln_tmp, out, clear_semaphores)


def second_norm(nc, dve, done, count, var_eps, rstd, square, tmp, eps):
    for ins in (lambda: nc.vector.tensor_tensor(square, rstd, rstd, ALU.mult),
                lambda: nc.vector.tensor_tensor(square, square, tmp[:, 4, :], ALU.mult),
                lambda: nc.vector.tensor_scalar(var_eps, square, 1.0 / D, float(eps), ALU.mult, ALU.add)):
        ins().then_inc(done, 1)
        count += 1
        dve.wait_ge(done, count)
    return count


def batch(tile, b):
    if isinstance(b, int):
        return tile[:, b, :]
    return tile[:, bass.ds(b, 1), :].rearrange("p a n -> p (a n)")


def one(tile, b):
    return tile[:, b:b + 1] if isinstance(b, int) else tile[:, bass.ds(b, 1)]


def phase_attn0(nc, a, sem, sb_, bank, X, ident, mean, var_eps, rstd, minus_half, stats, ln_tmp):
    local = ExitStack()
    with local:
        def sb(name, shape, dt=F32):
            return sb_(name, shape, dt, local)

        STAGES = 6
        h_of = sb("h_of", [128, D])
        WH = sb("WH", [128, 3, KD, HEADS0 * DK0], F32R)
        WL = sb("WL", [128, 3, KD, HEADS0 * DK0], F32R)
        WO = sb("WO", [128, HEADS0, D])
        stage = sb("stage", [128, STAGES, KD, QW])
        qk_bias = sb("qk_bias", [128, 2 * HEADS0 * DK0], BF16)
        ones_row = sb("ones_row", [128, 128], BF16)
        bias_in = sb("bias_in", [32, DK0])
        bias_part = sb("bias_part", [32, 3, DK0], BF16)
        bias_left = sb("bias_left", [32, 2, DK0])
        cos = sb("cos", [128, DK0])
        sin = sb("sin", [128, DK0])
        mask_f = sb("mask_f", [128, 128])
        mask = sb("mask", [128, 4, 128], BF16)
        ident_b = sb("ident_b", [128, 128], BF16)
        gb = sb("gb", [128, 2, KD])
        out_bias = sb("out_bias", [128, D])
        out_const = sb("out_const", [128, D])
        bv_col = sb("bv_col", [128, HEADS0])
        square = sb("square", [128, B])
        rstd2 = sb("rstd2", [128, B])
        rstd12 = sb("rstd12", [128, B])
        xn = sb("xn", [128, D])
        xT_full = sb("xT_full", [128, KD, 128])
        xT_hi = sb("xT_hi", [128, KD, 128], F32R)
        xT_lo = sb("xT_lo", [128, KD, 128], F32R)
        roped_q = sb("roped_q", [128, 2, QW])
        roped_k = sb("roped_k", [128, 2, QW])
        sin_q = sb("sin_q", [128, QW])
        sin_k = sb("sin_k", [128, QW])
        qT = sb("qT", [128, 4, 128])
        kT = sb("kT", [128, 4, 128])
        V = sb("V", [128, 4, QW])
        P = sb("P", [128, 4, 128])
        PT = sb("PT", [128, 4, 128])
        oT = sb("oT", [128, 4, 128])
        neg_max = sb("neg_max", [128, QUADS, 4])
        exp_sum = sb("exp_sum", [128, QUADS, 4])
        inv_sum = sb("inv_sum", [128, QUADS, 4])

        x_loaded = [sem(f"x{g}_loaded") for g in range(4)]
        consts_loaded = sem("consts_loaded")
        wo_loaded = sem("wo_loaded")
        stage_loaded = [sem(f"stage{i}_loaded") for i in range(STAGES)]
        weights_rounded = sem("weights_rounded")
        weights_split = sem("weights_split")
        bias_split = sem("bias_split")
        bias_placed = sem("bias_placed")
        consts_made = sem("consts_made")
        const_projected = sem("const_projected")
        const_ready = sem("const_ready")
        ln0 = sem("ln0")
        rstd_ready = sem("rstd_ready")
        half_set = sem("half_set")
        xn_ready = sem("xn_ready")
        x_transposed = sem("x_transposed")
        xT_evacuated = sem("xT_evacuated")
        xT_split = sem("xT_split")
        q_projected = sem("q_projected")
        k_projected = sem("k_projected")
        v_projected = sem("v_projected")
        q_products = sem("q_products")
        k_products = sem("k_products")
        q_roped = sem("q_roped")
        k_roped = sem("k_roped")
        v_ready = sem("v_ready")
        q_transposed = sem("q_transposed")
        k_transposed = sem("k_transposed")
        qT_ready = sem("qT_ready")
        kT_ready = sem("kT_ready")
        scored = sem("scored")
        max_found = sem("max_found")
        exps_done = sem("exps_done")
        inv_ready = sem("inv_ready")
        probs_ready = sem("probs_ready")
        p_transposed = sem("p_transposed")
        PT_ready = sem("PT_ready")
        pv_done = sem("pv_done")
        oT_ready = sem("oT_ready")
        out_projected = sem("out_projected")
        out_added = sem("out_added")
        h_added = sem("h_added")

        Q, K, V_, QT, KT, SC, PO, OUT = bank
        w_src = [a[n].rearrange("(k p) n -> p k n", p=128) for n in ("wqT", "wkT", "wvT")]
        ITEMS = [(q, w) for q in range(QUADS) for w in range(3)]

        with nc.Block() as block:
            @block.sync
            def _(sp):
                sp.dma_start(ident[:], a["ident"]).then_inc(consts_loaded, 16)
                sp.dma_start(mask_f[:], a["causal"]).then_inc(consts_loaded, 16)
                sp.dma_start(cos[:], a["cos"]).then_inc(consts_loaded, 16)
                sp.dma_start(sin[:], a["sin"]).then_inc(consts_loaded, 16)
                sp.dma_start(gb[:, 0, :], a["ln_gT"]).then_inc(consts_loaded, 16)
                sp.dma_start(gb[:, 1, :], a["ln_bT"]).then_inc(consts_loaded, 16)
                sp.dma_start(bias_in[0:16, :], a["L0_attn_bq"].rearrange("(h n) -> h n", n=DK0)).then_inc(consts_loaded, 16)
                sp.dma_start(bias_in[16:32, :], a["L0_attn_bk"].rearrange("(h n) -> h n", n=DK0)).then_inc(consts_loaded, 16)
                sp.dma_start(bv_col[:], a["bvT"]).then_inc(consts_loaded, 16)
                sp.dma_start(out_bias[:], a["L0_attn_bo"].rearrange("(a n) -> a n", a=1).broadcast_to([128, D])).then_inc(consts_loaded, 16)
                for i, (q, w) in enumerate(ITEMS):
                    wait(sp, weights_split, i - STAGES + 1)
                    sp.dma_start(stage[:, i % STAGES, :, :], w_src[w][:, :, q * QW:(q + 1) * QW]).then_inc(stage_loaded[i % STAGES], 16)
                    if i == 2:
                        sp.wait_ge(bias_split, 5)
                        for part in range(3):
                            sp.dma_start(qk_bias[part:part + 1, :].rearrange("a (h n) -> a h n", n=DK0),
                                         bias_part[:, part, :]).then_inc(bias_placed, 16)
                    if i == STAGES:
                        sp.dma_start(WO[:], a["woT"].rearrange("(h p) n -> p h n", p=DK0)).then_inc(wo_loaded, 16)

            @block.gpsimd
            def _(pool):
                nc.gpsimd.memset(minus_half[:], -0.5).then_inc(half_set, 1)
                pool.wait_ge(half_set, 1)
                pool.wait_ge(ln0, B + 7)
                nc.gpsimd.tensor_tensor(rstd[:], var_eps[:], minus_half[:], ALU.pow).then_inc(rstd_ready, 1)
                pool.wait_ge(ln0, B + 7 + 3)
                nc.gpsimd.tensor_tensor(rstd2[:], var_eps[:], minus_half[:], ALU.pow).then_inc(rstd_ready, 1)

                def step(t, q):
                    p = q % 2
                    pool.wait_ge(q_products, 2 * t + 2)
                    nc.gpsimd.tensor_tensor(roped_q[:, p, :], roped_q[:, p, :], sin_q[:], ALU.add).then_inc(q_roped, 1)
                    pool.wait_ge(k_products, 2 * t + 2)
                    nc.gpsimd.tensor_tensor(roped_k[:, p, :], roped_k[:, p, :], sin_k[:], ALU.add).then_inc(k_roped, 1)

                with pool.Fori(0, B) as b:
                    for q in range(QUADS):
                        step(b * QUADS + q, q)

            @block.scalar
            def _(act):
                def round_weights(i):
                    q, w = ITEMS[i]
                    act.wait_ge(stage_loaded[i % STAGES], 16 * (i // STAGES + 1))
                    nc.scalar.activation(WH[:, w, :, q * QW:(q + 1) * QW], stage[:, i % STAGES, :, :], ACT.Copy).then_inc(weights_rounded, 1)

                def evacuate_xT(b):
                    act.wait_ge(x_transposed, b + 1)
                    for k in range(KD):
                        wait(act, xT_split, 2 * b)
                        nc.scalar.activation(xT_full[:, k, :], V_[:, k * 128:(k + 1) * 128], ACT.Identity,
                                             bias=gb[:, 1, k:k + 1], scale=gb[:, 0, k:k + 1]).then_inc(xT_evacuated, 1)

                def step(s, q, b, first=False, last=False, drain=False):
                    u = s - 2
                    if not (isinstance(u, int) and u < 0):
                        uq = (q + 2) % 4
                        for h in range(4):
                            act.wait_ge(max_found, 1 + u)
                            wait(act, p_transposed, u)
                            ins = nc.scalar.activation(P[:, h, :], SC[:, h * 128:(h + 1) * 128], ACT.Exp,
                                                       bias=neg_max[:, uq, h:h + 1], accum_out=exp_sum[:, uq, h:h + 1])
                        ins.then_inc(exps_done, 1)
                    if not drain:
                        act.wait_ge(v_projected, s + 1)
                        wait(act, pv_done, s - 3)
                        nc.scalar.activation(V[:, q, :], V_[:], ACT.Copy).then_inc(v_ready, 1)
                        if first and q < 3:
                            for i in range(3 * q + 3, 3 * q + 6):
                                round_weights(i)
                    u = s - 1
                    if not (isinstance(u, int) and (u < 0 or u >= STEPS0)):
                        act.wait_ge(q_transposed, u + 1)
                        wait(act, scored, u)
                        nc.scalar.activation(qT[:].rearrange("p h n -> p (h n)"), QT[:], ACT.Copy, scale=1.0 / DK0 ** 0.5).then_inc(qT_ready, 1)
                        act.wait_ge(k_transposed, u + 1)
                        nc.scalar.activation(kT[:].rearrange("p h n -> p (h n)"), KT[:], ACT.Copy).then_inc(kT_ready, 1)
                    u = s - 2
                    if not (isinstance(u, int) and u < 0):
                        act.wait_ge(p_transposed, u + 1)
                        wait(act, pv_done, u)
                        nc.scalar.activation(PT[:].rearrange("p h n -> p (h n)"), PO[:], ACT.Copy).then_inc(PT_ready, 1)
                        act.wait_ge(pv_done, u + 1)
                        wait(act, out_projected, u)
                        nc.scalar.activation(oT[:].rearrange("p h n -> p (h n)"), PO[:], ACT.Copy).then_inc(oT_ready, 1)
                    if q == 2 and not last and not drain:
                        evacuate_xT(b + 1)

                for g in range(4):
                    some = slice(g * B // 4, (g + 1) * B // 4)
                    act.dma_start(X[:, some, :], a["x"][some].rearrange("b p d -> p b d")).then_inc(x_loaded[g], 16)
                for i in range(3):
                    round_weights(i)
                act.wait_ge(consts_loaded, 160)
                evacuate_xT(0)
                for q in range(QUADS):
                    step(q, q, 0, first=True)
                with act.Fori(1, B - 1) as b:
                    for q in range(QUADS):
                        step(b * QUADS + q, q, b)
                for q in range(QUADS):
                    step((B - 1) * QUADS + q, q, B - 1, last=True)
                for s in (STEPS0, STEPS0 + 1):
                    step(s, s % 4, B, drain=True)

            @block.vector
            def _(dve):
                dve.wait_ge(consts_loaded, 160)
                nc.vector.tensor_copy(ident_b[:], ident[:]).then_inc(consts_made, 1)
                for h in range(4):
                    nc.vector.tensor_copy(mask[:, h, :], mask_f[:]).then_inc(consts_made, 1)
                nc.vector.memset(ones_row[:], 0.0).then_inc(consts_made, 1)
                nc.vector.memset(qk_bias[:], 0.0).then_inc(consts_made, 1)
                dve.wait_ge(consts_made, 7)
                nc.vector.memset(ones_row[0:3, :], 1.0).then_inc(consts_made, 1)
                nc.vector.tensor_copy(bias_part[:, 0, :], bias_in[:]).then_inc(bias_split, 1)
                dve.wait_ge(bias_split, 1)
                nc.vector.tensor_tensor(bias_left[:, 0, :], bias_in[:], bias_part[:, 0, :], ALU.subtract).then_inc(bias_split, 1)
                dve.wait_ge(bias_split, 2)
                nc.vector.tensor_copy(bias_part[:, 1, :], bias_left[:, 0, :]).then_inc(bias_split, 1)
                dve.wait_ge(bias_split, 3)
                nc.vector.tensor_tensor(bias_left[:, 1, :], bias_left[:, 0, :], bias_part[:, 1, :], ALU.subtract).then_inc(bias_split, 1)
                dve.wait_ge(bias_split, 4)
                nc.vector.tensor_copy(bias_part[:, 2, :], bias_left[:, 1, :]).then_inc(bias_split, 1)

                for g in range(4):
                    dve.wait_ge(x_loaded[g], 16)
                    for b in range(g * B // 4, (g + 1) * B // 4):
                        nc.vector.bn_stats(stats[:, b, :], X[:, b, :]).then_inc(ln0, 1)
                dve.wait_ge(ln0, B)
                n = finish_stats(nc, dve, ln0, B, stats, mean[:], var_eps[:], ln_tmp, LN_EPS)
                dve.wait_ge(ln0, n)
                dve.wait_ge(rstd_ready, 1)
                n = second_norm(nc, dve, ln0, n, var_eps[:], rstd[:], square[:], ln_tmp, LN_EPS)
                dve.wait_ge(rstd_ready, 2)
                nc.vector.tensor_tensor(rstd12[:], rstd[:], rstd2[:], ALU.mult).then_inc(ln0, 1)
                dve.wait_ge(ln0, n + 1)

                def split_weights(i):
                    q, w = ITEMS[i]
                    dve.wait_ge(weights_rounded, i + 1)
                    cols = slice(q * QW, (q + 1) * QW)
                    nc.vector.tensor_tensor(WL[:, w, :, cols], stage[:, i % STAGES, :, :], WH[:, w, :, cols].bitcast(F32), ALU.subtract).then_inc(weights_split, 1)

                def normalise(b):
                    wait(dve, x_transposed, b)
                    nc.vector.tensor_scalar(xn[:], batch(X, b), one(mean, b), one(rstd12, b), ALU.subtract, ALU.mult).then_inc(xn_ready, 1)

                def split_xT(b):
                    dve.wait_ge(xT_evacuated, 2 * b + 2)
                    wait(dve, v_projected, 4 * b)
                    nc.vector.tensor_copy(xT_hi[:], xT_full[:]).then_inc(xT_split, 1)
                    dve.wait_ge(xT_split, 2 * b + 1)
                    nc.vector.tensor_tensor(xT_lo[:], xT_full[:], xT_hi[:].bitcast(F32), ALU.subtract).then_inc(xT_split, 1)

                def rope(t, p, src, projected, products, transposed, roped_sum, roped, sin_part):
                    dve.wait_ge(projected, t + 1)
                    wait(dve, transposed, t - 1)
                    quad = lambda ap: ap.rearrange("p (h n) -> p h n", h=4)
                    nc.vector.tensor_tensor(quad(roped[:, p, :]), quad(src[:]), cos[:].rearrange("p (h n) -> p h n", h=1).broadcast_to([128, 4, DK0]), ALU.mult).then_inc(products, 1)
                    wait(dve, roped_sum, t)
                    half = lambda ap, i: quad(ap)[:, :, i * 64:(i + 1) * 64]
                    for i in range(2):
                        ins = nc.vector.tensor_tensor(half(sin_part[:], i), half(src[:], 1 - i),
                                                      sin[:, i * 64:(i + 1) * 64].rearrange("p (h n) -> p h n", h=1).broadcast_to([128, 4, 64]), ALU.mult)
                    ins.then_inc(products, 1)

                def find_max(u, uq):
                    dve.wait_ge(scored, u + 1)
                    nc.vector.tensor_reduce(neg_max[:, uq, :], SC[:].rearrange("p (h n) -> p h n", h=4), AX.X, ALU.max, negate=True).then_inc(max_found, 1)

                def step(s, q, b, first=False, last=False, drain=False):
                    u, uq = s - 2, (q + 2) % 4
                    past = not (isinstance(u, int) and u < 0)
                    if past:
                        find_max(u, uq)
                    if not drain:
                        rope(s, q % 2, Q, q_projected, q_products, q_transposed, q_roped, roped_q, sin_q)
                    if past:
                        dve.wait_ge(exps_done, u + 1)
                        nc.vector.reciprocal(inv_sum[:, uq, :], exp_sum[:, uq, :]).then_inc(inv_ready, 1)
                        dve.wait_ge(inv_ready, u + 1)
                        nc.vector.tensor_tensor(P[:], P[:], inv_sum[:, uq, :].rearrange("p (h n) -> p h n", n=1).broadcast_to([128, 4, 128]), ALU.mult).then_inc(probs_ready, 1)
                    if not drain:
                        rope(s, q % 2, K, k_projected, k_products, k_transposed, k_roped, roped_k, sin_k)
                        if first and q < 3:
                            for i in range(3 * q + 3, 3 * q + 6):
                                split_weights(i)
                        if q == 0:
                            add_h(b)
                        if q == 1 and not last:
                            normalise(b + 1)
                        if q == 3 and not last:
                            split_xT(b + 1)

                def add_h(b):
                    nc.vector.tensor_scalar(h_of[:], batch(X, b), one(mean, b), one(rstd, b), ALU.subtract, ALU.mult).then_inc(h_added, 1)
                    dve.wait_ge(h_added, 2 * b + 1)
                    nc.vector.tensor_tensor(batch(X, b), batch(X, b), h_of[:], ALU.add).then_inc(h_added, 1)

                def add_out(b):
                    dve.wait_ge(out_projected, 4 * b + 4)
                    dve.wait_ge(h_added, 2 * b + 2)
                    nc.vector.tensor_tensor(batch(X, b), OUT[:, 0:D], batch(X, b), ALU.add).then_inc(out_added, 1)
                    dve.wait_ge(out_added, 2 * b + 1)
                    nc.vector.tensor_tensor(batch(X, b), batch(X, b), out_const[:], ALU.add).then_inc(out_added, 1)
                    dve.wait_ge(out_added, 2 * b + 2)
                    nc.vector.bn_stats(batch(stats, b), batch(X, b))

                normalise(0)
                for i in range(3):
                    split_weights(i)
                split_xT(0)
                for q in range(QUADS):
                    step(q, q, 0, first=True)
                dve.wait_ge(const_projected, 1)
                nc.vector.tensor_tensor(out_const[:], KT[:, 0:D], out_bias[:], ALU.add).then_inc(const_ready, 1)
                dve.wait_ge(const_ready, 1)
                with dve.Fori(1, B - 1) as b:
                    for q in range(QUADS):
                        step(b * QUADS + q, q, b)
                        if q == 2:
                            add_out(b - 1)
                for q in range(QUADS):
                    step((B - 1) * QUADS + q, q, B - 1, last=True)
                    if q == 2:
                        add_out(B - 2)
                for s in (STEPS0, STEPS0 + 1):
                    step(s, s % 4, B, drain=True)
                add_out(B - 1)

            @block.tensor
            def _(pe):
                def transpose_x(b):
                    pe.wait_ge(xn_ready, b + 1)
                    wait(pe, v_ready, 4 * b - 1)
                    for k in range(KD):
                        ins = nc.tensor.transpose(V_[:, k * 128:(k + 1) * 128], xn[:, k * 128:(k + 1) * 128], ident[:])
                    ins.then_inc(x_transposed, 1)

                def project(t, q, b):
                    if q == 0:
                        pe.wait_ge(xT_split, 2 * b + 2)
                    cols = slice(q * QW, (q + 1) * QW)
                    for w, (dst, done, free, n_free) in enumerate((
                            (Q, q_projected, q_products, 2 * t),
                            (K, k_projected, k_products, 2 * t),
                            (V_, v_projected, v_ready, t))):
                        wait(pe, free, n_free)
                        if isinstance(t, int) and t < QUADS:
                            pe.wait_ge(weights_split, 3 * q + w + 1)
                            if t == 0 and w == 0:
                                pe.wait_ge(consts_made, 8)
                                pe.wait_ge(bias_placed, 48)
                        if w == 2 and q == 3:
                            wait(pe, xT_evacuated, 4 + 2 * b) if not (isinstance(b, int) and b == B - 1) else None
                        if w < 2:
                            nc.tensor.matmul(dst[:], ones_row[:], qk_bias[:, w * HEADS0 * DK0 + q * QW:w * HEADS0 * DK0 + (q + 1) * QW], start=True, stop=False)
                        for k in range(KD):
                            ins = matmul3(nc, dst[:], (xT_hi[:, k, :], xT_lo[:, k, :]), (WH[:, w, k, cols], WL[:, w, k, cols]),
                                          first=(w == 2 and k == 0), last=(k == KD - 1))
                        ins.then_inc(done, 1)

                def transpose_qk(u, uq):
                    for src, ready, dst, done, free in ((roped_q, q_roped, QT, q_transposed, qT_ready), (roped_k, k_roped, KT, k_transposed, kT_ready)):
                        pe.wait_ge(ready, u + 1)
                        wait(pe, free, u)
                        for h in range(4):
                            ins = nc.tensor.transpose(dst[:, h * 128:(h + 1) * 128], src[:, uq % 2, h * 128:(h + 1) * 128], ident[:])
                        ins.then_inc(done, 1)

                def transpose_p(u):
                    pe.wait_ge(probs_ready, u + 1)
                    wait(pe, oT_ready, u)
                    for h in range(4):
                        ins = nc.tensor.transpose(PO[:, h * 128:(h + 1) * 128], P[:, h, :], ident[:])
                    ins.then_inc(p_transposed, 1)

                def out_project(u, uq):
                    pe.wait_ge(oT_ready, u + 1)
                    if uq == 0:
                        wait(pe, out_added, u // 4 * 2 if isinstance(u, int) else None) if isinstance(u, int) else pe.wait_ge(out_added, out_count[0])
                    for h in range(4):
                        ins = nc.tensor.matmul(OUT[:, 0:D], oT[:, h, :], WO[:, 4 * uq + h, :], start=(uq == 0 and h == 0), stop=(uq == 3 and h == 3))
                    ins.then_inc(out_projected, 1)

                def score(u):
                    pe.wait_ge(qT_ready, u + 1)
                    pe.wait_ge(kT_ready, u + 1)
                    wait(pe, exps_done, u)
                    nc.tensor.matmul(SC[:], ident_b[:], mask[:].rearrange("p h n -> p (h n)"), start=True, stop=True)
                    for h in range(4):
                        ins = nc.tensor.matmul(SC[:, h * 128:(h + 1) * 128], qT[:, h, :], kT[:, h, :], start=False, stop=True, skip_group_check=True)
                    ins.then_inc(scored, 1)

                def weigh(u, uq):
                    pe.wait_ge(PT_ready, u + 1)
                    for h in range(4):
                        ins = nc.tensor.matmul(PO[:, h * 128:(h + 1) * 128], V[:, uq, h * 128:(h + 1) * 128], PT[:, h, :], start=True, stop=True)
                    ins.then_inc(pv_done, 1)

                out_count = [0]

                def step(s, q, b, last=False):
                    live = lambda u: not isinstance(u, int) or 0 <= u < STEPS0
                    if live(s):
                        project(s, q, b)
                    if live(s - 1):
                        transpose_qk(s - 1, (q + 3) % 4)
                    if live(s - 2):
                        transpose_p(s - 2)
                    if live(s - 3):
                        if not isinstance(b, int):
                            out_count[0] = 2 * b
                        out_project(s - 3, (q + 1) % 4)
                    if live(s - 1):
                        score(s - 1)
                    if live(s - 2):
                        weigh(s - 2, (q + 2) % 4)
                    if q == 2 and not last:
                        transpose_x(b + 1)

                pe.wait_ge(consts_loaded, 160)
                transpose_x(0)
                for q in range(QUADS):
                    step(q, q, 0)
                pe.wait_ge(wo_loaded, 16)
                pe.wait_ge(kT_ready, 3)
                for h in range(HEADS0):
                    ins = nc.tensor.matmul(KT[:, 0:D], bv_col[:, h:h + 1].broadcast_to([128, 128]), WO[:, h, :], start=(h == 0), stop=(h == HEADS0 - 1))
                ins.then_inc(const_projected, 1)
                pe.wait_ge(const_ready, 1)
                with pe.Fori(1, B - 1) as b:
                    for q in range(QUADS):
                        step(b * QUADS + q, q, b)
                for q in range(QUADS):
                    step((B - 1) * QUADS + q, q, B - 1, last=True)
                for s in range(STEPS0, STEPS0 + 3):
                    step(s, s % 4, B, last=True)

def live(u, n=B):
    return not isinstance(u, int) or 0 <= u < n


def run_pairs(eng, step, extra, peeled=1):
    for s in range(2 * peeled):
        step(s, s % 2)
    with eng.Fori(peeled, B // 2 - 1) as i:
        for j in range(2):
            step(i * 2 + j, j)
    for s in range(B - 2, B + extra):
        step(s, s % 2)


def phase_retention(nc, a, sem, sb_, bank, X, ident, mean, var_eps, rstd, minus_half, stats, ln_tmp, ahead, ahead_loaded):
    local = ExitStack()
    with local:
        def sb(name, shape, dt=F32):
            return sb_(name, shape, dt, local)

        H_ = 2
        V = sb("ret_V", [128, H_, B, 128])
        gate = sb("ret_gate", [128, B, D])
        O = sb("ret_O", [128, B, D])
        AT = sb("ret_AT", [128, H_, 128])
        decay = sb("ret_decay", [128, H_, 128])
        Wh = sb("ret_Wh", [128, H_, 128])
        WhT = sb("ret_WhT", [128, H_, 128])
        G = sb("ret_G", [128, H_, 128])
        w_in = sb("ret_w_in", [128, 2, KD, D])
        w_hi = sb("ret_w_hi", [128, 2, KD, D], F32R)
        w_lo = sb("ret_w_lo", [128, 2, KD, D], F32R)
        gn = sb("ret_gn", [128, 2, D])
        ctx_all = sb("ret_ctx_all", [128, KD, B * S])
        ctxT = sb("ret_ctxT", [128, 2, H_, 128])
        xn = sb("ret_xn", [128, 2, D])
        xT_full = sb("ret_xT_full", [128, 2, KD, 128])
        xT_hi = sb("ret_xT_hi", [128, 2, KD, 128], F32R)
        xT_lo = sb("ret_xT_lo", [128, 2, KD, 128], F32R)
        TT = sb("ret_TT", [128, 2, H_, 128])
        zeros = sb("ret_zeros", [128, D], BF16)

        consts = sem("ret_consts")
        ctx_loaded = sem("ret_ctx_loaded")
        ctx_copied = sem("ret_ctx_copied")
        w_rounded = sem("ret_w_rounded")
        w_split = sem("ret_w_split")
        zeroed = sem("ret_zeroed")
        gram_done = sem("ret_gram_done")
        G_ready = sem("ret_G_ready")
        ln = sem("ret_ln")
        rstd_ready = sem("ret_rstd")
        xn_ready = sem("ret_xn_ready")
        transposed = sem("ret_transposed")
        full_ready = sem("ret_full_ready")
        hi_ready = sem("ret_hi_ready")
        lo_ready = sem("ret_lo_ready")
        T_done = sem("ret_T_done")
        gate_done = sem("ret_gate_done")
        TT_ready = sem("ret_TT_ready")
        V_ready = sem("ret_V_ready")
        gate_ready = sem("ret_gate_ready")
        scored = sem("ret_scored")
        AT_ready = sem("ret_AT_ready")

        with nc.Block() as block:
            @block.sync
            def _(sp):
                for dst, src in ((WhT[:], a["WhT"]), (Wh[:], a["L0_xattn_Wh"].rearrange("h e d -> e h d")),
                                 (w_in[:, 0], a["L0_xattn_wg_w"].rearrange("(k p) n -> p k n", p=128)),
                                 (w_in[:, 1], a["L0_xattn_wo_w"].rearrange("(k p) n -> p k n", p=128)),
                                 (decay[:], a["decayT"]),
                                 (gn[:, 0, :], a["L0_xattn_gn_gamma"].rearrange("(a n) -> a n", a=1).broadcast_to([128, D])),
                                 (gn[:, 1, :], a["L0_xattn_gn_beta"].rearrange("(a n) -> a n", a=1).broadcast_to([128, D]))):
                    sp.dma_start(dst, src).then_inc(consts, 16)
                sp.dma_start(ctx_all[:], a["ctxT"].rearrange("(k p) n -> p k n", p=128)).then_inc(ctx_loaded, 16)
                for dst, src in ahead:
                    sp.dma_start(dst, src).then_inc(ahead_loaded, 16)

            @block.gpsimd
            def _(pool):
                pool.wait_ge(ln, 7)
                nc.gpsimd.tensor_tensor(rstd[:], var_eps[:], minus_half[:], ALU.pow).then_inc(rstd_ready, 1)

            @block.scalar
            def _(act):
                act.wait_ge(consts, 112)
                nc.scalar.activation(w_hi[:], w_in[:], ACT.Copy).then_inc(w_rounded, 1)
                act.wait_ge(gram_done, 1)
                nc.scalar.activation(G[:].rearrange("p h n -> p (h n)"), bank[7][:, 0:256], ACT.Copy).then_inc(G_ready, 1)

                def step(s, j):
                    if live(s):
                        act.wait_ge(transposed, s + 1)
                        wait(act, gate_done, s - 1)
                        nc.scalar.activation(flat(xT_full[:, j]), bank[j][:, 0:256], ACT.Copy).then_inc(full_ready, 1)
                        nc.scalar.activation(flat(xT_hi[:, j]), bank[j][:, 0:256], ACT.Copy).then_inc(hi_ready, 1)
                    if live(s - 1):
                        act.wait_ge(T_done, s)
                        wait(act, scored, s - 2)
                        nc.scalar.activation(flat(TT[:, 1 - j]), bank[3 - j][:, 0:256], ACT.Copy).then_inc(TT_ready, 1)
                run_pairs(act, step, 1)

            @block.vector
            def _(dve):
                n = finish_stats(nc, dve, ln, 0, stats, mean[:], var_eps[:], ln_tmp, LN_EPS)
                nc.vector.memset(zeros[:], 0.0).then_inc(zeroed, 1)
                dve.wait_ge(w_rounded, 1)
                nc.vector.tensor_tensor(w_lo[:], w_in[:], w_hi[:].bitcast(F32), ALU.subtract).then_inc(w_split, 1)
                dve.wait_ge(rstd_ready, 1)
                dve.wait_ge(ln, n)

                def normalise(b, j):
                    wait(dve, transposed, b - 1)
                    nc.vector.tensor_scalar(xn[:, j, :], batch(X, b), one(mean, b), one(rstd, b), ALU.subtract, ALU.mult).then_inc(xn_ready, 1)

                def copy_ctx(b, j):
                    wait(dve, scored, b - 1)
                    at = slice(b * S, (b + 1) * S) if isinstance(b, int) else bass.ds(b * S, S)
                    nc.vector.tensor_scalar(ctxT[:, j], ctx_all[:, :, at], 1.0, None, ALU.mult).then_inc(ctx_copied, 1)

                normalise(0, 0)
                dve.wait_ge(ctx_loaded, 16)

                def step(s, j):
                    if live(s + 1):
                        normalise(s + 1, 1 - j)
                    if live(s):
                        copy_ctx(s, j)
                    if live(s):
                        dve.wait_ge(hi_ready, s + 1)
                        nc.vector.tensor_tensor(flat(xT_lo[:, j]), flat(xT_full[:, j]), flat(xT_hi[:, j]).bitcast(F32), ALU.subtract).then_inc(lo_ready, 1)
                    if live(s - 1):
                        dve.wait_ge(gate_done, s)
                        v_out = V[:, :, s - 1, :] if isinstance(s, int) else V[:, :, bass.ds(s - 1, 1), :].rearrange("p h a n -> p h (a n)")
                        nc.vector.tensor_scalar(v_out, bank[5 - j][:, 256:512].rearrange("p (h n) -> p h n", h=H_), 1.0, None, ALU.mult).then_inc(V_ready, 1)
                        nc.vector.tensor_scalar(batch(gate, s - 1), bank[5 - j][:, 0:D], 0.0, None, ALU.max).then_inc(gate_ready, 1)
                run_pairs(dve, step, 1)
                dve.wait_ge(scored, B)
                nc.vector.tensor_tensor(flat(AT[:]), bank[6][:, 0:256], flat(decay[:]), ALU.mult).then_inc(AT_ready, 1)
                dve.wait_ge(AT_ready, 1)
                nc.vector.scalar_tensor_tensor(flat(AT[:]), flat(AT[:]), -1.0, flat(AT[:]), ALU.mult, ALU.max).then_inc(AT_ready, 1)
                dve.wait_ge(AT_ready, 2)
                nc.vector.tensor_scalar(flat(AT[:]), flat(AT[:]), 1.0, None, ALU.max).then_inc(AT_ready, 1)

            @block.tensor
            def _(pe):
                pe.wait_ge(consts, 112)
                for h in range(H_):
                    ins = nc.tensor.matmul(bank[7][:, h * 128:(h + 1) * 128], WhT[:, h, :], WhT[:, h, :], start=True, stop=True)
                ins.then_inc(gram_done, 1)
                pe.wait_ge(zeroed, 1)
                nc.tensor.matmul(bank[6][:, 0:256], zeros[:, 0:128], zeros[:], start=True, stop=True)
                pe.wait_ge(G_ready, 1)
                pe.wait_ge(w_split, 1)

                def step(s, j):
                    if live(s):
                        pe.wait_ge(xn_ready, s + 1)
                        wait(pe, hi_ready, s - 1)
                        for k in range(KD):
                            ins = nc.tensor.transpose(bank[j][:, k * 128:(k + 1) * 128], xn[:, j, k * 128:(k + 1) * 128], ident[:])
                        ins.then_inc(transposed, 1)
                    u, i = s - 1, 1 - j
                    if live(u):
                        pe.wait_ge(full_ready, u + 1)
                        pe.wait_ge(ctx_copied, u + 1)
                        wait(pe, TT_ready, u - 1)
                        for h in range(H_):
                            ins = nc.tensor.matmul(bank[2 + i][:, h * 128:(h + 1) * 128], G[:, h, :], xT_full[:, i, h, :], start=True, stop=True)
                        ins.then_inc(T_done, 1)
                        wait(pe, gate_ready, u - 1)
                        for h in range(H_):
                            nc.tensor.matmul(bank[4 + i][:, 256 + h * 128:256 + (h + 1) * 128], ctxT[:, i, h, :], Wh[:, h, :], start=True, stop=True)
                        pe.wait_ge(lo_ready, u + 1)
                        for k in range(KD):
                            ins = matmul3(nc, bank[4 + i][:, 0:D], (xT_hi[:, i, k, :], xT_lo[:, i, k, :]), (w_hi[:, 0, k, :], w_lo[:, 0, k, :]),
                                          first=(k == 0), last=(k == KD - 1))
                        ins.then_inc(gate_done, 1)
                    u = s - 2
                    if live(u):
                        pe.wait_ge(TT_ready, u + 1)
                        for h in range(H_):
                            ins = nc.tensor.matmul(bank[6][:, h * 128:(h + 1) * 128], ctxT[:, j, h, :], TT[:, j, h, :], start=False, stop=True, skip_group_check=True)
                        ins.then_inc(scored, 1)
                run_pairs(pe, step, 2)

        vproj = sem("ret_av_done")
        O_ready = sem("ret_O_ready")
        ln2 = sem("ret_ln2")
        rstd2_ready = sem("ret_rstd2")
        normed = sem("ret_normed")
        gained = sem("ret_gained")
        beta_added = sem("ret_beta_added")
        wy_ready = sem("ret_wy_ready")
        wy_transposed = sem("ret_wy_transposed")
        wyT_full_ready = sem("ret_wyT_full")
        wyT_ready = sem("ret_wyT_hi")
        wyT_lo_ready = sem("ret_wyT_lo")
        wo_done = sem("ret_wo_done")
        added = sem("ret_added")
        y = sb("ret_y", [128, 2, D])
        y_gained = sb("ret_y_gained", [128, 2, D])
        y_shaped = sb("ret_y_shaped", [128, 2, D])
        GROUP = 4
        with nc.Block() as block:
            @block.gpsimd
            def _(pool):
                pool.wait_ge(ln2, B + 7)
                nc.gpsimd.tensor_tensor(rstd[:], var_eps[:], minus_half[:], ALU.pow).then_inc(rstd2_ready, 1)

                def step(s, j):
                    if live(s):
                        pool.wait_ge(normed, s + 1)
                        nc.gpsimd.tensor_tensor(y_gained[:, j, :], y[:, j, :], gn[:, 0, :], ALU.mult).then_inc(gained, 1)
                        pool.wait_ge(gained, s + 1)
                        wait(pool, wy_ready, s - 1)
                        nc.gpsimd.tensor_tensor(y_shaped[:, j, :], y_gained[:, j, :], gn[:, 1, :], ALU.add).then_inc(beta_added, 1)
                run_pairs(pool, step, 0)

            @block.tensor
            def _(pe):
                for g in range(B // GROUP):
                    for h in range(H_):
                        wait(pe, O_ready, 2 * (g - 1) + h - 1)
                        nc.tensor.matmul(bank[2 * (g % 2) + h][:], AT[:, h, :], V[:, h, g * GROUP:(g + 1) * GROUP, :].rearrange("p b n -> p (b n)"),
                                         start=True, stop=True).then_inc(vproj, 1)

                def step(s, j):
                    if live(s):
                        pe.wait_ge(wy_ready, s + 1)
                        wait(pe, wyT_ready, s - 1)
                        for k in range(KD):
                            ins = nc.tensor.transpose(bank[4 + j][:, k * 128:(k + 1) * 128], xn[:, j, k * 128:(k + 1) * 128], ident[:])
                        ins.then_inc(wy_transposed, 1)
                    u, i = s - 1, 1 - j
                    if live(u):
                        pe.wait_ge(wyT_lo_ready, u + 1)
                        wait(pe, added, u - 1)
                        for k in range(KD):
                            ins = matmul3(nc, bank[6 + i][:, 0:D], (xT_hi[:, i, k, :], xT_lo[:, i, k, :]), (w_hi[:, 1, k, :], w_lo[:, 1, k, :]),
                                          first=(k == 0), last=(k == KD - 1))
                        ins.then_inc(wo_done, 1)
                run_pairs(pe, step, 1)

            @block.scalar
            def _(act):
                for g in range(B // GROUP):
                    for h in range(H_):
                        act.wait_ge(vproj, 2 * g + h + 1)
                        nc.scalar.activation(O[:, g * GROUP:(g + 1) * GROUP, h * 128:(h + 1) * 128],
                                             bank[2 * (g % 2) + h][:].rearrange("p (b n) -> p b n", b=GROUP), ACT.Copy).then_inc(O_ready, 1)

                def step(s, j):
                    if live(s):
                        act.wait_ge(wy_transposed, s + 1)
                        wait(act, wo_done, s - 1)
                        nc.scalar.activation(flat(xT_full[:, j]), bank[4 + j][:, 0:256], ACT.Copy).then_inc(wyT_full_ready, 1)
                        nc.scalar.activation(flat(xT_hi[:, j]), bank[4 + j][:, 0:256], ACT.Copy).then_inc(wyT_ready, 1)
                run_pairs(act, step, 0)

            @block.vector
            def _(dve):
                for g in range(B // GROUP):
                    dve.wait_ge(O_ready, 2 * g + 2)
                    for b in range(g * GROUP, (g + 1) * GROUP):
                        nc.vector.bn_stats(stats[:, b, :], O[:, b, :]).then_inc(ln2, 1)
                dve.wait_ge(ln2, B)
                n = finish_stats(nc, dve, ln2, B, stats, mean[:], var_eps[:], ln_tmp, 1e-3)
                dve.wait_ge(rstd2_ready, 1)
                dve.wait_ge(ln2, n)

                def norm(b, j):
                    wait(dve, beta_added, b - 1)
                    nc.vector.tensor_scalar(y[:, j, :], batch(O, b), one(mean, b), one(rstd, b), ALU.subtract, ALU.mult).then_inc(normed, 1)

                def apply_gate(b, j):
                    dve.wait_ge(beta_added, b + 1)
                    wait(dve, wy_transposed, b - 1)
                    nc.vector.tensor_tensor(xn[:, j, :], y_shaped[:, j, :], batch(gate, b), ALU.mult).then_inc(wy_ready, 1)

                norm(0, 0)
                norm(1, 1)
                apply_gate(0, 0)

                def step(s, j):
                    if live(s + 2):
                        norm(s + 2, j)
                    if live(s + 1):
                        apply_gate(s + 1, 1 - j)
                    if live(s):
                        dve.wait_ge(wyT_ready, s + 1)
                        nc.vector.tensor_tensor(flat(xT_lo[:, j]), flat(xT_full[:, j]), flat(xT_hi[:, j]).bitcast(F32), ALU.subtract).then_inc(wyT_lo_ready, 1)
                    if live(s - 1):
                        dve.wait_ge(wo_done, s)
                        nc.vector.tensor_tensor(batch(X, s - 1), bank[7 - j][:, 0:D], batch(X, s - 1), ALU.add).then_inc(added, 1)
                        dve.wait_ge(added, s)
                        nc.vector.bn_stats(batch(stats, s - 1), batch(X, s - 1))
                run_pairs(dve, step, 1)


def flat(ap):
    return ap.rearrange("p h n -> p (h n)")


def pair_count(s, j, i, ahead=-1):
    if ahead < 0:
        return (s - j) * 8 + (16 if i < j else 0)
    return (s - j) * 8 + (16 if j < i else 32)


def ctx_columns(a, b):
    view = a["ctxT"].rearrange("(k p) n -> p k n", p=128)
    return view[:, :, b * S:(b + 1) * S] if isinstance(b, int) else view[:, :, bass.ds(b * S, S)]

def phase_spline(nc, a, sem, sb_, bank, X, ident, mean, var_eps, rstd, minus_half, stats, ln_tmp, w, ahead_loaded, n_ahead):
    local = ExitStack()
    with local:
        def sb(name, shape, dt=F32):
            return sb_(name, shape, dt, local)

        NT, W, GRID, NC_ = 64, 4, 16, 8
        BIG = 1e30
        TABW = 2 * W * GRID + 1
        H = sb("sp_H", [128, B, D])
        XF = sb("sp_XF", [128, B, D])
        sign = sb("sp_sign", [128, B, D])
        wide = sb("sp_wide", [128, B, D])
        gb = w["sp_gb"]
        square = sb("sp_square", [128, B])
        rstd2 = sb("sp_rstd2", [128, B])
        rstd12 = sb("sp_rstd12", [128, B])
        slopes_in = w["sp_slopes"]
        slope_sum = sb("sp_slope_sum", [128, D])
        slope_neg = sb("sp_slope_neg", [128, D])
        slope_sign = sb("sp_slope_sign", [128, D])
        tile_score = sb("sp_tile_score", [128, B, NT])
        cluster_score = sb("sp_cluster_score", [128, B, NC_])
        rank = w["sp_rank"]
        best = sb("sp_best", [128, 2, B])
        cluster_hot = sb("sp_cluster_hot", [128, B, NC_])
        hot = sb("sp_hot", [128, B, NT])
        xs = sb("sp_xs", [128, B, W])
        lo_hi = sb("sp_lo_hi", [128, 2, B])
        off = sb("sp_off", [128, B, NT])
        extreme = sb("sp_extreme", [128, 2, B, NT])
        tile_ext = sb("sp_tile_ext", [128, 2, NT])
        table = w["sp_table"]
        ext_table = sb("sp_ext_table", [NT, 2])
        hotT = sb("sp_hotT", [NT, B, 128])
        ext_found = sb("sp_ext_found", [128, B, 2])
        found = sb("sp_found", [128, B, TABW])
        span = sb("sp_span", [128, 2, B])
        u = sb("sp_u", [128, B, W])
        ge = sb("sp_ge", [128, B * W, GRID + 1])
        cell = sb("sp_cell", [128, B, W, GRID])
        picked = sb("sp_picked", [128, 2, B, W, GRID])
        coef = sb("sp_coef", [128, 4, B, W])

        stat = sem("sp_stat")
        rstd_ready = sem("sp_rstd_ready")
        ext_ready = sem("sp_ext_ready")
        ext_transposed = sem("sp_ext_transposed")
        table_ready = sem("sp_table_ready")
        hot_ready = sem("sp_hot_ready")
        xf_ready = sem("sp_xf_ready")
        f_made = sem("sp_f_made")
        ext_found_ready = sem("sp_ext_found_ready")
        ext_looked_up = sem("sp_ext_looked_up")
        hot_transposed = sem("sp_hot_transposed")
        hotT_ready = sem("sp_hotT_ready")
        looked_up = sem("sp_looked_up")
        found_ready = sem("sp_found_ready")
        chain = sem("sp_chain")

        with nc.Block() as block:
            @block.gpsimd
            def _(pool):
                pool.wait_ge(stat, 7)
                nc.gpsimd.tensor_tensor(rstd[:], var_eps[:], minus_half[:], ALU.pow).then_inc(rstd_ready, 1)
                pool.wait_ge(stat, 7 + 3)
                nc.gpsimd.tensor_tensor(rstd2[:], var_eps[:], minus_half[:], ALU.pow).then_inc(rstd_ready, 1)
                per_batch = lambda ap: ap.rearrange("p (b n) -> p b n", n=1).broadcast_to([128, B, D])
                nc.gpsimd.tensor_tensor(H[:], X[:], per_batch(mean[:]), ALU.subtract).then_inc(f_made, 1)
                pool.wait_ge(f_made, 1)
                nc.gpsimd.tensor_tensor(H[:], H[:], per_batch(rstd[:]), ALU.mult).then_inc(f_made, 1)
                pool.wait_ge(f_made, 2)
                pool.wait_ge(xf_ready, B)
                nc.gpsimd.tensor_tensor(X[:], X[:], H[:], ALU.add).then_inc(f_made, 1)

            @block.vector
            def _(dve):
                count = [0]

                def link(ins):
                    count[0] += 1
                    ins.then_inc(chain, 1)
                    dve.wait_ge(chain, count[0])

                TT, TS, STT = nc.vector.tensor_tensor, nc.vector.tensor_scalar, nc.vector.scalar_tensor_tensor
                n = finish_stats(nc, dve, stat, 0, stats, mean[:], var_eps[:], ln_tmp, LN_EPS)
                dve.wait_ge(ahead_loaded, n_ahead)
                link(nc.vector.tensor_reduce(slope_sum[:], slopes_in[:], AX.X, ALU.add))
                link(TS(slope_neg[:], slope_sum[:], 0.0, None, ALU.is_lt))
                link(STT(slope_sign[:], slope_sum[:], 0.0, slope_neg[:], ALU.is_gt, ALU.subtract))
                dve.wait_ge(stat, n)
                dve.wait_ge(rstd_ready, 1)
                n = second_norm(nc, dve, stat, n, var_eps[:], rstd[:], square[:], ln_tmp, LN_EPS)
                dve.wait_ge(rstd_ready, 2)
                TT(rstd12[:], rstd[:], rstd2[:], ALU.mult).then_inc(stat, 1)
                dve.wait_ge(stat, n + 1)
                for b in range(B):
                    TS(XF[:, b, :], X[:, b, :], mean[:, b:b + 1], rstd12[:, b:b + 1], ALU.subtract, ALU.mult).then_inc(xf_ready, 1)
                dve.wait_ge(xf_ready, B)

                rows = lambda ap: ap.rearrange("p (a n) -> p a n", a=1).broadcast_to([128, B, D])
                link(TT(XF[:], XF[:], rows(gb[:, 0, :]), ALU.mult))
                link(TT(XF[:], XF[:], rows(gb[:, 1, :]), ALU.add))
                link(TS(wide[:], XF[:], 0.0, None, ALU.is_lt))
                link(STT(sign[:], XF[:], 0.0, wide[:], ALU.is_gt, ALU.subtract))
                link(TT(sign[:], sign[:], rows(slope_sign[:]), ALU.mult))
                link(nc.vector.tensor_reduce(tile_score[:], sign[:].rearrange("p b (t j) -> p b t j", j=W), AX.X, ALU.add))
                link(nc.vector.tensor_reduce(cluster_score[:], tile_score[:].rearrange("p b (c t) -> p b c t", t=8), AX.X, ALU.add))
                col = lambda lo, m: rank[:, lo:lo + m].rearrange("p (a n) -> p a n", a=1).broadcast_to([128, B, m])
                over = lambda ap, m: ap.rearrange("p (b n) -> p b n", n=1).broadcast_to([128, B, m])
                link(STT(cluster_score[:], cluster_score[:], float(NC_), col(NT, NC_), ALU.mult, ALU.add))
                link(nc.vector.tensor_reduce(best[:, 0, :], cluster_score[:], AX.X, ALU.max))
                link(TT(cluster_hot[:], cluster_score[:], over(best[:, 0, :], NC_), ALU.is_equal))
                link(STT(tile_score[:], tile_score[:], float(NT), col(0, NT), ALU.mult, ALU.add))
                link(TS(cluster_hot[:], cluster_hot[:], 4096.0, None, ALU.mult))
                link(TT(tile_score[:].rearrange("p b (c t) -> p (b c) t", t=8), tile_score[:].rearrange("p b (c t) -> p (b c) t", t=8),
                        cluster_hot[:].rearrange("p b (c a) -> p (b c) a", a=1).broadcast_to([128, B * NC_, 8]), ALU.add))
                link(nc.vector.tensor_reduce(best[:, 1, :], tile_score[:], AX.X, ALU.max))
                TT(hot[:], tile_score[:], over(best[:, 1, :], NT), ALU.is_equal).then_inc(hot_ready, 1)
                dve.wait_ge(hot_ready, 1)
                per_tile = lambda t: t[:].rearrange("p b (t j) -> p (b t) j", j=W)
                hot_wide = hot[:].rearrange("p b (t a) -> p (b t) a", a=1).broadcast_to([128, B * NT, W])
                link(TT(per_tile(wide), per_tile(XF), hot_wide, ALU.mult))
                link(nc.vector.tensor_reduce(xs[:], wide[:].rearrange("p b (t j) -> p b j t", j=W), AX.X, ALU.add))
                link(nc.vector.tensor_reduce(lo_hi[:, 0, :], xs[:], AX.X, ALU.min))
                link(nc.vector.tensor_reduce(lo_hi[:, 1, :], xs[:], AX.X, ALU.max))
                link(TS(off[:], hot[:], -BIG, BIG, ALU.mult, ALU.add))
                for i, sgn in ((0, ALU.add), (1, ALU.subtract)):
                    link(TT(extreme[:, i], hot[:], over(lo_hi[:, i, :], NT), ALU.mult))
                    link(TT(extreme[:, i], extreme[:, i], off[:], sgn))
                    link(nc.vector.tensor_reduce(tile_ext[:, i, :], extreme[:, i].rearrange("p b t -> p t b"), AX.X, (ALU.min, ALU.max)[i]))
                nc.vector.tensor_copy(tile_ext[:, 0, 0:1], tile_ext[:, 0, 0:1]).then_inc(ext_ready, 1)
                dve.wait_ge(ext_transposed, 1)
                for i in range(2):
                    nc.vector.tensor_reduce(ext_table[:, i:i + 1], bank[0][0:NT, i * 128:(i + 1) * 128], AX.X, (ALU.min, ALU.max)[i]).then_inc(table_ready, 1)
                dve.wait_ge(ext_looked_up, 1)
                nc.vector.tensor_copy(flat(ext_found[:]), bank[1][:, 0:2 * B]).then_inc(ext_found_ready, 1)
                dve.wait_ge(ext_found_ready, 1)
                dve.wait_ge(found_ready, B // 2)

                link(TT(span[:, 0, :], ext_found[:, :, 1], ext_found[:, :, 0], ALU.subtract))
                link(TS(span[:, 0, :], span[:, 0, :], 1e-8, None, ALU.add))
                link(nc.vector.reciprocal(span[:, 1, :], span[:, 0, :]))
                link(TT(u[:], xs[:], over(ext_found[:, :, 0], W), ALU.subtract))
                link(TT(u[:], u[:], over(span[:, 1, :], W), ALU.mult))
                link(TS(u[:], u[:], 0.0, float(np.float32(1.0 - 1e-6)), ALU.max, ALU.min))
                link(TS(u[:], u[:], float(GRID), None, ALU.mult))
                u_flat = u[:].rearrange("p b w -> p (b w)")
                link(TT(ge[:], u_flat.rearrange("p (n a) -> p n a", a=1).broadcast_to([128, B * W, GRID + 1]),
                        rank[:, NT + NC_:].rearrange("p (a g) -> p a g", a=1).broadcast_to([128, B * W, GRID + 1]), ALU.is_ge))
                cells = lambda ap: ap.rearrange("p b w g -> p (b w) g")
                link(TT(cells(cell[:]), ge[:, :, 0:GRID], ge[:, :, 1:GRID + 1], ALU.subtract))
                for i in range(2):
                    link(TT(picked[:, i], cell[:], found[:, :, 64 * i:64 * (i + 1)].rearrange("p b (w g) -> p b w g", w=W), ALU.mult))
                    link(nc.vector.tensor_reduce(coef[:, i], picked[:, i], AX.X, ALU.add))
                link(nc.vector.tensor_reduce(coef[:, 2].rearrange("p b w -> p (b w)"), ge[:, :, 1:GRID + 1], AX.X, ALU.add))
                link(TT(coef[:, 2], u[:], coef[:, 2], ALU.subtract))
                link(TT(coef[:, 2], coef[:, 2], coef[:, 1], ALU.mult))
                link(TT(coef[:, 2], coef[:, 2], coef[:, 0], ALU.add))
                link(TT(coef[:, 3], coef[:, 2], over(found[:, :, 128], W), ALU.mult))
                for j in range(W):
                    link(TT(wide[:].rearrange("p b (t j) -> p b t j", j=W)[:, :, :, j], hot[:], over(coef[:, 3, :, j], NT), ALU.mult))
                dve.wait_ge(f_made, 3)
                link(TT(X[:], X[:], wide[:], ALU.add))

            @block.tensor
            def _(pe):
                pe.wait_ge(hot_ready, 1)
                for g in range(4):
                    for b in range(4 * g, 4 * g + 4):
                        ins = nc.tensor.transpose(bank[1 + g][0:NT, b % 4 * 128:(b % 4 + 1) * 128], hot[:, b, :], ident[:])
                    ins.then_inc(hot_transposed, 1)
                for p in range(B // 2):
                    pe.wait_ge(hotT_ready, p // 2 + 1)
                    wait(pe, found_ready, p - 2)
                    for i in range(2):
                        ins = nc.tensor.matmul(bank[5 + p % 3][:, i * TABW:(i + 1) * TABW], hotT[:, 2 * p + i, :], table[:], start=True, stop=True)
                    ins.then_inc(looked_up, 1)
                pe.wait_ge(ext_ready, 1)
                for i in range(2):
                    ins = nc.tensor.transpose(bank[0][0:NT, i * 128:(i + 1) * 128], tile_ext[:, i, :], ident[:])
                ins.then_inc(ext_transposed, 1)
                pe.wait_ge(table_ready, 2)
                for b in range(B):
                    ins = nc.tensor.matmul(bank[1][:, 2 * b:2 * b + 2], hotT[:, b, :], ext_table[:], start=True, stop=True)
                ins.then_inc(ext_looked_up, 1)

            @block.scalar
            def _(act):
                for g in range(4):
                    act.wait_ge(hot_transposed, g + 1)
                    nc.scalar.activation(flat(hotT[:, 4 * g:4 * g + 4, :]), bank[1 + g][0:NT, :], ACT.Copy).then_inc(hotT_ready, 1)
                for p in range(B // 2):
                    act.wait_ge(looked_up, p + 1)
                    nc.scalar.activation(flat(found[:, 2 * p:2 * p + 2, :]), bank[5 + p % 3][:, 0:2 * TABW], ACT.Copy).then_inc(found_ready, 1)


def phase_window(nc, a, sem, sb_, bank, X, ident, mean, var_eps, rstd, minus_half, stats, ln_tmp, w, ahead_loaded, n_ahead):
    local = ExitStack()
    with local:
        def sb(name, shape, dt=F32):
            return sb_(name, shape, dt, local)

        NH, DH, VW = 16, 16, 17
        wqk = w["win_wqk"]
        w_in = w["win_w_in"]
        w_hi = sb("win_w_hi", [128, 2, KD, D], F32R)
        w_lo = sb("win_w_lo", [128, 2, KD, D], F32R)
        band_f = w["win_band_in"]
        band = sb("win_band", [128, 4, 128], BF16)
        ident_b = sb("win_ident_b", [128, 128], BF16)
        parity = w["win_parity"]
        xn = sb("win_xn", [128, 2, D])
        xT_full = sb("win_xT_full", [128, KD, 128])
        xT_hi = sb("win_xT_hi", [128, KD, 128], F32R)
        xT_lo = sb("win_xT_lo", [128, KD, 128], F32R)
        qT = sb("win_qT", [128, 2, KD, 128])
        k_of = sb("win_k_of", [128, 2, KD, 2, 128])
        V = sb("win_V", [128, 2, NH, VW])
        P = sb("win_P", [128, 2, 4, 128])
        PT = sb("win_PT", [128, 2, 4, 128])
        neg_max = sb("win_neg_max", [128, 4, 4])
        inv = sb("win_inv", [128, 2, NH])
        o = sb("win_o", [128, 2, D])
        oT_hi = sb("win_oT_hi", [128, KD, 128], F32R)
        oT_lo = sb("win_oT_lo", [128, KD, 128], F32R)
        oT_full = sb("win_oT_full", [128, KD, 128])

        made = sem("win_made")
        w_rounded = sem("win_w_rounded")
        ln = sem("win_ln")
        rstd_ready = sem("win_rstd_ready")
        xn_ready = sem("win_xn_ready")
        x_transposed = sem("win_x_transposed")
        xT_full_ready = sem("win_xT_full_ready")
        xT_hi_ready = sem("win_xT_hi_ready")
        xT_lo_ready = sem("win_xT_lo_ready")
        qk_projected = sem("win_qk_projected")
        v_projected = sem("win_v_projected")
        qk_ready = sem("win_qk_ready")
        V_ready = sem("win_V_ready")
        scored = sem("win_scored")
        max_found = sem("win_max_found")
        exps_done = sem("win_exps_done")
        p_transposed = sem("win_p_transposed")
        PT_ready = sem("win_PT_ready")
        weighed = sem("win_weighed")
        inv_ready = sem("win_inv_ready")
        o_ready = sem("win_o_ready")
        o_transposed = sem("win_o_transposed")
        oT_full_ready = sem("win_oT_full_ready")
        oT_hi_ready = sem("win_oT_hi_ready")
        oT_lo_ready = sem("win_oT_lo_ready")
        out_projected = sem("win_out_projected")
        added = sem("win_added")

        QK, SC, PTB, OB, VB, MISC = bank[0], (bank[1], bank[2]), (bank[3], bank[4]), bank[5], bank[6], bank[7]
        STEPS = B * 4

        with nc.Block() as block:
            @block.gpsimd
            def _(pool):
                pool.wait_ge(ln, B + 7)
                nc.gpsimd.tensor_tensor(rstd[:], var_eps[:], minus_half[:], ALU.pow).then_inc(rstd_ready, 1)

            def run(eng, step, extra, first=None):
                for q in range(4):
                    step(q, q, 0, 0)
                for q in range(4):
                    step(4 + q, q, 1, 1)
                with eng.Fori(1, B // 2 - 1) as i:
                    for j in range(2):
                        for q in range(4):
                            step(i * 8 + 4 * j + q, q, i * 2 + j, j)
                for b in (B - 2, B - 1):
                    for q in range(4):
                        step(4 * b + q, q, b, b % 2)
                for x in range(extra):
                    step(STEPS + x, x % 4, B + x // 4, x // 4 % 2)

            @block.scalar
            def _(act):
                act.wait_ge(ahead_loaded, n_ahead)
                nc.scalar.activation(w_hi[:], w_in[:], ACT.Copy).then_inc(w_rounded, 1)

                def take_xT(b):
                    act.wait_ge(x_transposed, b + 1)
                    wait(act, v_projected, b)
                    nc.scalar.activation(flat(xT_full[:]), VB[:, D:2 * D], ACT.Copy).then_inc(xT_full_ready, 1)
                    nc.scalar.activation(flat(xT_hi[:]), VB[:, D:2 * D], ACT.Copy).then_inc(xT_hi_ready, 1)

                def take_qk(b, j):
                    act.wait_ge(qk_projected, b + 1)
                    wait(act, scored, 4 * b - 4)
                    nc.scalar.activation(flat(qT[:, j]), QK[:, 0:D], ACT.Copy, scale=1.0 / DH ** 0.5).then_inc(qk_ready, 1)
                    for par in range(2):
                        nc.scalar.activation(k_of[:, j, :, par, :], QK[:, D:2 * D].rearrange("p (k n) -> p k n", k=KD), ACT.Copy,
                                             scale=parity[:, par:par + 1]).then_inc(qk_ready, 1)

                def take_v(b, j):
                    act.wait_ge(v_projected, b + 1)
                    wait(act, weighed, 4 * b - 4)
                    nc.scalar.activation(V[:, j, :, 0:DH], VB[:, 0:D].rearrange("p (h n) -> p h n", h=NH), ACT.Copy).then_inc(V_ready, 1)

                def exps(t, q):
                    act.wait_ge(max_found, t + 1)
                    wait(act, p_transposed, t - 1)
                    for h in range(4):
                        ins = nc.scalar.activation(P[:, q % 2, h, :], SC[q % 2][:, h * 128:(h + 1) * 128], ACT.Exp, bias=neg_max[:, q, h:h + 1])
                    ins.then_inc(exps_done, 1)

                def take_oT(b):
                    act.wait_ge(o_transposed, b + 1)
                    wait(act, out_projected, b)
                    nc.scalar.activation(flat(oT_full[:]), MISC[:, D:2 * D], ACT.Copy).then_inc(oT_full_ready, 1)
                    nc.scalar.activation(flat(oT_hi[:]), MISC[:, D:2 * D], ACT.Copy).then_inc(oT_hi_ready, 1)

                take_xT(0)
                take_qk(0, 0)
                take_v(0, 0)

                def step(t, q, b, j):
                    if q == 0 and live(b - 2):
                        take_oT(b - 2)
                    if q == 1 and live(b + 1):
                        take_xT(b + 1)
                    if q == 2 and live(b + 1):
                        take_qk(b + 1, 1 - j)
                    if q == 3 and live(b + 1):
                        take_v(b + 1, 1 - j)
                    if live(t, STEPS):
                        exps(t, q)
                run(act, step, 5)

            @block.vector
            def _(dve):
                with dve.Fori(0, B) as b:
                    nc.vector.bn_stats(batch(stats, b), batch(X, b)).then_inc(ln, 1)
                dve.wait_ge(ln, B)
                n = finish_stats(nc, dve, ln, B, stats, mean[:], var_eps[:], ln_tmp, LN_EPS)
                dve.wait_ge(ahead_loaded, n_ahead)
                for h in range(4):
                    nc.vector.tensor_copy(band[:, h, :], band_f[:]).then_inc(made, 1)
                nc.vector.tensor_copy(ident_b[:], ident[:]).then_inc(made, 1)
                nc.vector.memset(V[:], 1.0).then_inc(made, 1)
                dve.wait_ge(w_rounded, 1)
                nc.vector.tensor_tensor(w_lo[:], w_in[:], w_hi[:].bitcast(F32), ALU.subtract).then_inc(made, 1)
                dve.wait_ge(ln, n)
                dve.wait_ge(rstd_ready, 1)

                def normalise(b, j):
                    wait(dve, x_transposed, b - 1)
                    nc.vector.tensor_scalar(xn[:, j, :], batch(X, b), one(mean, b), one(rstd, b), ALU.subtract, ALU.mult).then_inc(xn_ready, 1)

                def split_xT(b):
                    dve.wait_ge(xT_hi_ready, b + 1)
                    nc.vector.tensor_tensor(flat(xT_lo[:]), flat(xT_full[:]), flat(xT_hi[:]).bitcast(F32), ALU.subtract).then_inc(xT_lo_ready, 1)

                def find_max(t, q):
                    dve.wait_ge(scored, t + 1)
                    nc.vector.tensor_reduce(neg_max[:, q, :], SC[q % 2][:].rearrange("p (h n) -> p h n", h=4), AX.X, ALU.max, negate=True).then_inc(max_found, 1)

                def take_PT(t, q):
                    dve.wait_ge(p_transposed, t + 1)
                    wait(dve, weighed, t - 1)
                    nc.vector.tensor_copy(flat(PT[:, q % 2]), PTB[q % 2][:]).then_inc(PT_ready, 1)

                def norm_out(b, j):
                    dve.wait_ge(weighed, 4 * b + 4)
                    heads = OB[:, 0:NH * VW].rearrange("p (h n) -> p h n", h=NH)
                    nc.vector.reciprocal(inv[:, j, :], heads[:, :, DH]).then_inc(inv_ready, 1)
                    dve.wait_ge(inv_ready, b + 1)
                    wait(dve, o_transposed, b - 1)
                    nc.vector.tensor_tensor(o[:, j, :].rearrange("p (h n) -> p h n", h=NH), heads[:, :, 0:DH],
                                            inv[:, j, :].rearrange("p (h n) -> p h n", n=1).broadcast_to([128, NH, DH]), ALU.mult).then_inc(o_ready, 1)

                def split_oT(b):
                    dve.wait_ge(oT_hi_ready, b + 1)
                    nc.vector.tensor_tensor(flat(oT_lo[:]), flat(oT_full[:]), flat(oT_hi[:]).bitcast(F32), ALU.subtract).then_inc(oT_lo_ready, 1)

                def add_out(b):
                    dve.wait_ge(out_projected, b + 1)
                    nc.vector.tensor_tensor(batch(X, b), MISC[:, 0:D], batch(X, b), ALU.add).then_inc(added, 1)
                    dve.wait_ge(added, b + 1)
                    nc.vector.bn_stats(batch(stats, b), batch(X, b))

                normalise(0, 0)
                split_xT(0)
                normalise(1, 1)

                def step(t, q, b, j):
                    if live(t, STEPS):
                        find_max(t, q)
                    if q == 0 and live(b - 2):
                        split_oT(b - 2)
                    if q == 2 and live(b - 1):
                        norm_out(b - 1, 1 - j)
                    if live(t - 2, STEPS):
                        take_PT(t - 2, (q + 2) % 4)
                    if q == 1 and live(b + 1):
                        split_xT(b + 1)
                    if q == 2 and live(b + 2):
                        normalise(b + 2, j)
                    if q == 1 and live(b - 2):
                        add_out(b - 2)
                run(dve, step, 8)

            @block.tensor
            def _(pe):
                def transpose_x(b, j):
                    pe.wait_ge(xn_ready, b + 1)
                    wait(pe, V_ready, b)
                    for k in range(KD):
                        ins = nc.tensor.transpose(VB[:, D + k * 128:D + (k + 1) * 128], xn[:, j, k * 128:(k + 1) * 128], ident[:])
                    ins.then_inc(x_transposed, 1)

                def project_qk(b):
                    pe.wait_ge(xT_full_ready, b + 1)
                    wait(pe, qk_ready, 3 * b)
                    for c in range(4):
                        for k in range(KD):
                            ins = nc.tensor.matmul(QK[:, c * 128:(c + 1) * 128], wqk[:, k, c * 128:(c + 1) * 128], xT_full[:, k, :],
                                                   start=(k == 0), stop=(k == KD - 1))
                    ins.then_inc(qk_projected, 1)

                def project_v(b):
                    pe.wait_ge(xT_lo_ready, b + 1)
                    wait(pe, V_ready, b)
                    for k in range(KD):
                        ins = matmul3(nc, VB[:, 0:D], (xT_hi[:, k, :], xT_lo[:, k, :]), (w_hi[:, 0, k, :], w_lo[:, 0, k, :]),
                                      first=(k == 0), last=(k == KD - 1))
                    ins.then_inc(v_projected, 1)

                def score(t, q, b, j):
                    if q == 0:
                        pe.wait_ge(qk_ready, 3 * b + 3)
                    wait(pe, exps_done, t - 1)
                    dst = SC[q % 2]
                    nc.tensor.matmul(dst[:], ident_b[:], flat(band[:]), start=True, stop=True)
                    for pair in range(2):
                        rows = slice(32 * q, 32 * q + 32)
                        ins = nc.tensor.matmul(dst[:, pair * 256:(pair + 1) * 256], qT[rows, j, pair, :], k_of[rows, j, pair, :, :].rearrange("p a n -> p (a n)"),
                                               start=False, stop=True, skip_group_check=True)
                    ins.then_inc(scored, 1)

                def transpose_p(t, q):
                    pe.wait_ge(exps_done, t + 1)
                    wait(pe, PT_ready, t - 1)
                    for h in range(4):
                        ins = nc.tensor.transpose(PTB[q % 2][:, h * 128:(h + 1) * 128], P[:, q % 2, h, :], ident[:])
                    ins.then_inc(p_transposed, 1)

                def weigh(t, q, b, j):
                    pe.wait_ge(PT_ready, t + 1)
                    if q == 0:
                        pe.wait_ge(V_ready, b + 1)
                        wait(pe, o_ready, b)
                    for h in range(4):
                        head = 8 * (h // 2) + 2 * q + h % 2
                        ins = nc.tensor.matmul(OB[:, head * VW:(head + 1) * VW], PT[:, q % 2, h, :], V[:, j, head, :], start=True, stop=True)
                    ins.then_inc(weighed, 1)

                def transpose_o(b, j):
                    pe.wait_ge(o_ready, b + 1)
                    wait(pe, oT_hi_ready, b)
                    wait(pe, added, b)
                    for k in range(KD):
                        ins = nc.tensor.transpose(MISC[:, D + k * 128:D + (k + 1) * 128], o[:, j, k * 128:(k + 1) * 128], ident[:])
                    ins.then_inc(o_transposed, 1)

                def project_out(b):
                    pe.wait_ge(oT_lo_ready, b + 1)
                    for k in range(KD):
                        ins = matmul3(nc, MISC[:, 0:D], (oT_hi[:, k, :], oT_lo[:, k, :]), (w_hi[:, 1, k, :], w_lo[:, 1, k, :]),
                                      first=(k == 0), last=(k == KD - 1))
                    ins.then_inc(out_projected, 1)

                pe.wait_ge(ahead_loaded, n_ahead)
                transpose_x(0, 0)
                project_qk(0)
                pe.wait_ge(made, 7)
                project_v(0)

                def step(t, q, b, j):
                    if live(t, STEPS):
                        score(t, q, b, j)
                    if live(t - 3, STEPS):
                        weigh(t - 3, (q + 1) % 4, b if q == 3 else b - 1, j if q == 3 else 1 - j)
                    if live(t - 2, STEPS):
                        transpose_p(t - 2, (q + 2) % 4)
                    if q == 0:
                        if live(b + 1):
                            transpose_x(b + 1, 1 - j)
                        if live(b - 2):
                            project_out(b - 2)
                    if q == 1 and live(b + 1):
                        project_qk(b + 1)
                    if q == 2 and live(b + 1):
                        project_v(b + 1)
                    if q == 3 and live(b - 1):
                        transpose_o(b - 1, 1 - j)
                run(pe, step, 8)

def phase_cross(nc, a, sem, sb_, bank, X, ident, mean, var_eps, rstd, minus_half, stats, ln_tmp, w):
    local = ExitStack()
    with local:
        def sb(name, shape, dt=F32):
            return sb_(name, shape, dt, local)

        wqk = w["cr_wqk"]
        w_in = w["cr_w_in"]
        w_hi = sb("cr_w_hi", [128, 2, KD, D], F32R)
        w_lo = sb("cr_w_lo", [128, 2, KD, D], F32R)
        xn = sb("cr_xn", [128, 2, D])
        xT_full = sb("cr_xT_full", [128, 2, KD, 128])
        xT_hi = sb("cr_xT_hi", [128, 2, KD, 128], F32R)
        xT_lo = sb("cr_xT_lo", [128, 2, KD, 128], F32R)
        qT = sb("cr_qT", [128, KD, 128])
        kT = sb("cr_kT", [128, 2, KD, 2, 128])
        V = sb("cr_V", [128, 2, 2, D])
        P = sb("cr_P", [128, 2, 128])
        PT = sb("cr_PT", [128, 2, 128])
        oT_full = sb("cr_oT_full", [128, KD, 128])
        oT_hi = sb("cr_oT_hi", [128, KD, 128], F32R)
        oT_lo = sb("cr_oT_lo", [128, KD, 128], F32R)
        neg_max = sb("cr_neg_max", [128, 2])
        exp_sum = sb("cr_exp_sum", [128, 2])
        inv_sum = sb("cr_inv_sum", [128, 2])

        ctx_loaded = [sem("cr_ctx0"), sem("cr_ctx1")]
        w_rounded = sem("cr_w_rounded")
        w_split = sem("cr_w_split")
        ln = sem("cr_ln")
        rstd_ready = sem("cr_rstd_ready")
        xn_ready = sem("cr_xn_ready")
        x_transposed = sem("cr_x_transposed")
        xT_full_ready = sem("cr_xT_full_ready")
        xT_hi_ready = sem("cr_xT_hi_ready")
        xT_lo_ready = sem("cr_xT_lo_ready")
        qk_projected = sem("cr_qk_projected")
        qk_ready = sem("cr_qk_ready")
        v_projected = sem("cr_v_projected")
        V_ready = sem("cr_V_ready")
        scored = sem("cr_scored")
        max_found = sem("cr_max_found")
        exps_done = sem("cr_exps_done")
        inv_ready = sem("cr_inv_ready")
        probs_ready = sem("cr_probs_ready")
        p_transposed = sem("cr_p_transposed")
        PT_ready = sem("cr_PT_ready")
        weighed = sem("cr_weighed")
        oT_full_ready = sem("cr_oT_full_ready")
        oT_hi_ready = sem("cr_oT_hi_ready")
        oT_lo_ready = sem("cr_oT_lo_ready")
        out_projected = sem("cr_out_projected")
        added = sem("cr_added")
        XB, QKB, VB, PB, OB, SB_, OUT, _ = bank

        with nc.Block() as block:
            @block.sync
            def _(sp):
                def step(s, j):
                    if live(s):
                        wait(sp, weighed, s - 1)
                        sp.dma_start(kT[:, j, :, 0, :], ctx_columns(a, s)).then_inc(ctx_loaded[j], 16)
                        rows = a["ctx_2048"][s] if isinstance(s, int) else a["ctx_2048"][bass.ds(s, 1)].rearrange("a t d -> (a t) d")
                        sp.dma_start(V[:, j, 0, :], rows).then_inc(ctx_loaded[j], 16)
                run_pairs(sp, step, 0)

            @block.gpsimd
            def _(pool):
                pool.wait_ge(ln, 7)
                nc.gpsimd.tensor_tensor(rstd[:], var_eps[:], minus_half[:], ALU.pow).then_inc(rstd_ready, 1)

            @block.scalar
            def _(act):
                nc.scalar.activation(w_hi[:], w_in[:], ACT.Copy).then_inc(w_rounded, 1)

                def step(s, j):
                    u = s - 2
                    if live(u):
                        act.wait_ge(max_found, u + 1)
                        wait(act, p_transposed, u)
                        nc.scalar.activation(flat(P[:]), SB_[:, 0:2 * 128], ACT.Exp, bias=neg_max[:, j:j + 1], accum_out=exp_sum[:, j:j + 1]).then_inc(exps_done, 1)
                    if live(s):
                        act.wait_ge(x_transposed, s + 1)
                        wait(act, v_projected, s - 1)
                        nc.scalar.activation(flat(xT_full[:, j]), XB[:, 0:D], ACT.Copy).then_inc(xT_full_ready, 1)
                        nc.scalar.activation(flat(xT_hi[:, j]), XB[:, 0:D], ACT.Copy).then_inc(xT_hi_ready, 1)
                    u, i = s - 1, 1 - j
                    if live(u):
                        act.wait_ge(qk_projected, u + 1)
                        wait(act, scored, u)
                        nc.scalar.activation(flat(qT[:]), QKB[:, 0:D], ACT.Copy, scale=1.0 / D ** 0.5).then_inc(qk_ready, 1)
                        nc.scalar.activation(kT[:, i, :, 1, :], QKB[:, D:2 * D].rearrange("p (k n) -> p k n", k=KD), ACT.Copy).then_inc(qk_ready, 1)
                    u = s - 2
                    if live(u):
                        act.wait_ge(p_transposed, u + 1)
                        wait(act, weighed, u)
                        nc.scalar.activation(flat(PT[:]), PB[:, 0:2 * 128], ACT.Copy).then_inc(PT_ready, 1)
                    u, i = s - 1, 1 - j
                    if live(u):
                        act.wait_ge(v_projected, u + 1)
                        wait(act, weighed, u - 1)
                        nc.scalar.activation(V[:, i, 1, :], VB[:, 0:D], ACT.Copy).then_inc(V_ready, 1)
                    u = s - 2
                    if live(u):
                        act.wait_ge(weighed, u + 1)
                        wait(act, out_projected, u)
                        nc.scalar.activation(flat(oT_full[:]), OB[:, 0:D], ACT.Copy).then_inc(oT_full_ready, 1)
                        nc.scalar.activation(flat(oT_hi[:]), OB[:, 0:D], ACT.Copy).then_inc(oT_hi_ready, 1)
                run_pairs(act, step, 2)

            @block.vector
            def _(dve):
                n = finish_stats(nc, dve, ln, 0, stats, mean[:], var_eps[:], ln_tmp, LN_EPS)
                dve.wait_ge(w_rounded, 1)
                nc.vector.tensor_tensor(w_lo[:], w_in[:], w_hi[:].bitcast(F32), ALU.subtract).then_inc(w_split, 1)
                dve.wait_ge(ln, n)
                dve.wait_ge(rstd_ready, 1)

                def normalise(b, j):
                    wait(dve, x_transposed, b - 1)
                    nc.vector.tensor_scalar(xn[:, j, :], batch(X, b), one(mean, b), one(rstd, b), ALU.subtract, ALU.mult).then_inc(xn_ready, 1)

                normalise(0, 0)

                def step(s, j):
                    u = s - 2
                    if live(u):
                        dve.wait_ge(scored, u + 1)
                        nc.vector.tensor_reduce(neg_max[:, j:j + 1], SB_[:, 0:2 * 128], AX.X, ALU.max, negate=True).then_inc(max_found, 1)
                        dve.wait_ge(exps_done, u + 1)
                        nc.vector.reciprocal(inv_sum[:, j:j + 1], exp_sum[:, j:j + 1]).then_inc(inv_ready, 1)
                        dve.wait_ge(inv_ready, u + 1)
                        nc.vector.tensor_scalar(flat(P[:]), flat(P[:]), inv_sum[:, j:j + 1], None, ALU.mult).then_inc(probs_ready, 1)
                    if live(s):
                        dve.wait_ge(xT_hi_ready, s + 1)
                        nc.vector.tensor_tensor(flat(xT_lo[:, j]), flat(xT_full[:, j]), flat(xT_hi[:, j]).bitcast(F32), ALU.subtract).then_inc(xT_lo_ready, 1)
                    u = s - 3
                    if live(u):
                        dve.wait_ge(out_projected, u + 1)
                        nc.vector.tensor_tensor(batch(X, u), OUT[:, 0:D], batch(X, u), ALU.add).then_inc(added, 1)
                        dve.wait_ge(added, u + 1)
                        nc.vector.bn_stats(batch(stats, u), batch(X, u))
                    u = s - 2
                    if live(u):
                        dve.wait_ge(oT_hi_ready, u + 1)
                        nc.vector.tensor_tensor(flat(oT_lo[:]), flat(oT_full[:]), flat(oT_hi[:]).bitcast(F32), ALU.subtract).then_inc(oT_lo_ready, 1)
                    if live(s + 1):
                        normalise(s + 1, 1 - j)
                run_pairs(dve, step, 3, peeled=2)

            @block.tensor
            def _(pe):
                def step(s, j):
                    if live(s):
                        pe.wait_ge(xn_ready, s + 1)
                        wait(pe, xT_hi_ready, s)
                        for k in range(KD):
                            ins = nc.tensor.transpose(XB[:, k * 128:(k + 1) * 128], xn[:, j, k * 128:(k + 1) * 128], ident[:])
                        ins.then_inc(x_transposed, 1)
                    u, i = s - 1, 1 - j
                    if live(u):
                        pe.wait_ge(xT_full_ready, u + 1)
                        wait(pe, qk_ready, 2 * u)
                        for w in range(2):
                            for c in range(KD):
                                for k in range(KD):
                                    ins = nc.tensor.matmul(QKB[:, (2 * w + c) * 128:(2 * w + c + 1) * 128], wqk[:, w, k, c * 128:(c + 1) * 128], xT_full[:, i, k, :],
                                                           start=(k == 0), stop=(k == KD - 1))
                        ins.then_inc(qk_projected, 1)
                    u = s - 3
                    if live(u):
                        pe.wait_ge(oT_lo_ready, u + 1)
                        wait(pe, added, u)
                        for k in range(KD):
                            ins = matmul3(nc, OUT[:, 0:D], (oT_hi[:, k, :], oT_lo[:, k, :]), (w_hi[:, 1, k, :], w_lo[:, 1, k, :]),
                                          first=(k == 0), last=(k == KD - 1))
                        ins.then_inc(out_projected, 1)
                    u = s - 2
                    if live(u):
                        pe.wait_ge(probs_ready, u + 1)
                        wait(pe, PT_ready, u)
                        for c in range(2):
                            ins = nc.tensor.transpose(PB[:, c * 128:(c + 1) * 128], P[:, c, :], ident[:])
                        ins.then_inc(p_transposed, 1)
                    u, i = s - 1, 1 - j
                    if live(u):
                        if isinstance(u, int) and u == 0:
                            pe.wait_ge(w_split, 1)
                        pe.wait_ge(xT_lo_ready, u + 1)
                        wait(pe, V_ready, u)
                        for k in range(KD):
                            ins = matmul3(nc, VB[:, 0:D], (xT_hi[:, i, k, :], xT_lo[:, i, k, :]), (w_hi[:, 0, k, :], w_lo[:, 0, k, :]),
                                          first=(k == 0), last=(k == KD - 1))
                        ins.then_inc(v_projected, 1)
                    u = s - 2
                    if live(u):
                        pe.wait_ge(PT_ready, u + 1)
                        pe.wait_ge(V_ready, u + 1)
                        wait(pe, oT_hi_ready, u)
                        for c in range(KD):
                            for k in range(2):
                                ins = nc.tensor.matmul(OB[:, c * 128:(c + 1) * 128], V[:, j, k, c * 128:(c + 1) * 128], PT[:, k, :],
                                                       start=(k == 0), stop=(k == 1))
                        ins.then_inc(weighed, 1)
                    u, i = s - 1, 1 - j
                    if live(u):
                        pe.wait_ge(qk_ready, 2 * u + 2)
                        pe.wait_ge(ctx_loaded[i], 32 * (u // 2 + 1) if isinstance(u, int) else pair_count(s, j, i) * 2)
                        wait(pe, exps_done, u)
                        for c in range(KD):
                            ins = nc.tensor.matmul(SB_[:, 0:2 * 128], qT[:, c, :], kT[:, i, c, :, :].rearrange("p a n -> p (a n)"),
                                                   start=(c == 0), stop=(c == KD - 1))
                        ins.then_inc(scored, 1)
                run_pairs(pe, step, 3, peeled=2)


def phase_moe(nc, a, sem, sb_, bank, X, ident, mean, var_eps, rstd, minus_half, stats, ln_tmp, w, out):
    local = ExitStack()
    with local:
        def sb(name, shape, dt=F32):
            return sb_(name, shape, dt, local)

        E_, LAT, HID, GROUP = 16, 64, 128, 4
        GW = GROUP * S
        NG = B // GROUP
        XT_hi = sb("moe_XT_hi", [128, KD, B * S], F32R)
        XT_lo = sb("moe_XT_lo", [128, KD, B * S], F32R)
        XL = sb("moe_XL", [128, B * S], F32R)
        logits = sb("moe_logits", [128, B, E_])
        gates = sb("moe_gates", [128, B, E_])
        ranked = sb("moe_ranked", [128, B, E_])
        cut = sb("moe_cut", [128, B, E_])
        top = sb("moe_top", [128, B, 8])
        gate_sum = sb("moe_gate_sum", [128, 2, B])
        route_bias = w["moe_route_bias"]
        wg = w["moe_wg"]
        w_in = w["moe_w_in"]
        w_hi = sb("moe_w_hi", [128, 3, KD, 128], F32R)
        w_lo = sb("moe_w_lo", [128, 3, KD, 128], F32R)
        sw2_in = w["moe_sw2"]
        sw2_hi = sb("moe_sw2_hi", [128, D], F32R)
        sw2_lo = sb("moe_sw2_lo", [128, D], F32R)
        wup = w["moe_wup"]
        we2 = w["moe_we2"]
        low_rows = w["moe_low_rows"]
        xn = sb("moe_xn", [128, 2, D])
        xT = sb("moe_xT", [128, 2, KD, 128])
        lat_hi = sb("moe_lat_hi", [128, GW], F32R)
        acc = sb("moe_acc", [128, B, LAT])
        relu = sb("moe_relu", [128, 2, GW])
        prod = sb("moe_prod", [128, 2, GW])
        hidden = sb("moe_hidden", [128, 2, GW])
        y_hi = sb("moe_y_hi", [128, GW], F32R)
        y_lo = sb("moe_y_lo", [128, GW], F32R)

        w_rounded = sem("moe_w_rounded")
        w_split = sem("moe_w_split")
        ln = sem("moe_ln")
        rstd_ready = sem("moe_rstd_ready")
        xn_ready = sem("moe_xn_ready")
        x_transposed = sem("moe_x_transposed")
        xT_ready = sem("moe_xT_ready")
        XT_split = sem("moe_XT_split")
        routed = sem("moe_routed")
        logits_ready = sem("moe_logits_ready")
        chain = sem("moe_chain")
        exp_ready = sem("moe_exp_ready")
        lat_projected = sem("moe_lat_projected")
        lat_rounded = sem("moe_lat_rounded")
        XL_ready = sem("moe_XL_ready")
        up_done = sem("moe_up_done")
        sh_relu = sem("moe_sh_relu")
        sh_prod = sem("moe_sh_prod")
        y_rounded = sem("moe_y_rounded")
        y_split = sem("moe_y_split")
        sh_out = sem("moe_sh_out")
        sh_added = sem("moe_sh_added")

        with nc.Block() as block:
            @block.gpsimd
            def _(pool):
                pool.wait_ge(ln, 7)
                nc.gpsimd.tensor_tensor(rstd[:], var_eps[:], minus_half[:], ALU.pow).then_inc(rstd_ready, 1)
                nc.gpsimd.memset(acc[:], 0.0)

            @block.scalar
            def _(act):
                nc.scalar.activation(w_hi[:], w_in[:], ACT.Copy).then_inc(w_rounded, 1)
                nc.scalar.activation(sw2_hi[:], sw2_in[:], ACT.Copy).then_inc(w_rounded, 1)

                def step(s, j):
                    if live(s):
                        act.wait_ge(x_transposed, s + 1)
                        wait(act, routed, s - 1)
                        wait(act, XT_split, 2 * s - 2)
                        nc.scalar.activation(flat(xT[:, j]), bank[j][:, 0:D], ACT.Copy).then_inc(xT_ready, 1)
                run_pairs(act, step, 0)
                act.wait_ge(logits_ready, B)
                nc.scalar.activation(flat(gates[:]), flat(logits[:]), ACT.Exp, scale=-1.0).then_inc(exp_ready, 1)
                for g in range(NG):
                    act.wait_ge(lat_projected, g + 1)
                    wait(act, XL_ready, g)
                    nc.scalar.activation(lat_hi[:], bank[0][:], ACT.Copy).then_inc(lat_rounded, 1)
                    act.wait_ge(up_done, g + 1)
                    wait(act, sh_prod, 2 * g)
                    nc.scalar.activation(relu[:, 0, :], bank[2][:], ACT.Relu).then_inc(sh_relu, 1)
                    act.wait_ge(sh_prod, 2 * g + 2)
                    wait(act, sh_out, g)
                    nc.scalar.activation(y_hi[:], hidden[:, 0, :], ACT.Copy).then_inc(y_rounded, 1)

            @block.vector
            def _(dve):
                count = [0]

                def link(ins):
                    count[0] += 1
                    ins.then_inc(chain, 1)
                    dve.wait_ge(chain, count[0])

                TT, TS = nc.vector.tensor_tensor, nc.vector.tensor_scalar
                n = finish_stats(nc, dve, ln, 0, stats, mean[:], var_eps[:], ln_tmp, LN_EPS)
                dve.wait_ge(w_rounded, 2)
                TT(w_lo[:], w_in[:], w_hi[:].bitcast(F32), ALU.subtract).then_inc(w_split, 1)
                TT(sw2_lo[:], sw2_in[:], sw2_hi[:].bitcast(F32), ALU.subtract).then_inc(w_split, 1)
                dve.wait_ge(ln, n)
                dve.wait_ge(rstd_ready, 1)

                def normalise(b, j):
                    wait(dve, x_transposed, b - 1)
                    TS(xn[:, j, :], batch(X, b), one(mean, b), one(rstd, b), ALU.subtract, ALU.mult).then_inc(xn_ready, 1)

                normalise(0, 0)

                def step(s, j):
                    if live(s + 1):
                        normalise(s + 1, 1 - j)
                    if live(s):
                        dve.wait_ge(xT_ready, s + 1)
                        at = slice(s * S, (s + 1) * S) if isinstance(s, int) else bass.ds(s * S, S)
                        TS(XT_hi[:, :, at], xT[:, j], 1.0, None, ALU.mult).then_inc(XT_split, 1)
                        dve.wait_ge(XT_split, 2 * s + 1)
                        TT(XT_lo[:, :, at], xT[:, j], XT_hi[:, :, at].bitcast(F32), ALU.subtract).then_inc(XT_split, 1)
                    if live(s - 1):
                        dve.wait_ge(routed, s)
                        TS(batch(logits, s - 1), bank[3 - j][:, 0:E_], 1.0, None, ALU.mult).then_inc(logits_ready, 1)
                run_pairs(dve, step, 1)

                def add_shared(g):
                    dve.wait_ge(sh_out, g + 1)
                    for i in range(2):
                        rows = X[:, g * GROUP + 2 * i:g * GROUP + 2 * i + 2, :].rearrange("p b n -> p (b n)")
                        TT(rows, bank[4 + i][:], rows, ALU.add).then_inc(sh_added, 1)

                for g in range(NG):
                    dve.wait_ge(lat_rounded, g + 1)
                    nc.vector.scalar_tensor_tensor(XL[:, g * GW:(g + 1) * GW], lat_hi[:].bitcast(F32), low_rows[:, 0:1], bank[0][:],
                                                   ALU.mult, ALU.add).then_inc(XL_ready, 1)
                    dve.wait_ge(sh_relu, g + 1)
                    TT(prod[:, 0, :], bank[1][:], relu[:, 0, :], ALU.mult).then_inc(sh_prod, 1)
                    dve.wait_ge(sh_prod, 2 * g + 1)
                    wait(dve, y_split, g)
                    TT(hidden[:, 0, :], prod[:, 0, :], relu[:, 0, :], ALU.mult).then_inc(sh_prod, 1)
                    if g > 0:
                        add_shared(g - 1)
                    dve.wait_ge(y_rounded, g + 1)
                    wait(dve, sh_out, g)
                    TT(y_lo[:], hidden[:, 0, :], y_hi[:].bitcast(F32), ALU.subtract).then_inc(y_split, 1)

                add_shared(NG - 1)

                dve.wait_ge(exp_ready, 1)
                link(TS(gates[:], gates[:], 1.0, None, ALU.add))
                link(nc.vector.reciprocal(gates[:], gates[:]))
                link(TT(ranked[:], gates[:], route_bias[:].rearrange("p (a n) -> p a n", a=1).broadcast_to([128, B, E_]), ALU.add))
                for b in range(B):
                    ins = nc.vector.max(top[:, b, :], ranked[:, b, :])
                link(ins)
                for b in range(B):
                    ins = nc.vector.match_replace(cut[:, b, :], top[:, b, :], ranked[:, b, :], -1e30)
                link(ins)
                link(TT(cut[:], cut[:], ranked[:], ALU.not_equal))
                link(TT(gates[:], gates[:], cut[:], ALU.mult))
                link(nc.vector.tensor_reduce(gate_sum[:, 0, :], gates[:], AX.X, ALU.add))
                link(nc.vector.reciprocal(gate_sum[:, 1, :], gate_sum[:, 0, :]))
                link(TS(gate_sum[:, 1, :], gate_sum[:, 1, :], 2.5, None, ALU.mult))
                link(TT(gates[:], gates[:], gate_sum[:, 1, :].rearrange("p (b n) -> p b n", n=1).broadcast_to([128, B, E_]), ALU.mult))

            @block.tensor
            def _(pe):
                def step(s, j):
                    if live(s):
                        pe.wait_ge(xn_ready, s + 1)
                        wait(pe, xT_ready, s - 1)
                        for k in range(KD):
                            ins = nc.tensor.transpose(bank[j][:, k * 128:(k + 1) * 128], xn[:, j, k * 128:(k + 1) * 128], ident[:])
                        ins.then_inc(x_transposed, 1)
                    u, i = s - 1, 1 - j
                    if live(u):
                        pe.wait_ge(xT_ready, u + 1)
                        wait(pe, logits_ready, u - 1)
                        for k in range(KD):
                            ins = nc.tensor.matmul(bank[2 + i][:, 0:E_], xT[:, i, k, :], wg[:, k, :], start=(k == 0), stop=(k == KD - 1))
                        ins.then_inc(routed, 1)
                run_pairs(pe, step, 1)

                pe.wait_ge(w_split, 2)
                pe.wait_ge(XT_split, 2 * B)
                pe.wait_ge(logits_ready, B)

                def up(dst, w, g):
                    for k in range(KD):
                        at = slice(g * GW, (g + 1) * GW)
                        ins = matmul3(nc, dst[:], (w_hi[:, w, k, :], w_lo[:, w, k, :]), (XT_hi[:, k, at], XT_lo[:, k, at]),
                                      first=(k == 0), last=(k == KD - 1))
                    return ins

                def ups(g):
                    wait(pe, XL_ready, g)
                    up(bank[0], 0, g).then_inc(lat_projected, 1)
                    wait(pe, sh_prod, 2 * g - 1)
                    up(bank[2], 2, g)
                    up(bank[1], 1, g).then_inc(up_done, 1)

                ups(0)
                for g in range(NG):
                    if g + 1 < NG:
                        ups(g + 1)
                    pe.wait_ge(y_split, g + 1)
                    wait(pe, sh_added, 2 * g)
                    for i in range(GROUP):
                        tok = slice(i * S, (i + 1) * S)
                        ins = matmul3(nc, bank[4 + i // 2][:, (i % 2) * D:(i % 2 + 1) * D], (y_hi[:, tok], y_lo[:, tok]), (sw2_hi[:], sw2_lo[:]), True, True)
                    ins.then_inc(sh_out, 1)

        we_in = sb("moe_we_in", [128, 2, 2, HID])
        we_hi = sb("moe_we_hi", [128, 2, 2, HID], F32R)
        we_lo = sb("moe_we_lo", [128, 2, 2, HID], F32R)
        gate_of = sb("moe_gate_of", [128, 2, B])
        we_loaded = [sem("moe_we0"), sem("moe_we1")]
        we_rounded = sem("moe_we_rounded")
        we_split = sem("moe_we_split")
        gate_copied = sem("moe_gate_copied")
        ups_done = sem("moe_ups_done")
        relu_done = sem("moe_relu_done")
        prod_done = sem("moe_prod_done")
        hidden_done = sem("moe_hidden_done")
        downs_done = sem("moe_downs_done")
        acc_added = sem("moe_acc_added")
        STEPS = E_ * NG

        def run(eng, step, extra):
            for e in range(2):
                for g in range(NG):
                    step(e * NG + g, g, e, e)
            with eng.Fori(1, E_ // 2 - 1) as i:
                for j in range(2):
                    for g in range(NG):
                        step(i * 8 + 4 * j + g, g, i * 2 + j, j)
            for e in range(E_ - 2, E_):
                for g in range(NG):
                    step(e * NG + g, g, e, e % 2)
            for g in range(extra):
                step(STEPS + g, g, E_, 0)

        with nc.Block() as block:
            @block.sync
            def _(sp):
                def load(e, j):
                    wait(sp, we_split, e - 1)
                    for w, name in enumerate(("rw1T", "rwgT")):
                        src = a[name][e] if isinstance(e, int) else a[name][bass.ds(e, 1)].rearrange("a l n -> (a l) n")
                        for half in range(2):
                            sp.dma_start(we_in[half * LAT:(half + 1) * LAT, j, w, :], src).then_inc(we_loaded[j], 16)
                for e in range(2):
                    load(e, e)
                with sp.Fori(1, E_ // 2) as i:
                    for j in range(2):
                        load(i * 2 + j, j)

            @block.scalar
            def _(act):
                def round_weights(e, j, n):
                    act.wait_ge(we_loaded[j], n)
                    wait(act, ups_done, 4 * (e - 1))
                    nc.scalar.activation(we_hi[:, j], we_in[:, j], ACT.Copy).then_inc(we_rounded, 1)

                round_weights(0, 0, 64)

                def step(t, g, e, j):
                    if live(t, STEPS):
                        act.wait_ge(ups_done, t + 1)
                        wait(act, hidden_done, t - 1)
                        nc.scalar.activation(relu[:, g % 2, :], bank[2 + g % 2][:], ACT.Relu).then_inc(relu_done, 1)
                    if g == 1 and live(e + 1, E_):
                        round_weights(e + 1, 1 - j, 64 * ((e + 1) // 2 + 1) if isinstance(e, int) else pair_count(e, j, 1 - j, 1) * 4)
                run(act, step, 0)

            @block.gpsimd
            def _(pool):
                def step(t, g, e, j):
                    pool.wait_ge(prod_done, t + 1)
                    wait(pool, downs_done, t - 1)
                    nc.gpsimd.tensor_tensor(hidden[:, g % 2, :], prod[:, g % 2, :], relu[:, g % 2, :], ALU.mult).then_inc(hidden_done, 1)
                run(pool, step, 0)

            @block.vector
            def _(dve):
                def split_weights(e, j):
                    dve.wait_ge(we_rounded, e + 1)
                    wait(dve, ups_done, 4 * (e - 1))
                    nc.vector.tensor_tensor(we_lo[:, j], we_in[:, j], we_hi[:, j].bitcast(F32), ALU.subtract).then_inc(we_split, 1)
                    src = gates[:, :, e:e + 1] if isinstance(e, int) else gates[:, :, bass.ds(e, 1)]
                    wait(dve, acc_added, 4 * (e - 1))
                    nc.vector.tensor_scalar(gate_of[:, j, :], src.rearrange("p b a -> p (b a)"), 1.0, None, ALU.mult).then_inc(gate_copied, 1)

                split_weights(0, 0)

                def step(t, g, e, j):
                    if live(t, STEPS):
                        dve.wait_ge(relu_done, t + 1)
                        wait(dve, hidden_done, t - 1)
                        nc.vector.tensor_tensor(prod[:, g % 2, :], bank[g % 2][:], relu[:, g % 2, :], ALU.mult).then_inc(prod_done, 1)
                    u, ug = t - 3, (g + 1) % 4
                    if live(u, STEPS):
                        uj = j if g >= 3 else 1 - j
                        dve.wait_ge(downs_done, u + 1)
                        if ug == 0:
                            dve.wait_ge(gate_copied, e + 1)
                        wait(dve, acc_added, u - 3)
                        for i in range(GROUP):
                            b = ug * GROUP + i
                            ins = nc.vector.scalar_tensor_tensor(acc[:, b, :], bank[4 + ug % 2][:, i * LAT:(i + 1) * LAT], gate_of[:, uj, b:b + 1], acc[:, b, :],
                                                                 ALU.mult, ALU.add)
                        ins.then_inc(acc_added, 1)
                    if g == 2 and live(e + 1, E_):
                        split_weights(e + 1, 1 - j)
                run(dve, step, 3)

            @block.tensor
            def _(pe):
                def step(t, g, e, j):
                    if live(t, STEPS):
                        if g == 0:
                            pe.wait_ge(we_split, e + 1)
                        wait(pe, prod_done, t - 1)
                        wait(pe, relu_done, t - 1)
                        toks = XL[:, g * GW:(g + 1) * GW]
                        for w in (1, 0):
                            nc.tensor.matmul(bank[2 * w + g % 2][:], we_hi[:, j, w, :], toks, start=True, stop=False)
                            ins = nc.tensor.matmul(bank[2 * w + g % 2][:], we_lo[:, j, w, :], toks, start=False, stop=True)
                        ins.then_inc(ups_done, 1)
                    u, ug = t - 2, (g + 2) % 4
                    if live(u, STEPS):
                        ue = e if g >= 2 else e - 1
                        w2 = we2[:, ue, :] if isinstance(ue, int) else we2[:, bass.ds(ue, 1), :].rearrange("p a l -> p (a l)")
                        pe.wait_ge(hidden_done, u + 1)
                        wait(pe, acc_added, u - 1)
                        for i in range(GROUP):
                            ins = nc.tensor.matmul(bank[4 + ug % 2][:, i * LAT:(i + 1) * LAT], hidden[:, ug % 2, i * S:(i + 1) * S], w2, start=True, stop=True)
                        ins.then_inc(downs_done, 1)
                run(pe, step, 2)

        acc_b = sb("moe_acc_b", [128, 2, 128])
        accT = sb("moe_accT", [128, 2, 128])
        padded = sem("moe_padded")
        acc_copied = sem("moe_acc_copied")
        acc_transposed = sem("moe_acc_transposed")
        accT_ready = sem("moe_accT_ready")
        upped = sem("moe_upped")
        result_ready = sem("moe_result_ready")
        stored = sem("moe_stored")
        with nc.Block() as block:
            @block.vector
            def _(dve):
                nc.vector.memset(acc_b[:], 0.0).then_inc(padded, 1)
                dve.wait_ge(padded, 1)

                def step(s, j):
                    if live(s):
                        wait(dve, acc_transposed, s - 1)
                        nc.vector.tensor_scalar(acc_b[:, j, 0:LAT], batch(acc, s), 1.0, None, ALU.mult).then_inc(acc_copied, 1)
                    if live(s - 2):
                        dve.wait_ge(upped, s - 1)
                        nc.vector.tensor_tensor(batch(X, s - 2), bank[2 + j][:, 0:D], batch(X, s - 2), ALU.add).then_inc(result_ready, 1)
                run_pairs(dve, step, 2)

            @block.tensor
            def _(pe):
                def step(s, j):
                    if live(s):
                        pe.wait_ge(acc_copied, s + 1)
                        wait(pe, accT_ready, s - 1)
                        nc.tensor.transpose(bank[j][:, 0:128], acc_b[:, j, :], ident[:]).then_inc(acc_transposed, 1)
                    u, i = s - 1, 1 - j
                    if live(u):
                        pe.wait_ge(accT_ready, u + 1)
                        wait(pe, result_ready, u - 1)
                        nc.tensor.matmul(bank[2 + i][:, 0:D], accT[0:LAT, i, :], wup[:], start=True, stop=True).then_inc(upped, 1)
                run_pairs(pe, step, 1)

            @block.scalar
            def _(act):
                def step(s, j):
                    if live(s):
                        act.wait_ge(acc_transposed, s + 1)
                        wait(act, upped, s - 1)
                        nc.scalar.activation(accT[:, j, :], bank[j][:, 0:128], ACT.Copy).then_inc(accT_ready, 1)
                run_pairs(act, step, 0)

            @block.sync
            def _(sp):
                for g in range(NG):
                    done = slice(g * GROUP, (g + 1) * GROUP)
                    sp.wait_ge(result_ready, (g + 1) * GROUP)
                    sp.dma_start(out[done].rearrange("b p d -> p b d"), X[:, done, :]).then_inc(stored, 16)
                sp.wait_ge(stored, 16 * NG)


def weights_ahead(a, sb):
    chunks = lambda name: a[name].rearrange("(k p) n -> p k n", p=128)
    w = {name: sb(name, shape) for name, shape in (
        ("sp_gb", [128, 2, D]), ("sp_slopes", [128, D, 16]), ("sp_rank", [128, 89]), ("sp_table", [64, 129]),
        ("win_wqk", [128, KD, 2 * D]), ("win_w_in", [128, 2, KD, D]), ("win_band_in", [128, 128]), ("win_parity", [128, 2]),
        ("cr_wqk", [128, 2, KD, D]), ("cr_w_in", [128, 2, KD, D]),
        ("moe_wg", [128, KD, 16]), ("moe_w_in", [128, 3, KD, 128]), ("moe_sw2", [128, D]), ("moe_wup", [64, D]),
        ("moe_we2", [128, 16, 64]), ("moe_route_bias", [128, 16]), ("moe_low_rows", [128, 1]))}
    qkv = chunks("w_qkvT")
    row = lambda name: a[name].rearrange("(a n) -> a n", a=1).broadcast_to([128, D])
    transfers = [
        (w["sp_gb"][:, 0, :], row("L0_ffn_ln_gamma")), (w["sp_gb"][:, 1, :], row("L0_ffn_ln_beta")),
        (w["sp_slopes"][:].rearrange("p d g -> p (d g)"), a["L0_ffn_spline_slopes"].rearrange("(a t) j g -> a (t j g)", a=1).broadcast_to([128, D * 16])),
        (w["sp_rank"][:], a["rank"]),
        (w["sp_table"][:, 0:64], a["L0_ffn_spline_bases"].rearrange("t j g -> t (j g)")),
        (w["sp_table"][:, 64:128], a["L0_ffn_spline_slopes"].rearrange("t j g -> t (j g)")),
        (w["sp_table"][:, 128:129], a["L0_ffn_output_scale"].rearrange("(t a) -> t a", a=1)),
        (w["win_wqk"][:], qkv[:, :, 0:2 * D]), (w["win_w_in"][:, 0], qkv[:, :, 2 * D:3 * D]), (w["win_w_in"][:, 1], chunks("w_outT")),
        (w["win_band_in"][:], a["band"]), (w["win_parity"][:], a["parity"]),
        (w["cr_wqk"][:, 0], chunks("x_wqT")), (w["cr_wqk"][:, 1], chunks("x_wkT")),
        (w["cr_w_in"][:, 0], chunks("x_wvT")), (w["cr_w_in"][:, 1], chunks("x_woT")),
        (w["moe_wg"][:], chunks("WgT")), (w["moe_w_in"][:, 0, :, 0:64], chunks("WdownT")), (w["moe_w_in"][:, 0, :, 64:], chunks("WdownT")),
        (w["moe_w_in"][:, 1], chunks("sw1T")), (w["moe_w_in"][:, 2], chunks("swgT")), (w["moe_sw2"][:], a["sw2T"]), (w["moe_wup"][:], a["WupT"]),
        (w["moe_we2"][:], a["rw2T"].rearrange("e h l -> h e l")),
        (w["moe_route_bias"][:], a["L1_ffn_biases"].rearrange("(a n) -> a n", a=1).broadcast_to([128, 16])),
        (w["moe_low_rows"][:], a["low_rows"])]
    return w, transfers


def phase_rest(nc, a, sem, sb, bank, X, ident, mean, var_eps, rstd, minus_half, stats, ln_tmp, out, clear_semaphores):
    t = (nc, a, sem, sb, bank, X, ident, mean, var_eps, rstd, minus_half, stats, ln_tmp)
    w, transfers = weights_ahead(a, sb)
    ahead_loaded = sem("ahead_loaded")
    phase_retention(*t, transfers, ahead_loaded)
    phase_spline(*t, w, ahead_loaded, 16 * len(transfers))
    phase_window(*t, w, ahead_loaded, 16 * len(transfers))
    phase_cross(*t, w)
    clear_semaphores()
    phase_moe(*t, w, out)


INPUTS = ["x", "L0_attn_bq", "L0_attn_bk", "L0_attn_bo", "L0_xattn_Wh", "L0_xattn_wg_w", "L0_xattn_wo_w",
          "L0_xattn_gn_gamma", "L0_xattn_gn_beta", "L0_ffn_ln_gamma", "L0_ffn_ln_beta", "L0_ffn_spline_bases",
          "L0_ffn_spline_slopes", "L0_ffn_output_scale", "ctx_2048", "L1_ffn_biases"]


def kernel(**inputs):
    import concourse.bacc as bacc
    from concourse.bass_utils import run_bass_kernel_spmd

    f32 = np.float32
    arrays = {n: np.ascontiguousarray(inputs[n]) for n in INPUTS}
    for name, src in (("wqT", "L0_attn_wq"), ("wkT", "L0_attn_wk"), ("wvT", "L0_attn_wv"), ("woT", "L0_attn_wo")):
        arrays[name] = np.ascontiguousarray(np.asarray(inputs[src]).T)
    for name, src in (("ln_gT", "L0_attn_ln_g"), ("ln_bT", "L0_attn_ln_b"), ("bvT", "L0_attn_bv")):
        arrays[name] = np.ascontiguousarray(np.asarray(inputs[src]).reshape(-1, 128).T)
    arrays["ctxT"] = np.ascontiguousarray(np.asarray(inputs["ctx_2048"]).reshape(B * S, D).T)
    arrays["w_qkvT"] = np.ascontiguousarray(np.asarray(inputs["L1_attn_w_qkv"]).T)
    arrays["w_outT"] = np.ascontiguousarray(np.asarray(inputs["L1_attn_w_out"]).T)
    for name, src in (("x_wqT", "L1_xattn_wq"), ("x_wkT", "L1_xattn_wk"), ("x_wvT", "L1_xattn_wv"), ("x_woT", "L1_xattn_wo"),
                      ("WgT", "L1_ffn_Wg"), ("WdownT", "L1_ffn_Wdown"), ("sw1T", "L1_ffn_sw1"), ("swgT", "L1_ffn_swg"),
                      ("sw2T", "L1_ffn_sw2"), ("WupT", "L1_ffn_Wup")):
        arrays[name] = np.ascontiguousarray(np.asarray(inputs[src]).T)
    for name, src in (("rw1T", "L1_ffn_rw1"), ("rwgT", "L1_ffn_rwg"), ("rw2T", "L1_ffn_rw2")):
        arrays[name] = np.ascontiguousarray(np.asarray(inputs[src]).transpose(0, 2, 1))
    arrays["WhT"] = np.ascontiguousarray(np.asarray(inputs["L0_xattn_Wh"]).transpose(2, 0, 1))
    theta = (f32(1.0) / np.power(f32(10000.0), np.arange(0, DK0, 2, dtype=f32) / f32(DK0))).astype(f32)
    freqs = np.arange(S, dtype=f32)[:, None] * theta[None, :]
    cos, sin = np.cos(freqs).astype(f32), np.sin(freqs).astype(f32)
    arrays["cos"] = np.concatenate([cos, cos], axis=1)
    arrays["sin"] = np.concatenate([-sin, sin], axis=1)
    arrays["ident"] = np.eye(128, dtype=f32)
    row, col = np.arange(128)[:, None], np.arange(128)[None, :]
    arrays["causal"] = np.where(col <= row, f32(0), f32(MASKED)).astype(f32)
    gamma = (f32(1.0) - f32(2.0) ** (f32(-5.0) - np.arange(2, dtype=f32))).astype(f32)
    expo = np.arange(S, dtype=f32)[None, :] - np.arange(S, dtype=f32)[:, None]
    with np.errstate(over="ignore"):
        dec = np.where(expo[None] <= 0, gamma[:, None, None] ** expo[None], f32(0)).astype(f32)
    dec = dec / np.sqrt(dec.sum(axis=-1, dtype=f32))[:, None, :]
    arrays["decayT"] = np.ascontiguousarray((dec / np.sqrt(f32(128.0))).astype(f32).transpose(2, 0, 1))
    arrays["band"] = np.where((col <= row) & (col >= row - 64), f32(0), f32(MASKED)).astype(f32)
    head = np.arange(128) // 16
    arrays["parity"] = np.stack([head % 2 == 0, head % 2 == 1], axis=1).astype(f32)
    arrays["low_rows"] = np.where(np.arange(128)[:, None] < 64, f32(0), f32(-1)).astype(f32)
    ranks = np.concatenate([np.arange(63, -1, -1), np.arange(7, -1, -1), np.arange(17)]).astype(f32)
    arrays["rank"] = np.tile(ranks, (128, 1))
    nc = bacc.Bacc("TRN2", target_bir_lowering=False, num_devices=1)
    aps = {n: nc.dram_tensor(f"in_{n}", v.shape, mybir.dt.from_np(v.dtype), kind="ExternalInput").ap() for n, v in arrays.items()}
    out = nc.dram_tensor("out", (B, S, D), F32, kind="ExternalOutput").ap()
    decoder_kernel(nc, aps, out)
    result = run_bass_kernel_spmd(nc, [{f"in_{n}": v for n, v in arrays.items()}], core_ids=[0])
    return result.results[0]["out"]
```

```python
import numpy as np
import concourse.bass as bass
from concourse import mybir
from concourse.alu_op_type import AluOpType as ALU
from contextlib import ExitStack

F32 = mybir.dt.float32
F32R = mybir.dt.float32r
BF16 = mybir.dt.bfloat16
ACT = mybir.ActivationFunctionType
AX = mybir.AxisListType

B, S, D = 16, 128, 256
KD = D // 128
LN_EPS = 1e-5

HEADS0, DK0 = 16, 128
QUADS = HEADS0 // 4
QW = 4 * DK0
MASKED = -1e30


def wait(eng, sem, value):
    if isinstance(value, int) and value <= 0:
        return
    eng.wait_ge(sem, value)


def matmul3(nc, out, lhs, rhs, first, last):
    (lh, ll), (rh, rl) = lhs, rhs
    nc.tensor.matmul(out, lh, rl, start=first, stop=False)
    nc.tensor.matmul(out, ll, rh, start=False, stop=False)
    return nc.tensor.matmul(out, lh, rh, start=False, stop=last)


def finish_stats(nc, dve, done, count, stats, mean, var_eps, tmp, eps):
    half = D // 2
    me, m2e, mo, m2o = stats[:, :, 1], stats[:, :, 2], stats[:, :, 4], stats[:, :, 5]

    def link(ins):
        nonlocal count
        count += 1
        ins.then_inc(done, 1)

    link(nc.vector.tensor_tensor(tmp[:, 0, :], me, mo, ALU.add))
    link(nc.vector.tensor_tensor(tmp[:, 1, :], me, mo, ALU.subtract))
    link(nc.vector.tensor_tensor(tmp[:, 2, :], m2e, m2o, ALU.add))
    dve.wait_ge(done, count)
    link(nc.vector.tensor_scalar(mean, tmp[:, 0, :], 0.5, None, ALU.mult))
    link(nc.vector.scalar_tensor_tensor(tmp[:, 3, :], tmp[:, 1, :], half / 2.0, tmp[:, 1, :], ALU.mult, ALU.mult))
    dve.wait_ge(done, count)
    link(nc.vector.tensor_tensor(tmp[:, 4, :], tmp[:, 3, :], tmp[:, 2, :], ALU.add))
    dve.wait_ge(done, count)
    link(nc.vector.tensor_scalar(var_eps, tmp[:, 4, :], 1.0 / D, float(eps), ALU.mult, ALU.add))
    return count


def decoder_kernel(nc, a, out):
    ctx = ExitStack()
    with ctx:
        def sb(name, shape, dt=F32, where=ctx):
            return where.enter_context(nc.sbuf_tensor(name, shape, dt))

        sems_in_use = []

        def sem(name):
            sems_in_use.append(nc.alloc_semaphore(name=name))
            return sems_in_use[-1]

        def clear_semaphores():
            nc.clear_and_free_semaphores(sems_in_use)
            nc.all_engine_barrier()
            sems_in_use.clear()

        bank = [ctx.enter_context(nc.psum_tensor(f"bank{i}", [128, 512], F32)) for i in range(8)]
        X = sb("X", [128, B, D])
        ident = sb("ident", [128, 128])
        mean = sb("mean", [128, B])
        var_eps = sb("var_eps", [128, B])
        rstd = sb("rstd", [128, B])
        minus_half = sb("minus_half", [128, B])
        stats = sb("stats", [128, B, 6])
        ln_tmp = sb("ln_tmp", [128, 5, B])

        phase_attn0(nc, a, sem, sb, bank, X, ident, mean, var_eps, rstd, minus_half, stats, ln_tmp)
        phase_rest(nc, a, sem, sb, bank, X, ident, mean, var_eps, rstd, minus_half, stats, ln_tmp, out, clear_semaphores)


def second_norm(nc, dve, done, count, var_eps, rstd, square, tmp, eps):
    for ins in (lambda: nc.vector.tensor_tensor(square, rstd, rstd, ALU.mult),
                lambda: nc.vector.tensor_tensor(square, square, tmp[:, 4, :], ALU.mult),
                lambda: nc.vector.tensor_scalar(var_eps, square, 1.0 / D, float(eps), ALU.mult, ALU.add)):
        ins().then_inc(done, 1)
        count += 1
        dve.wait_ge(done, count)
    return count


def batch(tile, b):
    if isinstance(b, int):
        return tile[:, b, :]
    return tile[:, bass.ds(b, 1), :].rearrange("p a n -> p (a n)")


def one(tile, b):
    return tile[:, b:b + 1] if isinstance(b, int) else tile[:, bass.ds(b, 1)]


def phase_attn0(nc, a, sem, sb_, bank, X, ident, mean, var_eps, rstd, minus_half, stats, ln_tmp):
    local = ExitStack()
    with local:
        def sb(name, shape, dt=F32):
            return sb_(name, shape, dt, local)

        STAGES = 2
        GROUP = 4
        NG = B // GROUP
        GW = GROUP * S
        STEPS = NG * HEADS0
        WH = sb("WH", [128, 3, KD, HEADS0 * DK0], F32R)
        WL = sb("WL", [128, 3, KD, HEADS0 * DK0], F32R)
        WO_hi = sb("WO_hi", [128, HEADS0, D], F32R)
        WO_lo = sb("WO_lo", [128, HEADS0, D], F32R)
        stage = sb("stage", [128, STAGES, KD, QW])
        h_of = sb("h_of", [128, D])
        qk_bias = sb("qk_bias", [128, 2, HEADS0])
        rot_bias = sb("rot_bias", [128, 2, HEADS0])
        cos = sb("cos", [128, 2, S])
        sin = sb("sin", [128, 2, S])
        mask_f = h_of[:, 0:128]
        mask = sb("mask", [128, 128], BF16)
        ident_b = sb("ident_b", [128, 128], BF16)
        zeros_b = sb("zeros_b", [128, 128], BF16)
        gb = sb("gb", [128, 2, KD])
        out_bias = sb("out_bias", [128, D])
        bv_col = sb("bv_col", [128, HEADS0])
        square = sb("square", [128, B])
        rstd2 = sb("rstd2", [128, B])
        rstd12 = sb("rstd12", [128, B])
        xn = sb("xn", [128, D])
        xT_full = sb("xT_full", [128, KD, GW])
        xT_hi = sb("xT_hi", [128, KD, GW], F32R)
        xT_lo = sb("xT_lo", [128, KD, GW], F32R)
        roped = [sb("roped_q", [128, 2, GW]), sb("roped_k", [128, 2, GW])]
        sin_part = [sb("sin_q", [128, GW]), sb("sin_k", [128, GW])]
        V = sb("V", [128, 2, GROUP, QW])
        P = sb("P", [128, GROUP, 128])
        PT = sb("PT", [128, GROUP, 128])
        oT_hi = sb("oT_hi", [128, GROUP, 128], F32R)
        oT_lo = sb("oT_lo", [128, GROUP, 128], F32R)
        neg_max = sb("neg_max", [128, 2, GROUP])
        exp_sum = sb("exp_sum", [128, 2, GROUP])
        inv_sum = sb("inv_sum", [128, 2, GROUP])

        x_loaded = [sem(f"x{g}_loaded") for g in range(4)]
        first_loaded = sem("first_loaded")
        consts_loaded = sem("consts_loaded")
        stage_loaded = [sem(f"stage{i}_loaded") for i in range(STAGES)]
        weights_rounded = sem("weights_rounded")
        weights_split = sem("weights_split")
        consts_made = sem("consts_made")
        ln0 = sem("ln0")
        rstd_ready = sem("rstd_ready")
        half_set = sem("half_set")
        xn_ready = sem("xn_ready")
        x_transposed = sem("x_transposed")
        xT_evacuated = sem("xT_evacuated")
        xT_rounded = sem("xT_rounded")
        xT_split = sem("xT_split")
        projected = [sem("q_projected"), sem("k_projected")]
        rotated = [sem("q_rotated"), sem("k_rotated")]
        products = [sem("q_products"), sem("k_products")]
        roped_sum = [sem("q_roped"), sem("k_roped")]
        v_projected = sem("v_projected")
        v_ready = sem("v_ready")
        scored = sem("scored")
        max_found = sem("max_found")
        exps_done = sem("exps_done")
        inv_ready = sem("inv_ready")
        probs_ready = sem("probs_ready")
        p_transposed = sem("p_transposed")
        PT_ready = sem("PT_ready")
        pv_done = sem("pv_done")
        oT_hi_ready = sem("oT_hi_ready")
        oT_lo_ready = sem("oT_lo_ready")
        out_projected = sem("out_projected")
        out_added = sem("out_added")
        h_added = sem("h_added")

        QK, V_, SC, PO, OUT, XB = bank[0:2], bank[2], bank[3], bank[4], bank[5:7], bank[7]
        w_src = [a[n].rearrange("(k p) n -> p k n", p=128) for n in ("wqT", "wkT", "wvT")]
        woT = a["woT"].rearrange("(h p) n -> p h n", p=DK0)
        ITEMS = [(0, 0), (0, 1), (0, 2)] + [item for q in range(1, QUADS) for item in ((q, 2), (q - 1, 3), (q, 0), (q, 1))] + [(QUADS - 1, 3)]
        split_by = {item: i + 1 for i, item in enumerate(ITEMS)}
        four = lambda ap: ap.rearrange("p (a n) -> p a n", a=1).broadcast_to([128, 4, 128])

        def parts(i):
            q, w = ITEMS[i]
            src = stage[:, i % STAGES, :, :]
            if w == 3:
                heads = slice(4 * q, 4 * q + 4)
                return src.rearrange("p k n -> p (k n)").rearrange("p (h n) -> p h n", h=4), WO_hi[:, heads, :], WO_lo[:, heads, :]
            cols = slice(q * QW, (q + 1) * QW)
            return src, WH[:, w, :, cols], WL[:, w, :, cols]

        LN_PARTS = ((slice(0, GROUP), GROUP), (slice(GROUP, B), B + 11))

        def rounded_at(r):
            return [i for i in ((3, 4) if r == 0 else (r + 4,)) if i < len(ITEMS)]

        def split_at(r):
            return [i for i in (r + 3,) if i < len(ITEMS)]

        def v_at(r):
            return [(0, 2 * r), (0, 2 * r + 1)] if r < 2 else [((r + 2) // 4, (r + 2) % 4)] if r < 14 else []


        def run(eng, step):
            for r in range(HEADS0):
                step(r, r, 0)
            with eng.Fori(1, NG - 1) as g:
                for r in range(HEADS0):
                    step(g * HEADS0 + r, r, g)
            for r in range(HEADS0):
                step((NG - 1) * HEADS0 + r, r, NG - 1)
            for r in range(3):
                step(STEPS + r, r, NG)

        with nc.Block() as block:
            @block.sync
            def _(sp):
                def load_x(g):
                    some = slice(g * GROUP, (g + 1) * GROUP)
                    sp.dma_start(X[:, some, :], a["x"][some].rearrange("b p d -> p b d")).then_inc(x_loaded[g], 16)

                def load_weights(i):
                    q, w = ITEMS[i]
                    wait(sp, weights_split, i - STAGES + 1)
                    if w == 3:
                        src = woT[:, 4 * q:4 * q + 4, :]
                    else:
                        src = w_src[w][:, :, q * QW:(q + 1) * QW]
                    sp.dma_start(parts(i)[0], src).then_inc(stage_loaded[i % STAGES], 16)

                load_x(0)
                for dst, src in ((gb[:, 0, :], a["ln_gT"]), (gb[:, 1, :], a["ln_bT"]), (ident[:], a["ident"])):
                    sp.dma_start(dst, src).then_inc(first_loaded, 16)
                for i in range(STAGES):
                    load_weights(i)
                for dst, src in ((mask_f, a["causal"]),
                                 (cos[:, 0, :], a["cosT_q"]), (cos[:, 1, :], a["cosT_k"]), (sin[:, 0, :], a["sinT_q"]), (sin[:, 1, :], a["sinT_k"]),
                                 (qk_bias[:, 0, :], a["bqT"]), (qk_bias[:, 1, :], a["bkT"]), (bv_col[:], a["bvT"]),
                                 (rot_bias[:, 0, :], a["bqT_rot"]), (rot_bias[:, 1, :], a["bkT_rot"]),
                                 (out_bias[:], a["L0_attn_bo"].rearrange("(a n) -> a n", a=1).broadcast_to([128, D]))):
                    sp.dma_start(dst, src).then_inc(consts_loaded, 16)
                for g in range(1, NG):
                    load_x(g)
                for i in range(STAGES, len(ITEMS)):
                    load_weights(i)

            @block.gpsimd
            def _(pool):
                nc.gpsimd.memset(minus_half[:], -0.5).then_inc(half_set, 1)
                pool.wait_ge(half_set, 1)
                def power(part, second):
                    some, n = LN_PARTS[part]
                    pool.wait_ge(ln0, n + 7 + 3 * second)
                    nc.gpsimd.tensor_tensor((rstd, rstd2)[second][:, some], var_eps[:, some], minus_half[:, some], ALU.pow).then_inc(rstd_ready, 1)

                def step(t, p):
                    for w in range(2):
                        pool.wait_ge(products[w], 2 * t + 2)
                        nc.gpsimd.tensor_tensor(roped[w][:, p, :], roped[w][:, p, :], sin_part[w][:], ALU.add).then_inc(roped_sum[w], 1)

                power(0, 0)
                power(0, 1)
                for t in range(4):
                    step(t, t % 2)
                    if t in (2, 3):
                        power(1, t - 2)
                with pool.Fori(2, STEPS // 2) as i:
                    for p in range(2):
                        step(i * 2 + p, p)

            @block.scalar
            def _(act):
                def round_weights(i):
                    src, hi, _ = parts(i)
                    act.wait_ge(stage_loaded[i % STAGES], 16 * (i // STAGES + 1))
                    nc.scalar.activation(hi, src, ACT.Copy).then_inc(weights_rounded, 1)

                def evacuate_xT(b, i, group):
                    act.wait_ge(x_transposed, b + 1)
                    wait(act, xT_split, group)
                    for k in range(KD):
                        ins = nc.scalar.activation(xT_full[:, k, i * S:(i + 1) * S], XB[:, k * 128:(k + 1) * 128], ACT.Identity,
                                                   bias=gb[:, 1, k:k + 1], scale=gb[:, 0, k:k + 1])
                    ins.then_inc(xT_evacuated, 1)

                def round_xT(g):
                    act.wait_ge(xT_evacuated, GROUP * g + GROUP)
                    wait(act, projected[1], HEADS0 * g)
                    nc.scalar.activation(xT_hi[:], xT_full[:], ACT.Copy).then_inc(xT_rounded, 1)

                def step(s, r, g):
                    u = s - 2
                    if live(u, STEPS):
                        act.wait_ge(max_found, 1 + u)
                        wait(act, p_transposed, u)
                        for i in range(GROUP):
                            ins = nc.scalar.activation(P[:, i, :], SC[:, i * 128:(i + 1) * 128], ACT.Exp,
                                                       bias=neg_max[:, r % 2, i:i + 1], accum_out=exp_sum[:, r % 2, i:i + 1])
                        ins.then_inc(exps_done, 1)
                    if live(s, STEPS):
                        for w in range(2):
                            act.wait_ge(projected[w], s + 1)
                            wait(act, roped_sum[w], s)
                            for half in range(2):
                                ins = nc.scalar.activation(sin_part[w][64 * half:64 * half + 64, :], QK[w][64 * (1 - half):64 * (2 - half), :], ACT.Copy)
                            ins.then_inc(rotated[w], 1)
                            if w < len(v_at(r)):
                                quad, i = v_at(r)[w]
                                act.wait_ge(v_projected, (s - r) + 4 * quad + i + 1)
                                if i == 0:
                                    wait(act, pv_done, (s - r) + 4 * quad - 4)
                                nc.scalar.activation(V[:, quad % 2, i, :], V_[:], ACT.Copy).then_inc(v_ready, 1)
                    if r == 15 and live(g + 1, NG):
                        round_xT(g + 1)
                    if live(u, STEPS):
                        act.wait_ge(p_transposed, u + 1)
                        wait(act, pv_done, u)
                        nc.scalar.activation(flat(PT[:]), PO[:], ACT.Copy).then_inc(PT_ready, 1)
                        act.wait_ge(pv_done, u + 1)
                        wait(act, out_projected, u)
                        nc.scalar.activation(flat(oT_hi[:]), PO[:], ACT.Identity, bias=bv_col[:, (r - 2) % HEADS0:(r - 2) % HEADS0 + 1]).then_inc(oT_hi_ready, 1)
                    if isinstance(g, int) and g == 0:
                        for i in rounded_at(r):
                            round_weights(i)
                    if r in (5, 7, 9, 11) and live(g + 1, NG):
                        evacuate_xT(g * GROUP + GROUP + (r - 5) // 2, (r - 5) // 2, g + 1)

                for i in range(STAGES):
                    round_weights(i)
                act.wait_ge(first_loaded, 48)
                for b in range(GROUP):
                    evacuate_xT(b, b, 0)
                round_xT(0)
                round_weights(2)
                run(act, step)

            @block.vector
            def _(dve):
                def split_weights(i):
                    src, hi, lo = parts(i)
                    dve.wait_ge(weights_rounded, i + 1)
                    nc.vector.tensor_tensor(lo, src, hi.bitcast(F32), ALU.subtract).then_inc(weights_split, 1)

                def group_stats(g):
                    dve.wait_ge(x_loaded[g], 16)
                    for b in range(g * GROUP, g * GROUP + GROUP):
                        nc.vector.bn_stats(stats[:, b, :], X[:, b, :]).then_inc(ln0, 1)

                def first_stats(part):
                    some, n = LN_PARTS[part]
                    dve.wait_ge(ln0, n)
                    finish_stats(nc, dve, ln0, n, stats[:, some, :], mean[:, some], var_eps[:, some], ln_tmp[:, :, some], LN_EPS)

                def second_stats(part):
                    some, n = LN_PARTS[part]
                    dve.wait_ge(ln0, n + 7)
                    dve.wait_ge(rstd_ready, 2 * part + 1)
                    second_norm(nc, dve, ln0, n + 7, var_eps[:, some], rstd[:, some], square[:, some], ln_tmp[:, :, some], LN_EPS)

                def both_norms(part):
                    some, n = LN_PARTS[part]
                    dve.wait_ge(rstd_ready, 2 * part + 2)
                    nc.vector.tensor_tensor(rstd12[:, some], rstd[:, some], rstd2[:, some], ALU.mult).then_inc(ln0, 1)
                    dve.wait_ge(ln0, n + 11)

                def normalise(b):
                    wait(dve, x_transposed, b)
                    nc.vector.tensor_scalar(xn[:], batch(X, b), one(mean, b), one(rstd12, b), ALU.subtract, ALU.mult).then_inc(xn_ready, 1)

                def add_h(b):
                    wait(dve, h_added, 2 * b)
                    nc.vector.tensor_scalar(h_of[:], batch(X, b), one(mean, b), one(rstd, b), ALU.subtract, ALU.mult).then_inc(h_added, 1)
                    dve.wait_ge(h_added, 2 * b + 1)
                    nc.vector.tensor_tensor(batch(X, b), batch(X, b), h_of[:], ALU.add).then_inc(h_added, 1)

                def split_xT(g):
                    dve.wait_ge(xT_rounded, g + 1)
                    nc.vector.tensor_tensor(xT_lo[:], xT_full[:], xT_hi[:].bitcast(F32), ALU.subtract).then_inc(xT_split, 1)

                def rope(s, p, r, w):
                    dve.wait_ge(rotated[w], s + 1)
                    wait(dve, scored, s - 1)
                    per_batch = lambda ap: ap.rearrange("p (b n) -> p b n", b=GROUP)
                    table = lambda t: t[:, w, :].rearrange("p (a n) -> p a n", a=1).broadcast_to([128, GROUP, S])
                    nc.vector.scalar_tensor_tensor(per_batch(roped[w][:, p, :]), per_batch(QK[w][:]), qk_bias[:, w, r:r + 1], table(cos), ALU.add, ALU.mult).then_inc(products[w], 1)
                    nc.vector.scalar_tensor_tensor(per_batch(sin_part[w][:]), per_batch(sin_part[w][:]), rot_bias[:, w, r:r + 1], table(sin), ALU.add, ALU.mult).then_inc(products[w], 1)

                pair = lambda g, i: X[:, 4 * g + 2 * i:4 * g + 2 * i + 2, :] if isinstance(g, int) else X[:, bass.ds(g * 4 + 2 * i, 2), :]

                def add_out(g):
                    dve.wait_ge(out_projected, HEADS0 * g + HEADS0)
                    dve.wait_ge(h_added, 2 * GROUP * g + 2 * GROUP)
                    for i in range(2):
                        nc.vector.tensor_tensor(pair(g, i), OUT[i][:].rearrange("p (b n) -> p b n", b=2), pair(g, i), ALU.add).then_inc(out_added, 1)

                def add_const(g):
                    for i in range(2):
                        dve.wait_ge(out_added, 4 * g + 1 + i)
                        nc.vector.tensor_tensor(pair(g, i), pair(g, i), out_bias[:].rearrange("p (a n) -> p a n", a=1).broadcast_to([128, 2, D]), ALU.add).then_inc(out_added, 1)
                    dve.wait_ge(out_added, 4 * g + 4)
                    for i in range(GROUP):
                        nc.vector.bn_stats(batch(stats, g * GROUP + i), batch(X, g * GROUP + i))

                def step(s, r, g):
                    u = s - 2
                    if live(u, STEPS):
                        dve.wait_ge(scored, u + 1)
                        nc.vector.tensor_reduce(neg_max[:, r % 2, :], SC[:].rearrange("p (h n) -> p h n", h=GROUP), AX.X, ALU.max, negate=True).then_inc(max_found, 1)
                    if live(s - 3, STEPS):
                        dve.wait_ge(oT_hi_ready, s - 2)
                        nc.vector.scalar_tensor_tensor(flat(oT_lo[:]), PO[:], bv_col[:, (r - 3) % HEADS0:(r - 3) % HEADS0 + 1], flat(oT_hi[:]).bitcast(F32),
                                                       ALU.add, ALU.subtract).then_inc(oT_lo_ready, 1)
                    if live(u, STEPS):
                        dve.wait_ge(exps_done, u + 1)
                        nc.vector.reciprocal(inv_sum[:, r % 2, :], exp_sum[:, r % 2, :]).then_inc(inv_ready, 1)
                        dve.wait_ge(inv_ready, u + 1)
                        nc.vector.tensor_tensor(P[:], P[:], inv_sum[:, r % 2, :].rearrange("p (h n) -> p h n", n=1).broadcast_to([128, GROUP, 128]), ALU.mult).then_inc(probs_ready, 1)
                    if live(s, STEPS):
                        if r == 3 and live(g - 1, NG):
                            add_out(g - 1)
                        rope(s, r % 2, r, 0)
                        if r == 15 and live(g + 1, NG):
                            split_xT(g + 1)
                        rope(s, r % 2, r, 1)
                    if isinstance(g, int) and g == 0:
                        for i in split_at(r):
                            split_weights(i)
                        if r < GROUP:
                            add_h(r)
                        if r < 3:
                            group_stats(r + 1)
                        if r in (2, 3, 4):
                            (first_stats, second_stats, both_norms)[r - 2](1)
                    if r == 3 and live(g - 1, NG):
                        add_const(g - 1)
                    if r in (4, 6, 8, 10) and live(g + 1, NG):
                        normalise(g * GROUP + GROUP + (r - 4) // 2)
                    if r in (5, 7, 9, 11) and live(g + 1, NG):
                        add_h(g * GROUP + GROUP + (r - 5) // 2)

                group_stats(0)
                first_stats(0)
                split_weights(0)
                second_stats(0)
                split_weights(1)
                both_norms(0)
                for b in range(GROUP):
                    normalise(b)
                dve.wait_ge(consts_loaded, 16 * 11)
                nc.vector.tensor_copy(ident_b[:], ident[:]).then_inc(consts_made, 1)
                nc.vector.tensor_copy(mask[:], mask_f).then_inc(consts_made, 1)
                nc.vector.memset(zeros_b[:], 0.0).then_inc(consts_made, 1)
                split_xT(0)
                split_weights(2)
                run(dve, step)
                add_out(NG - 1)
                add_const(NG - 1)

            @block.tensor
            def _(pe):
                def transpose_x(b):
                    pe.wait_ge(xn_ready, b + 1)
                    wait(pe, xT_evacuated, b)
                    for k in range(KD):
                        ins = nc.tensor.transpose(XB[:, k * 128:(k + 1) * 128], xn[:, k * 128:(k + 1) * 128], ident[:])
                    ins.then_inc(x_transposed, 1)

                def project_v(s, r, g, quad, i):
                    wait(pe, v_ready, (s - r) + 4 * quad + i)
                    if isinstance(g, int) and g == 0 and i == 0:
                        pe.wait_ge(weights_split, split_by[quad, 2])
                    cols = slice(quad * QW, (quad + 1) * QW)
                    for k in range(KD):
                        ins = matmul3(nc, V_[:], (xT_hi[:, k, i * S:(i + 1) * S], xT_lo[:, k, i * S:(i + 1) * S]), (WH[:, 2, k, cols], WL[:, 2, k, cols]),
                                      first=(k == 0), last=(k == KD - 1))
                    ins.then_inc(v_projected, 1)

                def project(s, r, g):
                    if r == 0:
                        pe.wait_ge(xT_split, g + 1)
                    if isinstance(g, int) and g == 0 and r % 4 == 0:
                        pe.wait_ge(weights_split, split_by[r // 4, 1])
                    cols = slice(r * DK0, (r + 1) * DK0)
                    for w in range(2):
                        wait(pe, products[w], 2 * s)
                        for k in range(KD):
                            ins = matmul3(nc, QK[w][:], (WH[:, w, k, cols], WL[:, w, k, cols]), (xT_hi[:, k, :], xT_lo[:, k, :]),
                                          first=(k == 0), last=(k == KD - 1))
                        ins.then_inc(projected[w], 1)
                        if w < len(v_at(r)):
                            project_v(s, r, g, *v_at(r)[w])

                def transpose_p(u):
                    pe.wait_ge(probs_ready, u + 1)
                    wait(pe, oT_lo_ready, u)
                    for i in range(GROUP):
                        ins = nc.tensor.transpose(PO[:, i * 128:(i + 1) * 128], P[:, i, :], ident[:])
                    ins.then_inc(p_transposed, 1)

                def out_project(u, ur, ug):
                    pe.wait_ge(oT_lo_ready, u + 1)
                    if ur == 0:
                        wait(pe, out_added, 4 * ug - 2 if isinstance(ug, int) else 4 * ug + (-2))
                        for i in range(2):
                            nc.tensor.matmul(OUT[i][:], zeros_b[:], four(zeros_b[:]), start=True, stop=True)
                    for i in range(GROUP):
                        for lhs, rhs in ((oT_hi, WO_lo), (oT_lo, WO_hi), (oT_hi, WO_hi)):
                            ins = nc.tensor.matmul(OUT[i // 2][:, i % 2 * D:(i % 2 + 1) * D], lhs[:, i, :], rhs[:, ur, :], start=False, stop=True, skip_group_check=True)
                    ins.then_inc(out_projected, 1)

                def score(u, p):
                    for w in range(2):
                        pe.wait_ge(roped_sum[w], u + 1)
                    wait(pe, exps_done, u)
                    nc.tensor.matmul(SC[:], ident_b[:], four(mask[:]), start=True, stop=True)
                    for i in range(GROUP):
                        toks = slice(i * S, (i + 1) * S)
                        ins = nc.tensor.matmul(SC[:, i * 128:(i + 1) * 128], roped[0][:, p, toks], roped[1][:, p, toks], start=False, stop=True, skip_group_check=True)
                    ins.then_inc(scored, 1)

                def weigh(u, ur):
                    pe.wait_ge(PT_ready, u + 1)
                    if ur % 4 == 0:
                        pe.wait_ge(v_ready, u + GROUP)
                    h = ur % 4
                    for i in range(GROUP):
                        ins = nc.tensor.matmul(PO[:, i * 128:(i + 1) * 128], V[:, ur // 4 % 2, i, h * 128:(h + 1) * 128], PT[:, i, :], start=True, stop=True)
                    ins.then_inc(pv_done, 1)

                def step(s, r, g):
                    if live(s, STEPS):
                        project(s, r, g)
                    if r in (5, 7, 9, 11) and live(g + 1, NG):
                        transpose_x(g * GROUP + GROUP + (r - 5) // 2)
                    if live(s - 3, STEPS):
                        if isinstance(s, int) and s <= HEADS0 and (s - 3) % 4 == 0:
                            pe.wait_ge(weights_split, split_by[(s - 3) // 4, 3])
                        out_project(s - 3, (r - 3) % HEADS0, g if r >= 3 else g - 1)
                    if live(s - 2, STEPS):
                        transpose_p(s - 2)
                    if live(s - 1, STEPS):
                        score(s - 1, (r + 1) % 2)
                    if live(s - 2, STEPS):
                        weigh(s - 2, (r - 2) % HEADS0)

                pe.wait_ge(first_loaded, 48)
                for b in range(GROUP):
                    transpose_x(b)
                pe.wait_ge(consts_made, 3)
                run(pe, step)


def live(u, n=B):
    return not isinstance(u, int) or 0 <= u < n


def run_pairs(eng, step, extra, peeled=1):
    for s in range(2 * peeled):
        step(s, s % 2)
    with eng.Fori(peeled, B // 2 - 1) as i:
        for j in range(2):
            step(i * 2 + j, j)
    for s in range(B - 2, B + extra):
        step(s, s % 2)


def phase_retention(nc, a, sem, sb_, bank, X, ident, mean, var_eps, rstd, minus_half, stats, ln_tmp, ahead, ahead_loaded):
    local = ExitStack()
    with local:
        def sb(name, shape, dt=F32):
            return sb_(name, shape, dt, local)

        H_ = 2
        V = sb("ret_V", [128, H_, B, 128])
        gate = sb("ret_gate", [128, B, D])
        O = sb("ret_O", [128, B, D])
        AT = sb("ret_AT", [128, H_, 128])
        decay = sb("ret_decay", [128, H_, 128])
        Wh = sb("ret_Wh", [128, H_, 128])
        WhT = sb("ret_WhT", [128, H_, 128])
        G = sb("ret_G", [128, H_, 128])
        w_in = sb("ret_w_in", [128, 2, KD, D])
        w_hi = sb("ret_w_hi", [128, 2, KD, D], F32R)
        w_lo = sb("ret_w_lo", [128, 2, KD, D], F32R)
        gn = sb("ret_gn", [128, 2, D])
        ctx_all = sb("ret_ctx_all", [128, KD, B * S])
        ctxT = sb("ret_ctxT", [128, 2, H_, 128])
        xn = sb("ret_xn", [128, 2, D])
        xT_full = sb("ret_xT_full", [128, 2, KD, 128])
        xT_hi = sb("ret_xT_hi", [128, 2, KD, 128], F32R)
        xT_lo = sb("ret_xT_lo", [128, 2, KD, 128], F32R)
        TT = sb("ret_TT", [128, 2, H_, 128])
        zeros = sb("ret_zeros", [128, D], BF16)

        consts = sem("ret_consts")
        ctx_loaded = sem("ret_ctx_loaded")
        ctx_copied = sem("ret_ctx_copied")
        w_rounded = sem("ret_w_rounded")
        w_split = sem("ret_w_split")
        zeroed = sem("ret_zeroed")
        gram_done = sem("ret_gram_done")
        G_ready = sem("ret_G_ready")
        ln = sem("ret_ln")
        rstd_ready = sem("ret_rstd")
        xn_ready = sem("ret_xn_ready")
        transposed = sem("ret_transposed")
        full_ready = sem("ret_full_ready")
        hi_ready = sem("ret_hi_ready")
        lo_ready = sem("ret_lo_ready")
        T_done = sem("ret_T_done")
        gate_done = sem("ret_gate_done")
        TT_ready = sem("ret_TT_ready")
        V_ready = sem("ret_V_ready")
        gate_ready = sem("ret_gate_ready")
        scored = sem("ret_scored")
        AT_ready = sem("ret_AT_ready")

        with nc.Block() as block:
            @block.sync
            def _(sp):
                for dst, src in ((WhT[:], a["WhT"]), (Wh[:], a["L0_xattn_Wh"].rearrange("h e d -> e h d")),
                                 (w_in[:, 0], a["L0_xattn_wg_w"].rearrange("(k p) n -> p k n", p=128)),
                                 (w_in[:, 1], a["L0_xattn_wo_w"].rearrange("(k p) n -> p k n", p=128)),
                                 (decay[:], a["decayT"]),
                                 (gn[:, 0, :], a["L0_xattn_gn_gamma"].rearrange("(a n) -> a n", a=1).broadcast_to([128, D])),
                                 (gn[:, 1, :], a["L0_xattn_gn_beta"].rearrange("(a n) -> a n", a=1).broadcast_to([128, D]))):
                    sp.dma_start(dst, src).then_inc(consts, 16)
                sp.dma_start(ctx_all[:], a["ctxT"].rearrange("(k p) n -> p k n", p=128)).then_inc(ctx_loaded, 16)
                for dst, src in ahead:
                    sp.dma_start(dst, src).then_inc(ahead_loaded, 16)

            @block.gpsimd
            def _(pool):
                pool.wait_ge(ln, 7)
                nc.gpsimd.tensor_tensor(rstd[:], var_eps[:], minus_half[:], ALU.pow).then_inc(rstd_ready, 1)

            @block.scalar
            def _(act):
                act.wait_ge(consts, 112)
                nc.scalar.activation(w_hi[:], w_in[:], ACT.Copy).then_inc(w_rounded, 1)
                act.wait_ge(gram_done, 1)
                nc.scalar.activation(G[:].rearrange("p h n -> p (h n)"), bank[7][:, 0:256], ACT.Copy).then_inc(G_ready, 1)

                def step(s, j):
                    if live(s):
                        act.wait_ge(transposed, s + 1)
                        wait(act, gate_done, s - 1)
                        nc.scalar.activation(flat(xT_full[:, j]), bank[j][:, 0:256], ACT.Copy).then_inc(full_ready, 1)
                        nc.scalar.activation(flat(xT_hi[:, j]), bank[j][:, 0:256], ACT.Copy).then_inc(hi_ready, 1)
                    if live(s - 1):
                        act.wait_ge(T_done, s)
                        wait(act, scored, s - 2)
                        nc.scalar.activation(flat(TT[:, 1 - j]), bank[3 - j][:, 0:256], ACT.Copy).then_inc(TT_ready, 1)
                run_pairs(act, step, 1)

            @block.vector
            def _(dve):
                n = finish_stats(nc, dve, ln, 0, stats, mean[:], var_eps[:], ln_tmp, LN_EPS)
                nc.vector.memset(zeros[:], 0.0).then_inc(zeroed, 1)
                dve.wait_ge(w_rounded, 1)
                nc.vector.tensor_tensor(w_lo[:], w_in[:], w_hi[:].bitcast(F32), ALU.subtract).then_inc(w_split, 1)
                dve.wait_ge(rstd_ready, 1)
                dve.wait_ge(ln, n)

                def normalise(b, j):
                    wait(dve, transposed, b - 1)
                    nc.vector.tensor_scalar(xn[:, j, :], batch(X, b), one(mean, b), one(rstd, b), ALU.subtract, ALU.mult).then_inc(xn_ready, 1)

                def copy_ctx(b, j):
                    wait(dve, scored, b - 1)
                    at = slice(b * S, (b + 1) * S) if isinstance(b, int) else bass.ds(b * S, S)
                    nc.vector.tensor_scalar(ctxT[:, j], ctx_all[:, :, at], 1.0, None, ALU.mult).then_inc(ctx_copied, 1)

                normalise(0, 0)
                dve.wait_ge(ctx_loaded, 16)

                def step(s, j):
                    if live(s + 1):
                        normalise(s + 1, 1 - j)
                    if live(s):
                        copy_ctx(s, j)
                    if live(s):
                        dve.wait_ge(hi_ready, s + 1)
                        nc.vector.tensor_tensor(flat(xT_lo[:, j]), flat(xT_full[:, j]), flat(xT_hi[:, j]).bitcast(F32), ALU.subtract).then_inc(lo_ready, 1)
                    if live(s - 1):
                        dve.wait_ge(gate_done, s)
                        v_out = V[:, :, s - 1, :] if isinstance(s, int) else V[:, :, bass.ds(s - 1, 1), :].rearrange("p h a n -> p h (a n)")
                        nc.vector.tensor_scalar(v_out, bank[5 - j][:, 256:512].rearrange("p (h n) -> p h n", h=H_), 1.0, None, ALU.mult).then_inc(V_ready, 1)
                        nc.vector.tensor_scalar(batch(gate, s - 1), bank[5 - j][:, 0:D], 0.0, None, ALU.max).then_inc(gate_ready, 1)
                run_pairs(dve, step, 1)
                dve.wait_ge(scored, B)
                nc.vector.tensor_tensor(flat(AT[:]), bank[6][:, 0:256], flat(decay[:]), ALU.mult).then_inc(AT_ready, 1)
                dve.wait_ge(AT_ready, 1)
                nc.vector.scalar_tensor_tensor(flat(AT[:]), flat(AT[:]), -1.0, flat(AT[:]), ALU.mult, ALU.max).then_inc(AT_ready, 1)
                dve.wait_ge(AT_ready, 2)
                nc.vector.tensor_scalar(flat(AT[:]), flat(AT[:]), 1.0, None, ALU.max).then_inc(AT_ready, 1)

            @block.tensor
            def _(pe):
                pe.wait_ge(consts, 112)
                for h in range(H_):
                    ins = nc.tensor.matmul(bank[7][:, h * 128:(h + 1) * 128], WhT[:, h, :], WhT[:, h, :], start=True, stop=True)
                ins.then_inc(gram_done, 1)
                pe.wait_ge(zeroed, 1)
                nc.tensor.matmul(bank[6][:, 0:256], zeros[:, 0:128], zeros[:], start=True, stop=True)
                pe.wait_ge(G_ready, 1)
                pe.wait_ge(w_split, 1)

                def step(s, j):
                    if live(s):
                        pe.wait_ge(xn_ready, s + 1)
                        wait(pe, hi_ready, s - 1)
                        for k in range(KD):
                            ins = nc.tensor.transpose(bank[j][:, k * 128:(k + 1) * 128], xn[:, j, k * 128:(k + 1) * 128], ident[:])
                        ins.then_inc(transposed, 1)
                    u, i = s - 1, 1 - j
                    if live(u):
                        pe.wait_ge(full_ready, u + 1)
                        pe.wait_ge(ctx_copied, u + 1)
                        wait(pe, TT_ready, u - 1)
                        for h in range(H_):
                            ins = nc.tensor.matmul(bank[2 + i][:, h * 128:(h + 1) * 128], G[:, h, :], xT_full[:, i, h, :], start=True, stop=True)
                        ins.then_inc(T_done, 1)
                        wait(pe, gate_ready, u - 1)
                        for h in range(H_):
                            nc.tensor.matmul(bank[4 + i][:, 256 + h * 128:256 + (h + 1) * 128], ctxT[:, i, h, :], Wh[:, h, :], start=True, stop=True)
                        pe.wait_ge(lo_ready, u + 1)
                        for k in range(KD):
                            ins = matmul3(nc, bank[4 + i][:, 0:D], (xT_hi[:, i, k, :], xT_lo[:, i, k, :]), (w_hi[:, 0, k, :], w_lo[:, 0, k, :]),
                                          first=(k == 0), last=(k == KD - 1))
                        ins.then_inc(gate_done, 1)
                    u = s - 2
                    if live(u):
                        pe.wait_ge(TT_ready, u + 1)
                        for h in range(H_):
                            ins = nc.tensor.matmul(bank[6][:, h * 128:(h + 1) * 128], ctxT[:, j, h, :], TT[:, j, h, :], start=False, stop=True, skip_group_check=True)
                        ins.then_inc(scored, 1)
                run_pairs(pe, step, 2)

        vproj = sem("ret_av_done")
        O_ready = sem("ret_O_ready")
        ln2 = sem("ret_ln2")
        rstd2_ready = sem("ret_rstd2")
        normed = sem("ret_normed")
        gained = sem("ret_gained")
        beta_added = sem("ret_beta_added")
        wy_ready = sem("ret_wy_ready")
        wy_transposed = sem("ret_wy_transposed")
        wyT_full_ready = sem("ret_wyT_full")
        wyT_ready = sem("ret_wyT_hi")
        wyT_lo_ready = sem("ret_wyT_lo")
        wo_done = sem("ret_wo_done")
        added = sem("ret_added")
        y = sb("ret_y", [128, 2, D])
        y_gained = sb("ret_y_gained", [128, 2, D])
        y_shaped = sb("ret_y_shaped", [128, 2, D])
        GROUP = 4
        with nc.Block() as block:
            @block.gpsimd
            def _(pool):
                pool.wait_ge(ln2, B + 7)
                nc.gpsimd.tensor_tensor(rstd[:], var_eps[:], minus_half[:], ALU.pow).then_inc(rstd2_ready, 1)

                def step(s, j):
                    if live(s):
                        pool.wait_ge(normed, s + 1)
                        nc.gpsimd.tensor_tensor(y_gained[:, j, :], y[:, j, :], gn[:, 0, :], ALU.mult).then_inc(gained, 1)
                        pool.wait_ge(gained, s + 1)
                        wait(pool, wy_ready, s - 1)
                        nc.gpsimd.tensor_tensor(y_shaped[:, j, :], y_gained[:, j, :], gn[:, 1, :], ALU.add).then_inc(beta_added, 1)
                run_pairs(pool, step, 0)

            @block.tensor
            def _(pe):
                for g in range(B // GROUP):
                    for h in range(H_):
                        wait(pe, O_ready, 2 * (g - 1) + h - 1)
                        nc.tensor.matmul(bank[2 * (g % 2) + h][:], AT[:, h, :], V[:, h, g * GROUP:(g + 1) * GROUP, :].rearrange("p b n -> p (b n)"),
                                         start=True, stop=True).then_inc(vproj, 1)

                def step(s, j):
                    if live(s):
                        pe.wait_ge(wy_ready, s + 1)
                        wait(pe, wyT_ready, s - 1)
                        for k in range(KD):
                            ins = nc.tensor.transpose(bank[4 + j][:, k * 128:(k + 1) * 128], xn[:, j, k * 128:(k + 1) * 128], ident[:])
                        ins.then_inc(wy_transposed, 1)
                    u, i = s - 1, 1 - j
                    if live(u):
                        pe.wait_ge(wyT_lo_ready, u + 1)
                        wait(pe, added, u - 1)
                        for k in range(KD):
                            ins = matmul3(nc, bank[6 + i][:, 0:D], (xT_hi[:, i, k, :], xT_lo[:, i, k, :]), (w_hi[:, 1, k, :], w_lo[:, 1, k, :]),
                                          first=(k == 0), last=(k == KD - 1))
                        ins.then_inc(wo_done, 1)
                run_pairs(pe, step, 1)

            @block.scalar
            def _(act):
                for g in range(B // GROUP):
                    for h in range(H_):
                        act.wait_ge(vproj, 2 * g + h + 1)
                        nc.scalar.activation(O[:, g * GROUP:(g + 1) * GROUP, h * 128:(h + 1) * 128],
                                             bank[2 * (g % 2) + h][:].rearrange("p (b n) -> p b n", b=GROUP), ACT.Copy).then_inc(O_ready, 1)

                def step(s, j):
                    if live(s):
                        act.wait_ge(wy_transposed, s + 1)
                        wait(act, wo_done, s - 1)
                        nc.scalar.activation(flat(xT_full[:, j]), bank[4 + j][:, 0:256], ACT.Copy).then_inc(wyT_full_ready, 1)
                        nc.scalar.activation(flat(xT_hi[:, j]), bank[4 + j][:, 0:256], ACT.Copy).then_inc(wyT_ready, 1)
                run_pairs(act, step, 0)

            @block.vector
            def _(dve):
                for g in range(B // GROUP):
                    dve.wait_ge(O_ready, 2 * g + 2)
                    for b in range(g * GROUP, (g + 1) * GROUP):
                        nc.vector.bn_stats(stats[:, b, :], O[:, b, :]).then_inc(ln2, 1)
                dve.wait_ge(ln2, B)
                n = finish_stats(nc, dve, ln2, B, stats, mean[:], var_eps[:], ln_tmp, 1e-3)
                dve.wait_ge(rstd2_ready, 1)
                dve.wait_ge(ln2, n)

                def norm(b, j):
                    wait(dve, beta_added, b - 1)
                    nc.vector.tensor_scalar(y[:, j, :], batch(O, b), one(mean, b), one(rstd, b), ALU.subtract, ALU.mult).then_inc(normed, 1)

                def apply_gate(b, j):
                    dve.wait_ge(beta_added, b + 1)
                    wait(dve, wy_transposed, b - 1)
                    nc.vector.tensor_tensor(xn[:, j, :], y_shaped[:, j, :], batch(gate, b), ALU.mult).then_inc(wy_ready, 1)

                norm(0, 0)
                norm(1, 1)
                apply_gate(0, 0)

                def step(s, j):
                    if live(s + 2):
                        norm(s + 2, j)
                    if live(s + 1):
                        apply_gate(s + 1, 1 - j)
                    if live(s):
                        dve.wait_ge(wyT_ready, s + 1)
                        nc.vector.tensor_tensor(flat(xT_lo[:, j]), flat(xT_full[:, j]), flat(xT_hi[:, j]).bitcast(F32), ALU.subtract).then_inc(wyT_lo_ready, 1)
                    if live(s - 1):
                        dve.wait_ge(wo_done, s)
                        nc.vector.tensor_tensor(batch(X, s - 1), bank[7 - j][:, 0:D], batch(X, s - 1), ALU.add).then_inc(added, 1)
                        dve.wait_ge(added, s)
                        nc.vector.bn_stats(batch(stats, s - 1), batch(X, s - 1))
                run_pairs(dve, step, 1)


def flat(ap):
    return ap.rearrange("p h n -> p (h n)")


def pair_count(s, j, i, ahead=-1):
    if ahead < 0:
        return (s - j) * 8 + (16 if i < j else 0)
    return (s - j) * 8 + (16 if j < i else 32)


def ctx_columns(a, b):
    view = a["ctxT"].rearrange("(k p) n -> p k n", p=128)
    return view[:, :, b * S:(b + 1) * S] if isinstance(b, int) else view[:, :, bass.ds(b * S, S)]

def phase_spline(nc, a, sem, sb_, bank, X, ident, mean, var_eps, rstd, minus_half, stats, ln_tmp, w, ahead_loaded, n_ahead):
    local = ExitStack()
    with local:
        def sb(name, shape, dt=F32):
            return sb_(name, shape, dt, local)

        NT, W, GRID, NC_ = 64, 4, 16, 8
        BIG = 1e30
        TABW = 2 * W * GRID + 1
        H = sb("sp_H", [128, B, D])
        XF = sb("sp_XF", [128, B, D])
        sign = sb("sp_sign", [128, B, D])
        wide = sb("sp_wide", [128, B, D])
        gb = w["sp_gb"]
        square = sb("sp_square", [128, B])
        rstd2 = sb("sp_rstd2", [128, B])
        rstd12 = sb("sp_rstd12", [128, B])
        slopes_in = w["sp_slopes"]
        slope_sum = sb("sp_slope_sum", [128, D])
        slope_neg = sb("sp_slope_neg", [128, D])
        slope_sign = sb("sp_slope_sign", [128, D])
        tile_score = sb("sp_tile_score", [128, B, NT])
        cluster_score = sb("sp_cluster_score", [128, B, NC_])
        rank = w["sp_rank"]
        best = sb("sp_best", [128, 2, B])
        cluster_hot = sb("sp_cluster_hot", [128, B, NC_])
        hot = sb("sp_hot", [128, B, NT])
        xs = sb("sp_xs", [128, B, W])
        lo_hi = sb("sp_lo_hi", [128, 2, B])
        shift = sb("sp_shift", [128, B])
        off = sb("sp_off", [128, B, NT])
        extreme = sb("sp_extreme", [128, 2, B, NT])
        tile_ext = sb("sp_tile_ext", [128, 2, NT])
        table = w["sp_table"]
        ext_table = sb("sp_ext_table", [NT, 2])
        hotT = sb("sp_hotT", [NT, B, 128])
        ext_found = sb("sp_ext_found", [128, B, 2])
        found = sb("sp_found", [128, B, TABW])
        span = sb("sp_span", [128, 2, B])
        u = sb("sp_u", [128, B, W])
        ge = sb("sp_ge", [128, B * W, GRID + 1])
        cell = sb("sp_cell", [128, B, W, GRID])
        picked = sb("sp_picked", [128, 2, B, W, GRID])
        coef = sb("sp_coef", [128, 4, B, W])

        stat = sem("sp_stat")
        rstd_ready = sem("sp_rstd_ready")
        ext_ready = sem("sp_ext_ready")
        ext_transposed = sem("sp_ext_transposed")
        table_ready = sem("sp_table_ready")
        hot_ready = sem("sp_hot_ready")
        xf_ready = sem("sp_xf_ready")
        summed = sem("sp_summed")
        pool_made = sem("sp_pool_made")
        RESIDUAL, POOL_WIDE, POOL_SPLINE = 5, 6, 7
        handed_over = sem("sp_handed_over")
        SHIFT, SLOPES, SPLINE = 1, 2, 3
        signed_dve = sem("sp_signed_dve")
        signed_pool = sem("sp_signed_pool")
        signs_ready = sem("sp_signs_ready")
        scores_ready = sem("sp_scores_ready")
        f_made = sem("sp_f_made")
        ext_found_ready = sem("sp_ext_found_ready")
        ext_looked_up = sem("sp_ext_looked_up")
        hot_transposed = sem("sp_hot_transposed")
        hotT_ready = sem("sp_hotT_ready")
        looked_up = sem("sp_looked_up")
        found_ready = sem("sp_found_ready")
        chain = sem("sp_chain")

        rows = lambda ap: ap.rearrange("p (a n) -> p a n", a=1).broadcast_to([128, B // 4, D])

        over = lambda ap, m: ap.rearrange("p (b n) -> p b n", n=1).broadcast_to([128, B, m])
        per_tile = lambda ap: ap.rearrange("p b (t j) -> p (b t) j", j=W)

        def hot_wide(some):
            n = some.stop - some.start
            return hot[:, some, :].rearrange("p b (t a) -> p (b t) a", a=1).broadcast_to([128, n * NT, W])

        POOL_FROM = 12

        with nc.Block() as block:
            @block.gpsimd
            def _(pool):
                pool.wait_ge(stat, 7)
                nc.gpsimd.tensor_tensor(rstd[:], var_eps[:], minus_half[:], ALU.pow).then_inc(rstd_ready, 1)
                pool.wait_ge(stat, 7 + 3)
                nc.gpsimd.tensor_tensor(rstd2[:], var_eps[:], minus_half[:], ALU.pow).then_inc(rstd_ready, 1)
                for i in range(2):
                    part = XF[:, (2 + i) * B // 4:(3 + i) * B // 4, :]
                    pool.wait_ge(xf_ready, 4 * (i + 1))
                    nc.gpsimd.tensor_tensor(part, part, rows(gb[:, 0, :]), ALU.mult).then_inc(pool_made, 1)
                    pool.wait_ge(pool_made, 2 * i + 1)
                    nc.gpsimd.tensor_tensor(part, part, rows(gb[:, 1, :]), ALU.add).then_inc(pool_made, 1)
                    pool.wait_ge(pool_made, 2 * i + 2)
                    pool.wait_ge(handed_over, SLOPES)
                    nc.gpsimd.tensor_tensor(sign[:, (2 + i) * B // 4:(3 + i) * B // 4, :], part, rows(slope_sign[:]), ALU.mult).then_inc(signed_pool, 1)
                pool.wait_ge(f_made, B)
                pool.wait_ge(xf_ready, B)
                nc.gpsimd.tensor_tensor(X[:], X[:], H[:], ALU.add).then_inc(pool_made, 1)
                pool.wait_ge(hot_ready, 1)
                pool.wait_ge(signed_pool, 2)
                own = slice(POOL_FROM, B)
                nc.gpsimd.tensor_tensor(per_tile(wide[:, own, :]), per_tile(XF[:, own, :]), hot_wide(own), ALU.mult).then_inc(pool_made, 1)
                pool.wait_ge(handed_over, SPLINE)
                nc.gpsimd.tensor_tensor(wide[:].rearrange("p b (t j) -> p b t j", j=W)[:, :, :, W - 1], hot[:], over(coef[:, 3, :, W - 1], NT), ALU.mult).then_inc(pool_made, 1)

            @block.vector
            def _(dve):
                count = [0]

                def link(ins):
                    count[0] += 1
                    ins.then_inc(chain, 1)
                    dve.wait_ge(chain, count[0])

                TT, TS, STT = nc.vector.tensor_tensor, nc.vector.tensor_scalar, nc.vector.scalar_tensor_tensor
                n = finish_stats(nc, dve, stat, 0, stats, mean[:], var_eps[:], ln_tmp, LN_EPS)
                dve.wait_ge(ahead_loaded, n_ahead)
                nc.vector.tensor_reduce(slope_sum[:, 0:D // 2], slopes_in[:, 0:D // 2, :], AX.X, ALU.add).then_inc(summed, 1)
                dve.wait_ge(stat, n)
                dve.wait_ge(rstd_ready, 1)
                n = second_norm(nc, dve, stat, n, var_eps[:], rstd[:], square[:], ln_tmp, LN_EPS)
                nc.vector.scalar_tensor_tensor(shift[:], mean[:], -1.0, rstd[:], ALU.mult, ALU.mult).then_inc(handed_over, 1)
                nc.vector.tensor_reduce(slope_sum[:, D // 2:], slopes_in[:, D // 2:, :], AX.X, ALU.add).then_inc(summed, 1)
                dve.wait_ge(summed, 2)
                link(TS(slope_neg[:], slope_sum[:], 0.0, None, ALU.is_lt))
                STT(slope_sign[:], slope_sum[:], 0.0, slope_neg[:], ALU.is_gt, ALU.subtract).then_inc(handed_over, 1)
                dve.wait_ge(handed_over, SLOPES)
                dve.wait_ge(rstd_ready, 2)
                TT(rstd12[:], rstd[:], rstd2[:], ALU.mult).then_inc(stat, 1)
                dve.wait_ge(stat, n + 1)
                quarter = lambda c: slice(c * B // 4, (c + 1) * B // 4)

                def norm(c):
                    for b in range(c * B // 4, (c + 1) * B // 4):
                        TS(XF[:, b, :], X[:, b, :], mean[:, b:b + 1], rstd12[:, b:b + 1], ALU.subtract, ALU.mult).then_inc(xf_ready, 1)

                def tile_scores(c):
                    dve.wait_ge(signs_ready, c + 1)
                    nc.vector.tensor_reduce(tile_score[:, quarter(c), :], sign[:, quarter(c), :].rearrange("p b (t j) -> p b t j", j=W), AX.X, ALU.add).then_inc(scores_ready, 1)

                norm(2)
                norm(3)
                for c in range(2):
                    norm(c)
                    dve.wait_ge(xf_ready, 4 * (c + 3))
                    part = XF[:, quarter(c), :]
                    link(TT(part, part, rows(gb[:, 0, :]), ALU.mult))
                    link(TT(part, part, rows(gb[:, 1, :]), ALU.add))
                    TT(sign[:, quarter(c), :], part, rows(slope_sign[:]), ALU.mult).then_inc(signed_dve, 1)
                for c in range(4):
                    tile_scores(c)
                dve.wait_ge(scores_ready, 4)
                link(nc.vector.tensor_reduce(cluster_score[:], tile_score[:].rearrange("p b (c t) -> p b c t", t=8), AX.X, ALU.add))
                col = lambda lo, m: rank[:, lo:lo + m].rearrange("p (a n) -> p a n", a=1).broadcast_to([128, B, m])
                link(STT(cluster_score[:], cluster_score[:], float(NC_), col(NT, NC_), ALU.mult, ALU.add))
                link(nc.vector.tensor_reduce(best[:, 0, :], cluster_score[:], AX.X, ALU.max))
                link(TT(cluster_hot[:], cluster_score[:], over(best[:, 0, :], NC_), ALU.is_equal))
                link(STT(tile_score[:], tile_score[:], float(NT), col(0, NT), ALU.mult, ALU.add))
                link(TS(cluster_hot[:], cluster_hot[:], 4096.0, None, ALU.mult))
                link(TT(tile_score[:].rearrange("p b (c t) -> p (b c) t", t=8), tile_score[:].rearrange("p b (c t) -> p (b c) t", t=8),
                        cluster_hot[:].rearrange("p b (c a) -> p (b c) a", a=1).broadcast_to([128, B * NC_, 8]), ALU.add))
                link(nc.vector.tensor_reduce(best[:, 1, :], tile_score[:], AX.X, ALU.max))
                TT(hot[:], tile_score[:], over(best[:, 1, :], NT), ALU.is_equal).then_inc(hot_ready, 1)
                dve.wait_ge(hot_ready, 1)
                own = slice(0, POOL_FROM)
                link(TT(per_tile(wide[:, own, :]), per_tile(XF[:, own, :]), hot_wide(own), ALU.mult))
                dve.wait_ge(pool_made, POOL_WIDE)
                link(nc.vector.tensor_reduce(xs[:], wide[:].rearrange("p b (t j) -> p b j t", j=W), AX.X, ALU.add))
                link(nc.vector.tensor_reduce(lo_hi[:, 0, :], xs[:], AX.X, ALU.min))
                link(nc.vector.tensor_reduce(lo_hi[:, 1, :], xs[:], AX.X, ALU.max))
                link(TS(off[:], hot[:], -BIG, BIG, ALU.mult, ALU.add))
                for i, sgn in ((0, ALU.add), (1, ALU.subtract)):
                    link(TT(extreme[:, i], hot[:], over(lo_hi[:, i, :], NT), ALU.mult))
                    link(TT(extreme[:, i], extreme[:, i], off[:], sgn))
                    link(nc.vector.tensor_reduce(tile_ext[:, i, :], extreme[:, i].rearrange("p b t -> p t b"), AX.X, (ALU.min, ALU.max)[i]))
                nc.vector.tensor_copy(tile_ext[:, 0, 0:1], tile_ext[:, 0, 0:1]).then_inc(ext_ready, 1)
                dve.wait_ge(ext_transposed, 1)
                for i in range(2):
                    nc.vector.tensor_reduce(ext_table[:, i:i + 1], bank[0][0:NT, i * 128:(i + 1) * 128], AX.X, (ALU.min, ALU.max)[i]).then_inc(table_ready, 1)
                dve.wait_ge(ext_looked_up, 1)
                nc.vector.tensor_copy(flat(ext_found[:]), bank[1][:, 0:2 * B]).then_inc(ext_found_ready, 1)
                dve.wait_ge(ext_found_ready, 1)
                dve.wait_ge(found_ready, B // 2)

                link(TT(span[:, 0, :], ext_found[:, :, 1], ext_found[:, :, 0], ALU.subtract))
                link(TS(span[:, 0, :], span[:, 0, :], 1e-8, None, ALU.add))
                link(nc.vector.reciprocal(span[:, 1, :], span[:, 0, :]))
                link(TT(u[:], xs[:], over(ext_found[:, :, 0], W), ALU.subtract))
                link(TT(u[:], u[:], over(span[:, 1, :], W), ALU.mult))
                link(TS(u[:], u[:], 0.0, float(np.float32(1.0 - 1e-6)), ALU.max, ALU.min))
                link(TS(u[:], u[:], float(GRID), None, ALU.mult))
                u_flat = u[:].rearrange("p b w -> p (b w)")
                link(TT(ge[:], u_flat.rearrange("p (n a) -> p n a", a=1).broadcast_to([128, B * W, GRID + 1]),
                        rank[:, NT + NC_:].rearrange("p (a g) -> p a g", a=1).broadcast_to([128, B * W, GRID + 1]), ALU.is_ge))
                cells = lambda ap: ap.rearrange("p b w g -> p (b w) g")
                link(TT(cells(cell[:]), ge[:, :, 0:GRID], ge[:, :, 1:GRID + 1], ALU.subtract))
                for i in range(2):
                    link(TT(picked[:, i], cell[:], found[:, :, 64 * i:64 * (i + 1)].rearrange("p b (w g) -> p b w g", w=W), ALU.mult))
                    link(nc.vector.tensor_reduce(coef[:, i], picked[:, i], AX.X, ALU.add))
                link(nc.vector.tensor_reduce(coef[:, 2].rearrange("p b w -> p (b w)"), ge[:, :, 1:GRID + 1], AX.X, ALU.add))
                link(TT(coef[:, 2], u[:], coef[:, 2], ALU.subtract))
                link(TT(coef[:, 2], coef[:, 2], coef[:, 1], ALU.mult))
                link(TT(coef[:, 2], coef[:, 2], coef[:, 0], ALU.add))
                TT(coef[:, 3], coef[:, 2], over(found[:, :, 128], W), ALU.mult).then_inc(handed_over, 1)
                dve.wait_ge(handed_over, SPLINE)
                for j in range(W - 1):
                    link(TT(wide[:].rearrange("p b (t j) -> p b t j", j=W)[:, :, :, j], hot[:], over(coef[:, 3, :, j], NT), ALU.mult))
                dve.wait_ge(pool_made, POOL_SPLINE)
                for g in range(4):
                    some = slice(g * B // 4, (g + 1) * B // 4)
                    link(TT(X[:, some, :], X[:, some, :], wide[:, some, :], ALU.add))
                    for b in range(some.start, some.stop):
                        nc.vector.bn_stats(stats[:, b, :], X[:, b, :])

            @block.tensor
            def _(pe):
                pe.wait_ge(hot_ready, 1)
                for g in range(4):
                    for b in range(4 * g, 4 * g + 4):
                        ins = nc.tensor.transpose(bank[1 + g][0:NT, b % 4 * 128:(b % 4 + 1) * 128], hot[:, b, :], ident[:])
                    ins.then_inc(hot_transposed, 1)
                for p in range(B // 2):
                    pe.wait_ge(hotT_ready, p // 2 + 1)
                    wait(pe, found_ready, p - 2)
                    for i in range(2):
                        ins = nc.tensor.matmul(bank[5 + p % 3][:, i * TABW:(i + 1) * TABW], hotT[:, 2 * p + i, :], table[:], start=True, stop=True)
                    ins.then_inc(looked_up, 1)
                pe.wait_ge(ext_ready, 1)
                for i in range(2):
                    ins = nc.tensor.transpose(bank[0][0:NT, i * 128:(i + 1) * 128], tile_ext[:, i, :], ident[:])
                ins.then_inc(ext_transposed, 1)
                pe.wait_ge(table_ready, 2)
                for b in range(B):
                    ins = nc.tensor.matmul(bank[1][:, 2 * b:2 * b + 2], hotT[:, b, :], ext_table[:], start=True, stop=True)
                ins.then_inc(ext_looked_up, 1)

            @block.scalar
            def _(act):
                act.wait_ge(handed_over, SHIFT)
                for b in range(B):
                    nc.scalar.activation(H[:, b, :], X[:, b, :], ACT.Identity, bias=shift[:, b:b + 1], scale=rstd[:, b:b + 1]).then_inc(f_made, 1)
                for c in range(4):
                    some = slice(c * B // 4, (c + 1) * B // 4)
                    if c < 2:
                        act.wait_ge(signed_dve, c + 1)
                    else:
                        act.wait_ge(signed_pool, c - 1)
                    nc.scalar.activation(sign[:, some, :], sign[:, some, :], ACT.Sign).then_inc(signs_ready, 1)
                for g in range(4):
                    act.wait_ge(hot_transposed, g + 1)
                    nc.scalar.activation(flat(hotT[:, 4 * g:4 * g + 4, :]), bank[1 + g][0:NT, :], ACT.Copy).then_inc(hotT_ready, 1)
                for p in range(B // 2):
                    act.wait_ge(looked_up, p + 1)
                    nc.scalar.activation(flat(found[:, 2 * p:2 * p + 2, :]), bank[5 + p % 3][:, 0:2 * TABW], ACT.Copy).then_inc(found_ready, 1)


def phase_window(nc, a, sem, sb_, bank, X, ident, mean, var_eps, rstd, minus_half, stats, ln_tmp, w, ahead_loaded, n_ahead):
    local = ExitStack()
    with local:
        def sb(name, shape, dt=F32):
            return sb_(name, shape, dt, local)

        NH, DH, VW = 16, 16, 17
        wqk = w["win_wqk"]
        w_in = w["win_w_in"]
        w_hi = sb("win_w_hi", [128, 2, KD, D], F32R)
        w_lo = sb("win_w_lo", [128, 2, KD, D], F32R)
        band_f = w["win_band_in"]
        band = sb("win_band", [128, 4, 128], BF16)
        ident_b = sb("win_ident_b", [128, 128], BF16)
        parity = w["win_parity"]
        xn = sb("win_xn", [128, 2, D])
        xT_full = sb("win_xT_full", [128, KD, 128])
        xT_hi = sb("win_xT_hi", [128, KD, 128], F32R)
        xT_lo = sb("win_xT_lo", [128, KD, 128], F32R)
        q_hi = sb("win_q_hi", [128, 2, KD, 128], F32R)
        q_lo = sb("win_q_lo", [128, 2, KD, 128], F32R)
        k_hi = sb("win_k_hi", [128, 2, KD, 2, 128], F32R)
        k_lo = sb("win_k_lo", [128, 2, KD, 2, 128], F32R)
        V = sb("win_V", [128, 2, NH, VW])
        P = sb("win_P", [128, 2, 4, 128])
        PT = sb("win_PT", [128, 2, 4, 128])
        neg_max = sb("win_neg_max", [128, 4, 4])
        inv = sb("win_inv", [128, 2, NH])
        o = sb("win_o", [128, 2, D])
        oT_hi = sb("win_oT_hi", [128, KD, 128], F32R)
        oT_lo = sb("win_oT_lo", [128, KD, 128], F32R)
        oT_full = sb("win_oT_full", [128, KD, 128])

        made = sem("win_made")
        w_rounded = sem("win_w_rounded")
        ln = sem("win_ln")
        rstd_ready = sem("win_rstd_ready")
        xn_ready = sem("win_xn_ready")
        x_transposed = sem("win_x_transposed")
        xT_full_ready = sem("win_xT_full_ready")
        xT_hi_ready = sem("win_xT_hi_ready")
        xT_lo_ready = sem("win_xT_lo_ready")
        qk_projected = sem("win_qk_projected")
        v_projected = sem("win_v_projected")
        qk_rounded = sem("win_qk_rounded")
        qk_ready = sem("win_qk_ready")
        V_ready = sem("win_V_ready")
        scored = sem("win_scored")
        max_found = sem("win_max_found")
        exps_done = sem("win_exps_done")
        p_transposed = sem("win_p_transposed")
        PT_ready = sem("win_PT_ready")
        weighed = sem("win_weighed")
        inv_ready = sem("win_inv_ready")
        o_ready = sem("win_o_ready")
        o_transposed = sem("win_o_transposed")
        oT_full_ready = sem("win_oT_full_ready")
        oT_hi_ready = sem("win_oT_hi_ready")
        oT_lo_ready = sem("win_oT_lo_ready")
        out_projected = sem("win_out_projected")
        added = sem("win_added")

        QK, SC, PTB, OB, VB, MISC = bank[0], (bank[1], bank[2]), (bank[3], bank[4]), bank[5], bank[6], bank[7]
        STEPS = B * 4

        with nc.Block() as block:
            @block.gpsimd
            def _(pool):
                pool.wait_ge(ln, 7)
                nc.gpsimd.tensor_tensor(rstd[:], var_eps[:], minus_half[:], ALU.pow).then_inc(rstd_ready, 1)

            def run(eng, step, extra, first=None):
                for q in range(4):
                    step(q, q, 0, 0)
                for q in range(4):
                    step(4 + q, q, 1, 1)
                with eng.Fori(1, B // 2 - 1) as i:
                    for j in range(2):
                        for q in range(4):
                            step(i * 8 + 4 * j + q, q, i * 2 + j, j)
                for b in (B - 2, B - 1):
                    for q in range(4):
                        step(4 * b + q, q, b, b % 2)
                for x in range(extra):
                    step(STEPS + x, x % 4, B + x // 4, x // 4 % 2)

            @block.scalar
            def _(act):
                act.wait_ge(ahead_loaded, n_ahead)
                nc.scalar.activation(w_hi[:], w_in[:], ACT.Copy).then_inc(w_rounded, 1)

                def take_xT(b):
                    act.wait_ge(x_transposed, b + 1)
                    wait(act, v_projected, b)
                    nc.scalar.activation(flat(xT_full[:]), VB[:, D:2 * D], ACT.Copy).then_inc(xT_full_ready, 1)
                    nc.scalar.activation(flat(xT_hi[:]), VB[:, D:2 * D], ACT.Copy).then_inc(xT_hi_ready, 1)

                def take_qk(b, j):
                    act.wait_ge(qk_projected, b + 1)
                    wait(act, scored, 4 * b - 4)
                    nc.scalar.activation(flat(q_hi[:, j]), QK[:, 0:D], ACT.Copy, scale=1.0 / DH ** 0.5).then_inc(qk_rounded, 1)
                    for par in range(2):
                        nc.scalar.activation(k_hi[:, j, :, par, :], QK[:, D:2 * D].rearrange("p (k n) -> p k n", k=KD), ACT.Copy,
                                             scale=parity[:, par:par + 1]).then_inc(qk_rounded, 1)

                def take_v(b, j):
                    act.wait_ge(v_projected, b + 1)
                    wait(act, weighed, 4 * b - 4)
                    nc.scalar.activation(V[:, j, :, 0:DH], VB[:, 0:D].rearrange("p (h n) -> p h n", h=NH), ACT.Copy).then_inc(V_ready, 1)

                def exps(t, q):
                    act.wait_ge(max_found, t + 1)
                    wait(act, p_transposed, t - 1)
                    for h in range(4):
                        ins = nc.scalar.activation(P[:, q % 2, h, :], SC[q % 2][:, h * 128:(h + 1) * 128], ACT.Exp, bias=neg_max[:, q, h:h + 1])
                    ins.then_inc(exps_done, 1)

                def take_oT(b):
                    act.wait_ge(o_transposed, b + 1)
                    wait(act, out_projected, b)
                    nc.scalar.activation(flat(oT_full[:]), MISC[:, D:2 * D], ACT.Copy).then_inc(oT_full_ready, 1)
                    nc.scalar.activation(flat(oT_hi[:]), MISC[:, D:2 * D], ACT.Copy).then_inc(oT_hi_ready, 1)

                take_xT(0)
                take_qk(0, 0)
                take_v(0, 0)

                def step(t, q, b, j):
                    if q == 0 and live(b - 2):
                        take_oT(b - 2)
                    if q == 1 and live(b + 1):
                        take_xT(b + 1)
                    if q == 2 and live(b + 1):
                        take_qk(b + 1, 1 - j)
                    if q == 3 and live(b + 1):
                        take_v(b + 1, 1 - j)
                    if live(t, STEPS):
                        exps(t, q)
                run(act, step, 5)

            @block.vector
            def _(dve):
                n = finish_stats(nc, dve, ln, 0, stats, mean[:], var_eps[:], ln_tmp, LN_EPS)
                dve.wait_ge(ahead_loaded, n_ahead)
                for h in range(4):
                    nc.vector.tensor_copy(band[:, h, :], band_f[:]).then_inc(made, 1)
                nc.vector.tensor_copy(ident_b[:], ident[:]).then_inc(made, 1)
                nc.vector.memset(V[:], 1.0).then_inc(made, 1)
                dve.wait_ge(w_rounded, 1)
                nc.vector.tensor_tensor(w_lo[:], w_in[:], w_hi[:].bitcast(F32), ALU.subtract).then_inc(made, 1)
                dve.wait_ge(ln, n)
                dve.wait_ge(rstd_ready, 1)

                def normalise(b, j):
                    wait(dve, x_transposed, b - 1)
                    nc.vector.tensor_scalar(xn[:, j, :], batch(X, b), one(mean, b), one(rstd, b), ALU.subtract, ALU.mult).then_inc(xn_ready, 1)

                def split_xT(b):
                    dve.wait_ge(xT_hi_ready, b + 1)
                    nc.vector.tensor_tensor(flat(xT_lo[:]), flat(xT_full[:]), flat(xT_hi[:]).bitcast(F32), ALU.subtract).then_inc(xT_lo_ready, 1)

                def split_qk(b, j):
                    dve.wait_ge(qk_rounded, 3 * b + 3)
                    nc.vector.scalar_tensor_tensor(flat(q_lo[:, j]), QK[:, 0:D], 1.0 / DH ** 0.5, flat(q_hi[:, j]).bitcast(F32), ALU.mult, ALU.subtract).then_inc(qk_ready, 1)
                    for par in range(2):
                        nc.vector.scalar_tensor_tensor(k_lo[:, j, :, par, :], QK[:, D:2 * D].rearrange("p (k n) -> p k n", k=KD), parity[:, par:par + 1],
                                                       k_hi[:, j, :, par, :].bitcast(F32), ALU.mult, ALU.subtract).then_inc(qk_ready, 1)

                def find_max(t, q):
                    dve.wait_ge(scored, t + 1)
                    nc.vector.tensor_reduce(neg_max[:, q, :], SC[q % 2][:].rearrange("p (h n) -> p h n", h=4), AX.X, ALU.max, negate=True).then_inc(max_found, 1)

                def take_PT(t, q):
                    dve.wait_ge(p_transposed, t + 1)
                    wait(dve, weighed, t - 1)
                    nc.vector.tensor_copy(flat(PT[:, q % 2]), PTB[q % 2][:]).then_inc(PT_ready, 1)

                def norm_out(b, j):
                    dve.wait_ge(weighed, 4 * b + 4)
                    heads = OB[:, 0:NH * VW].rearrange("p (h n) -> p h n", h=NH)
                    nc.vector.reciprocal(inv[:, j, :], heads[:, :, DH]).then_inc(inv_ready, 1)
                    dve.wait_ge(inv_ready, b + 1)
                    wait(dve, o_transposed, b - 1)
                    nc.vector.tensor_tensor(o[:, j, :].rearrange("p (h n) -> p h n", h=NH), heads[:, :, 0:DH],
                                            inv[:, j, :].rearrange("p (h n) -> p h n", n=1).broadcast_to([128, NH, DH]), ALU.mult).then_inc(o_ready, 1)

                def split_oT(b):
                    dve.wait_ge(oT_hi_ready, b + 1)
                    nc.vector.tensor_tensor(flat(oT_lo[:]), flat(oT_full[:]), flat(oT_hi[:]).bitcast(F32), ALU.subtract).then_inc(oT_lo_ready, 1)

                def add_out(b):
                    dve.wait_ge(out_projected, b + 1)
                    nc.vector.tensor_tensor(batch(X, b), MISC[:, 0:D], batch(X, b), ALU.add).then_inc(added, 1)
                    dve.wait_ge(added, b + 1)
                    nc.vector.bn_stats(batch(stats, b), batch(X, b))

                normalise(0, 0)
                split_xT(0)
                split_qk(0, 0)
                normalise(1, 1)

                def step(t, q, b, j):
                    if live(t, STEPS):
                        find_max(t, q)
                    if q == 0 and live(b - 2):
                        split_oT(b - 2)
                    if q == 2 and live(b - 1):
                        norm_out(b - 1, 1 - j)
                    if live(t - 2, STEPS):
                        take_PT(t - 2, (q + 2) % 4)
                    if q == 1 and live(b + 1):
                        split_xT(b + 1)
                    if q == 2 and live(b + 1):
                        split_qk(b + 1, 1 - j)
                    if q == 3 and live(b + 2):
                        normalise(b + 2, j)
                    if q == 1 and live(b - 2):
                        add_out(b - 2)
                run(dve, step, 8)

            @block.tensor
            def _(pe):
                def transpose_x(b, j):
                    pe.wait_ge(xn_ready, b + 1)
                    wait(pe, V_ready, b)
                    for k in range(KD):
                        ins = nc.tensor.transpose(VB[:, D + k * 128:D + (k + 1) * 128], xn[:, j, k * 128:(k + 1) * 128], ident[:])
                    ins.then_inc(x_transposed, 1)

                def project_qk(b):
                    pe.wait_ge(xT_full_ready, b + 1)
                    wait(pe, qk_ready, 3 * b)
                    for c in range(4):
                        for k in range(KD):
                            ins = nc.tensor.matmul(QK[:, c * 128:(c + 1) * 128], wqk[:, k, c * 128:(c + 1) * 128], xT_full[:, k, :],
                                                   start=(k == 0), stop=(k == KD - 1))
                    ins.then_inc(qk_projected, 1)

                def project_v(b):
                    pe.wait_ge(xT_lo_ready, b + 1)
                    wait(pe, V_ready, b)
                    for k in range(KD):
                        ins = matmul3(nc, VB[:, 0:D], (xT_hi[:, k, :], xT_lo[:, k, :]), (w_hi[:, 0, k, :], w_lo[:, 0, k, :]),
                                      first=(k == 0), last=(k == KD - 1))
                    ins.then_inc(v_projected, 1)

                def score(t, q, b, j):
                    if q == 0:
                        pe.wait_ge(qk_ready, 3 * b + 3)
                    wait(pe, exps_done, t - 1)
                    dst = SC[q % 2]
                    nc.tensor.matmul(dst[:], ident_b[:], flat(band[:]), start=True, stop=True)
                    for pair in range(2):
                        rows = slice(32 * q, 32 * q + 32)
                        for lhs, rhs in ((q_hi, k_lo), (q_lo, k_hi), (q_hi, k_hi)):
                            ins = nc.tensor.matmul(dst[:, pair * 256:(pair + 1) * 256], lhs[rows, j, pair, :], rhs[rows, j, pair, :, :].rearrange("p a n -> p (a n)"),
                                                   start=False, stop=True, skip_group_check=True)
                    ins.then_inc(scored, 1)

                def transpose_p(t, q):
                    pe.wait_ge(exps_done, t + 1)
                    wait(pe, PT_ready, t - 1)
                    for h in range(4):
                        ins = nc.tensor.transpose(PTB[q % 2][:, h * 128:(h + 1) * 128], P[:, q % 2, h, :], ident[:])
                    ins.then_inc(p_transposed, 1)

                def weigh(t, q, b, j):
                    pe.wait_ge(PT_ready, t + 1)
                    if q == 0:
                        pe.wait_ge(V_ready, b + 1)
                        wait(pe, o_ready, b)
                    for h in range(4):
                        head = 8 * (h // 2) + 2 * q + h % 2
                        ins = nc.tensor.matmul(OB[:, head * VW:(head + 1) * VW], PT[:, q % 2, h, :], V[:, j, head, :], start=True, stop=True)
                    ins.then_inc(weighed, 1)

                def transpose_o(b, j):
                    pe.wait_ge(o_ready, b + 1)
                    wait(pe, oT_hi_ready, b)
                    wait(pe, added, b)
                    for k in range(KD):
                        ins = nc.tensor.transpose(MISC[:, D + k * 128:D + (k + 1) * 128], o[:, j, k * 128:(k + 1) * 128], ident[:])
                    ins.then_inc(o_transposed, 1)

                def project_out(b):
                    pe.wait_ge(oT_lo_ready, b + 1)
                    for k in range(KD):
                        ins = matmul3(nc, MISC[:, 0:D], (oT_hi[:, k, :], oT_lo[:, k, :]), (w_hi[:, 1, k, :], w_lo[:, 1, k, :]),
                                      first=(k == 0), last=(k == KD - 1))
                    ins.then_inc(out_projected, 1)

                pe.wait_ge(ahead_loaded, n_ahead)
                transpose_x(0, 0)
                project_qk(0)
                pe.wait_ge(made, 7)
                project_v(0)

                def step(t, q, b, j):
                    if live(t, STEPS):
                        score(t, q, b, j)
                    if live(t - 3, STEPS):
                        weigh(t - 3, (q + 1) % 4, b if q == 3 else b - 1, j if q == 3 else 1 - j)
                    if live(t - 2, STEPS):
                        transpose_p(t - 2, (q + 2) % 4)
                    if q == 0:
                        if live(b + 1):
                            transpose_x(b + 1, 1 - j)
                        if live(b - 2):
                            project_out(b - 2)
                    if q == 1 and live(b + 1):
                        project_qk(b + 1)
                    if q == 2 and live(b + 1):
                        project_v(b + 1)
                    if q == 3 and live(b - 1):
                        transpose_o(b - 1, 1 - j)
                run(pe, step, 8)

def phase_cross(nc, a, sem, sb_, bank, X, ident, mean, var_eps, rstd, minus_half, stats, ln_tmp, w):
    local = ExitStack()
    with local:
        def sb(name, shape, dt=F32):
            return sb_(name, shape, dt, local)

        wqk = w["cr_wqk"]
        w_in = w["cr_w_in"]
        w_hi = sb("cr_w_hi", [128, 2, KD, D], F32R)
        w_lo = sb("cr_w_lo", [128, 2, KD, D], F32R)
        xn = sb("cr_xn", [128, 2, D])
        xT_full = sb("cr_xT_full", [128, 2, KD, 128])
        xT_hi = sb("cr_xT_hi", [128, 2, KD, 128], F32R)
        xT_lo = sb("cr_xT_lo", [128, 2, KD, 128], F32R)
        qT = sb("cr_qT", [128, KD, 128])
        kT = sb("cr_kT", [128, 2, KD, 2, 128])
        V = sb("cr_V", [128, 2, 2, D])
        P = sb("cr_P", [128, 2, 128])
        PT = sb("cr_PT", [128, 2, 128])
        oT_full = sb("cr_oT_full", [128, KD, 128])
        oT_hi = sb("cr_oT_hi", [128, KD, 128], F32R)
        oT_lo = sb("cr_oT_lo", [128, KD, 128], F32R)
        neg_max = sb("cr_neg_max", [128, 2])
        exp_sum = sb("cr_exp_sum", [128, 2])
        inv_sum = sb("cr_inv_sum", [128, 2])

        ctx_loaded = [sem("cr_ctx0"), sem("cr_ctx1")]
        w_rounded = sem("cr_w_rounded")
        w_split = sem("cr_w_split")
        ln = sem("cr_ln")
        rstd_ready = sem("cr_rstd_ready")
        xn_ready = sem("cr_xn_ready")
        x_transposed = sem("cr_x_transposed")
        xT_full_ready = sem("cr_xT_full_ready")
        xT_hi_ready = sem("cr_xT_hi_ready")
        xT_lo_ready = sem("cr_xT_lo_ready")
        qk_projected = sem("cr_qk_projected")
        qk_ready = sem("cr_qk_ready")
        v_projected = sem("cr_v_projected")
        V_ready = sem("cr_V_ready")
        scored = sem("cr_scored")
        max_found = sem("cr_max_found")
        exps_done = sem("cr_exps_done")
        inv_ready = sem("cr_inv_ready")
        probs_ready = sem("cr_probs_ready")
        p_transposed = sem("cr_p_transposed")
        PT_ready = sem("cr_PT_ready")
        weighed = sem("cr_weighed")
        oT_full_ready = sem("cr_oT_full_ready")
        oT_hi_ready = sem("cr_oT_hi_ready")
        oT_lo_ready = sem("cr_oT_lo_ready")
        out_projected = sem("cr_out_projected")
        added = sem("cr_added")
        XB, QKB, VB, PB, OB, SB_, OUT, _ = bank

        with nc.Block() as block:
            @block.sync
            def _(sp):
                def step(s, j):
                    if live(s):
                        wait(sp, weighed, s - 1)
                        sp.dma_start(kT[:, j, :, 0, :], ctx_columns(a, s)).then_inc(ctx_loaded[j], 16)
                        rows = a["ctx_2048"][s] if isinstance(s, int) else a["ctx_2048"][bass.ds(s, 1)].rearrange("a t d -> (a t) d")
                        sp.dma_start(V[:, j, 0, :], rows).then_inc(ctx_loaded[j], 16)
                run_pairs(sp, step, 0)

            @block.gpsimd
            def _(pool):
                pool.wait_ge(ln, 7)
                nc.gpsimd.tensor_tensor(rstd[:], var_eps[:], minus_half[:], ALU.pow).then_inc(rstd_ready, 1)

            @block.scalar
            def _(act):
                nc.scalar.activation(w_hi[:], w_in[:], ACT.Copy).then_inc(w_rounded, 1)

                def step(s, j):
                    u = s - 2
                    if live(u):
                        act.wait_ge(max_found, u + 1)
                        wait(act, p_transposed, u)
                        nc.scalar.activation(flat(P[:]), SB_[:, 0:2 * 128], ACT.Exp, bias=neg_max[:, j:j + 1], accum_out=exp_sum[:, j:j + 1]).then_inc(exps_done, 1)
                    if live(s):
                        act.wait_ge(x_transposed, s + 1)
                        wait(act, v_projected, s - 1)
                        nc.scalar.activation(flat(xT_full[:, j]), XB[:, 0:D], ACT.Copy).then_inc(xT_full_ready, 1)
                        nc.scalar.activation(flat(xT_hi[:, j]), XB[:, 0:D], ACT.Copy).then_inc(xT_hi_ready, 1)
                    u, i = s - 1, 1 - j
                    if live(u):
                        act.wait_ge(qk_projected, u + 1)
                        wait(act, scored, u)
                        nc.scalar.activation(flat(qT[:]), QKB[:, 0:D], ACT.Copy, scale=1.0 / D ** 0.5).then_inc(qk_ready, 1)
                        nc.scalar.activation(kT[:, i, :, 1, :], QKB[:, D:2 * D].rearrange("p (k n) -> p k n", k=KD), ACT.Copy).then_inc(qk_ready, 1)
                    u = s - 2
                    if live(u):
                        act.wait_ge(p_transposed, u + 1)
                        wait(act, weighed, u)
                        nc.scalar.activation(flat(PT[:]), PB[:, 0:2 * 128], ACT.Copy).then_inc(PT_ready, 1)
                    u, i = s - 1, 1 - j
                    if live(u):
                        act.wait_ge(v_projected, u + 1)
                        wait(act, weighed, u - 1)
                        nc.scalar.activation(V[:, i, 1, :], VB[:, 0:D], ACT.Copy).then_inc(V_ready, 1)
                    u = s - 2
                    if live(u):
                        act.wait_ge(weighed, u + 1)
                        wait(act, out_projected, u)
                        nc.scalar.activation(flat(oT_full[:]), OB[:, 0:D], ACT.Copy).then_inc(oT_full_ready, 1)
                        nc.scalar.activation(flat(oT_hi[:]), OB[:, 0:D], ACT.Copy).then_inc(oT_hi_ready, 1)
                run_pairs(act, step, 2)

            @block.vector
            def _(dve):
                n = finish_stats(nc, dve, ln, 0, stats, mean[:], var_eps[:], ln_tmp, LN_EPS)
                dve.wait_ge(w_rounded, 1)
                nc.vector.tensor_tensor(w_lo[:], w_in[:], w_hi[:].bitcast(F32), ALU.subtract).then_inc(w_split, 1)
                dve.wait_ge(ln, n)
                dve.wait_ge(rstd_ready, 1)

                def normalise(b, j):
                    wait(dve, x_transposed, b - 1)
                    nc.vector.tensor_scalar(xn[:, j, :], batch(X, b), one(mean, b), one(rstd, b), ALU.subtract, ALU.mult).then_inc(xn_ready, 1)

                normalise(0, 0)

                def step(s, j):
                    u = s - 2
                    if live(u):
                        dve.wait_ge(scored, u + 1)
                        nc.vector.tensor_reduce(neg_max[:, j:j + 1], SB_[:, 0:2 * 128], AX.X, ALU.max, negate=True).then_inc(max_found, 1)
                        dve.wait_ge(exps_done, u + 1)
                        nc.vector.reciprocal(inv_sum[:, j:j + 1], exp_sum[:, j:j + 1]).then_inc(inv_ready, 1)
                        dve.wait_ge(inv_ready, u + 1)
                        nc.vector.tensor_scalar(flat(P[:]), flat(P[:]), inv_sum[:, j:j + 1], None, ALU.mult).then_inc(probs_ready, 1)
                    if live(s):
                        dve.wait_ge(xT_hi_ready, s + 1)
                        nc.vector.tensor_tensor(flat(xT_lo[:, j]), flat(xT_full[:, j]), flat(xT_hi[:, j]).bitcast(F32), ALU.subtract).then_inc(xT_lo_ready, 1)
                    u = s - 3
                    if live(u):
                        dve.wait_ge(out_projected, u + 1)
                        nc.vector.tensor_tensor(batch(X, u), OUT[:, 0:D], batch(X, u), ALU.add).then_inc(added, 1)
                        dve.wait_ge(added, u + 1)
                        nc.vector.bn_stats(batch(stats, u), batch(X, u))
                    u = s - 2
                    if live(u):
                        dve.wait_ge(oT_hi_ready, u + 1)
                        nc.vector.tensor_tensor(flat(oT_lo[:]), flat(oT_full[:]), flat(oT_hi[:]).bitcast(F32), ALU.subtract).then_inc(oT_lo_ready, 1)
                    if live(s + 1):
                        normalise(s + 1, 1 - j)
                run_pairs(dve, step, 3, peeled=2)

            @block.tensor
            def _(pe):
                def step(s, j):
                    if live(s):
                        pe.wait_ge(xn_ready, s + 1)
                        wait(pe, xT_hi_ready, s)
                        for k in range(KD):
                            ins = nc.tensor.transpose(XB[:, k * 128:(k + 1) * 128], xn[:, j, k * 128:(k + 1) * 128], ident[:])
                        ins.then_inc(x_transposed, 1)
                    u, i = s - 1, 1 - j
                    if live(u):
                        pe.wait_ge(xT_full_ready, u + 1)
                        wait(pe, qk_ready, 2 * u)
                        for w in range(2):
                            for c in range(KD):
                                for k in range(KD):
                                    ins = nc.tensor.matmul(QKB[:, (2 * w + c) * 128:(2 * w + c + 1) * 128], wqk[:, w, k, c * 128:(c + 1) * 128], xT_full[:, i, k, :],
                                                           start=(k == 0), stop=(k == KD - 1))
                        ins.then_inc(qk_projected, 1)
                    u = s - 3
                    if live(u):
                        pe.wait_ge(oT_lo_ready, u + 1)
                        wait(pe, added, u)
                        for k in range(KD):
                            ins = matmul3(nc, OUT[:, 0:D], (oT_hi[:, k, :], oT_lo[:, k, :]), (w_hi[:, 1, k, :], w_lo[:, 1, k, :]),
                                          first=(k == 0), last=(k == KD - 1))
                        ins.then_inc(out_projected, 1)
                    u = s - 2
                    if live(u):
                        pe.wait_ge(probs_ready, u + 1)
                        wait(pe, PT_ready, u)
                        for c in range(2):
                            ins = nc.tensor.transpose(PB[:, c * 128:(c + 1) * 128], P[:, c, :], ident[:])
                        ins.then_inc(p_transposed, 1)
                    u, i = s - 1, 1 - j
                    if live(u):
                        if isinstance(u, int) and u == 0:
                            pe.wait_ge(w_split, 1)
                        pe.wait_ge(xT_lo_ready, u + 1)
                        wait(pe, V_ready, u)
                        for k in range(KD):
                            ins = matmul3(nc, VB[:, 0:D], (xT_hi[:, i, k, :], xT_lo[:, i, k, :]), (w_hi[:, 0, k, :], w_lo[:, 0, k, :]),
                                          first=(k == 0), last=(k == KD - 1))
                        ins.then_inc(v_projected, 1)
                    u = s - 2
                    if live(u):
                        pe.wait_ge(PT_ready, u + 1)
                        pe.wait_ge(V_ready, u + 1)
                        wait(pe, oT_hi_ready, u)
                        for c in range(KD):
                            for k in range(2):
                                ins = nc.tensor.matmul(OB[:, c * 128:(c + 1) * 128], V[:, j, k, c * 128:(c + 1) * 128], PT[:, k, :],
                                                       start=(k == 0), stop=(k == 1))
                        ins.then_inc(weighed, 1)
                    u, i = s - 1, 1 - j
                    if live(u):
                        pe.wait_ge(qk_ready, 2 * u + 2)
                        pe.wait_ge(ctx_loaded[i], 32 * (u // 2 + 1) if isinstance(u, int) else pair_count(s, j, i) * 2)
                        wait(pe, exps_done, u)
                        for c in range(KD):
                            ins = nc.tensor.matmul(SB_[:, 0:2 * 128], qT[:, c, :], kT[:, i, c, :, :].rearrange("p a n -> p (a n)"),
                                                   start=(c == 0), stop=(c == KD - 1))
                        ins.then_inc(scored, 1)
                run_pairs(pe, step, 3, peeled=2)


def phase_moe(nc, a, sem, sb_, bank, X, ident, mean, var_eps, rstd, minus_half, stats, ln_tmp, w, out):
    local = ExitStack()
    with local:
        def sb(name, shape, dt=F32):
            return sb_(name, shape, dt, local)

        E_, LAT, HID, GROUP = 16, 64, 128, 4
        GW = GROUP * S
        NG = B // GROUP
        XT_hi = sb("moe_XT_hi", [128, KD, B * S], F32R)
        XT_lo = sb("moe_XT_lo", [128, KD, B * S], F32R)
        XL = sb("moe_XL", [128, B * S], F32R)
        logits = sb("moe_logits", [128, B, E_])
        gates = sb("moe_gates", [128, B, E_])
        ranked = sb("moe_ranked", [128, B, E_])
        cut = sb("moe_cut", [128, B, E_])
        top = sb("moe_top", [128, B, 8])
        gate_sum = sb("moe_gate_sum", [128, 2, B])
        route_bias = w["moe_route_bias"]
        wg = w["moe_wg"]
        w_in = w["moe_w_in"]
        w_hi = sb("moe_w_hi", [128, 3, KD, 128], F32R)
        w_lo = sb("moe_w_lo", [128, 3, KD, 128], F32R)
        sw2_in = w["moe_sw2"]
        sw2_hi = sb("moe_sw2_hi", [128, D], F32R)
        sw2_lo = sb("moe_sw2_lo", [128, D], F32R)
        wup = w["moe_wup"]
        we2 = w["moe_we2"]
        low_rows = w["moe_low_rows"]
        xn = sb("moe_xn", [128, 2, D])
        xT = sb("moe_xT", [128, 2, KD, 128])
        lat_hi = sb("moe_lat_hi", [128, GW], F32R)
        acc = sb("moe_acc", [128, B, LAT])
        relu = sb("moe_relu", [128, GROUP, GW])
        prod = sb("moe_prod", [128, GROUP, GW])
        hidden = sb("moe_hidden", [128, GROUP, GW])
        y_hi = sb("moe_y_hi", [128, GW], F32R)
        y_lo = sb("moe_y_lo", [128, GW], F32R)

        w_rounded = sem("moe_w_rounded")
        w_split = sem("moe_w_split")
        ln = sem("moe_ln")
        rstd_ready = sem("moe_rstd_ready")
        xn_ready = sem("moe_xn_ready")
        x_transposed = sem("moe_x_transposed")
        xT_ready = sem("moe_xT_ready")
        XT_split = sem("moe_XT_split")
        routed = sem("moe_routed")
        logits_ready = sem("moe_logits_ready")
        chain = sem("moe_chain")
        exp_ready = sem("moe_exp_ready")
        lat_projected = sem("moe_lat_projected")
        lat_rounded = sem("moe_lat_rounded")
        XL_ready = sem("moe_XL_ready")
        up_done = sem("moe_up_done")
        sh_relu = sem("moe_sh_relu")
        sh_prod = sem("moe_sh_prod")
        y_rounded = sem("moe_y_rounded")
        y_split = sem("moe_y_split")
        sh_out = sem("moe_sh_out")
        sh_added = sem("moe_sh_added")
        we_in = sb("moe_we_in", [128, 2, 2, HID])
        we_loaded = [sem("moe_we0"), sem("moe_we1")]

        def load_expert(sp, e, j):
            for w, name in enumerate(("rw1T", "rwgT")):
                src = a[name][e] if isinstance(e, int) else a[name][bass.ds(e, 1)].rearrange("a l n -> (a l) n")
                for half in range(2):
                    sp.dma_start(we_in[half * LAT:(half + 1) * LAT, j, w, :], src).then_inc(we_loaded[j], 16)

        with nc.Block() as block:
            @block.sync
            def _(sp):
                for e in range(2):
                    load_expert(sp, e, e)

            @block.gpsimd
            def _(pool):
                pool.wait_ge(ln, 7)
                nc.gpsimd.tensor_tensor(rstd[:], var_eps[:], minus_half[:], ALU.pow).then_inc(rstd_ready, 1)
                nc.gpsimd.memset(acc[:], 0.0)

            @block.scalar
            def _(act):
                nc.scalar.activation(w_hi[:], w_in[:], ACT.Copy).then_inc(w_rounded, 1)
                nc.scalar.activation(sw2_hi[:], sw2_in[:], ACT.Copy).then_inc(w_rounded, 1)

                def step(s, j):
                    if live(s):
                        act.wait_ge(x_transposed, s + 1)
                        wait(act, routed, s - 1)
                        wait(act, XT_split, 2 * s - 2)
                        nc.scalar.activation(flat(xT[:, j]), bank[j][:, 0:D], ACT.Copy).then_inc(xT_ready, 1)
                run_pairs(act, step, 0)
                act.wait_ge(logits_ready, B)
                nc.scalar.activation(flat(gates[:]), flat(logits[:]), ACT.Exp, scale=-1.0).then_inc(exp_ready, 1)
                for g in range(NG):
                    act.wait_ge(lat_projected, g + 1)
                    wait(act, XL_ready, g)
                    nc.scalar.activation(lat_hi[:], bank[0][:], ACT.Copy).then_inc(lat_rounded, 1)
                    act.wait_ge(up_done, g + 1)
                    wait(act, sh_prod, 2 * g)
                    nc.scalar.activation(relu[:, 0, :], bank[2][:], ACT.Relu).then_inc(sh_relu, 1)
                    act.wait_ge(sh_prod, 2 * g + 2)
                    wait(act, sh_out, g)
                    nc.scalar.activation(y_hi[:], hidden[:, 0, :], ACT.Copy).then_inc(y_rounded, 1)

            @block.vector
            def _(dve):
                count = [0]

                def link(ins):
                    count[0] += 1
                    ins.then_inc(chain, 1)
                    dve.wait_ge(chain, count[0])

                TT, TS = nc.vector.tensor_tensor, nc.vector.tensor_scalar
                n = finish_stats(nc, dve, ln, 0, stats, mean[:], var_eps[:], ln_tmp, LN_EPS)
                dve.wait_ge(w_rounded, 2)
                TT(w_lo[:], w_in[:], w_hi[:].bitcast(F32), ALU.subtract).then_inc(w_split, 1)
                TT(sw2_lo[:], sw2_in[:], sw2_hi[:].bitcast(F32), ALU.subtract).then_inc(w_split, 1)
                dve.wait_ge(ln, n)
                dve.wait_ge(rstd_ready, 1)

                def normalise(b, j):
                    wait(dve, x_transposed, b - 1)
                    TS(xn[:, j, :], batch(X, b), one(mean, b), one(rstd, b), ALU.subtract, ALU.mult).then_inc(xn_ready, 1)

                normalise(0, 0)

                def step(s, j):
                    if live(s + 1):
                        normalise(s + 1, 1 - j)
                    if live(s):
                        dve.wait_ge(xT_ready, s + 1)
                        at = slice(s * S, (s + 1) * S) if isinstance(s, int) else bass.ds(s * S, S)
                        TS(XT_hi[:, :, at], xT[:, j], 1.0, None, ALU.mult).then_inc(XT_split, 1)
                        dve.wait_ge(XT_split, 2 * s + 1)
                        TT(XT_lo[:, :, at], xT[:, j], XT_hi[:, :, at].bitcast(F32), ALU.subtract).then_inc(XT_split, 1)
                    if live(s - 1):
                        dve.wait_ge(routed, s)
                        TS(batch(logits, s - 1), bank[3 - j][:, 0:E_], 1.0, None, ALU.mult).then_inc(logits_ready, 1)
                run_pairs(dve, step, 1)

                def router(part):
                    if part == 0:
                        dve.wait_ge(exp_ready, 1)
                        link(TS(gates[:], gates[:], 1.0, None, ALU.add))
                        link(nc.vector.reciprocal(gates[:], gates[:]))
                        link(TT(ranked[:], gates[:], route_bias[:].rearrange("p (a n) -> p a n", a=1).broadcast_to([128, B, E_]), ALU.add))
                    if part == 1:
                        for b in range(B):
                            ins = nc.vector.max(top[:, b, :], ranked[:, b, :])
                        link(ins)
                    if part == 2:
                        for b in range(B):
                            ins = nc.vector.match_replace(cut[:, b, :], top[:, b, :], ranked[:, b, :], -1e30)
                        link(ins)
                    if part == 3:
                        link(TT(cut[:], cut[:], ranked[:], ALU.not_equal))
                        link(TT(gates[:], gates[:], cut[:], ALU.mult))
                        link(nc.vector.tensor_reduce(gate_sum[:, 0, :], gates[:], AX.X, ALU.add))
                        link(nc.vector.reciprocal(gate_sum[:, 1, :], gate_sum[:, 0, :]))
                        link(TS(gate_sum[:, 1, :], gate_sum[:, 1, :], 2.5, None, ALU.mult))
                        link(TT(gates[:], gates[:], gate_sum[:, 1, :].rearrange("p (b n) -> p b n", n=1).broadcast_to([128, B, E_]), ALU.mult))

                def add_shared(g):
                    dve.wait_ge(sh_out, g + 1)
                    for i in range(2):
                        rows = X[:, g * GROUP + 2 * i:g * GROUP + 2 * i + 2, :].rearrange("p b n -> p (b n)")
                        TT(rows, bank[4 + i][:], rows, ALU.add).then_inc(sh_added, 1)

                for g in range(NG):
                    dve.wait_ge(lat_rounded, g + 1)
                    nc.vector.scalar_tensor_tensor(XL[:, g * GW:(g + 1) * GW], lat_hi[:].bitcast(F32), low_rows[:, 0:1], bank[0][:],
                                                   ALU.mult, ALU.add).then_inc(XL_ready, 1)
                    dve.wait_ge(sh_relu, g + 1)
                    TT(prod[:, 0, :], bank[1][:], relu[:, 0, :], ALU.mult).then_inc(sh_prod, 1)
                    dve.wait_ge(sh_prod, 2 * g + 1)
                    wait(dve, y_split, g)
                    TT(hidden[:, 0, :], prod[:, 0, :], relu[:, 0, :], ALU.mult).then_inc(sh_prod, 1)
                    router(g)
                    if g > 0:
                        add_shared(g - 1)
                    dve.wait_ge(y_rounded, g + 1)
                    wait(dve, sh_out, g)
                    TT(y_lo[:], hidden[:, 0, :], y_hi[:].bitcast(F32), ALU.subtract).then_inc(y_split, 1)

                add_shared(NG - 1)

            @block.tensor
            def _(pe):
                def step(s, j):
                    if live(s):
                        pe.wait_ge(xn_ready, s + 1)
                        wait(pe, xT_ready, s - 1)
                        for k in range(KD):
                            ins = nc.tensor.transpose(bank[j][:, k * 128:(k + 1) * 128], xn[:, j, k * 128:(k + 1) * 128], ident[:])
                        ins.then_inc(x_transposed, 1)
                    u, i = s - 1, 1 - j
                    if live(u):
                        pe.wait_ge(xT_ready, u + 1)
                        wait(pe, logits_ready, u - 1)
                        for k in range(KD):
                            ins = nc.tensor.matmul(bank[2 + i][:, 0:E_], xT[:, i, k, :], wg[:, k, :], start=(k == 0), stop=(k == KD - 1))
                        ins.then_inc(routed, 1)
                run_pairs(pe, step, 1)

                pe.wait_ge(w_split, 2)
                pe.wait_ge(XT_split, 2 * B)
                pe.wait_ge(logits_ready, B)

                def up(dst, w, g):
                    for k in range(KD):
                        at = slice(g * GW, (g + 1) * GW)
                        ins = matmul3(nc, dst[:], (w_hi[:, w, k, :], w_lo[:, w, k, :]), (XT_hi[:, k, at], XT_lo[:, k, at]),
                                      first=(k == 0), last=(k == KD - 1))
                    return ins

                def ups(g):
                    wait(pe, XL_ready, g)
                    up(bank[0], 0, g).then_inc(lat_projected, 1)
                    wait(pe, sh_prod, 2 * g - 1)
                    up(bank[2], 2, g)
                    up(bank[1], 1, g).then_inc(up_done, 1)

                ups(0)
                for g in range(NG):
                    if g + 1 < NG:
                        ups(g + 1)
                    pe.wait_ge(y_split, g + 1)
                    wait(pe, sh_added, 2 * g)
                    for i in range(GROUP):
                        tok = slice(i * S, (i + 1) * S)
                        ins = matmul3(nc, bank[4 + i // 2][:, (i % 2) * D:(i % 2 + 1) * D], (y_hi[:, tok], y_lo[:, tok]), (sw2_hi[:], sw2_lo[:]), True, True)
                    ins.then_inc(sh_out, 1)

        we_hi = sb("moe_we_hi", [128, 2, 2, HID], F32R)
        we_lo = sb("moe_we_lo", [128, 2, 2, HID], F32R)
        gate_of = sb("moe_gate_of", [128, 2, B])
        we_rounded = sem("moe_we_rounded")
        we_split = sem("moe_we_split")
        gate_copied = sem("moe_gate_copied")
        ups_done = sem("moe_ups_done")
        relu_done = sem("moe_relu_done")
        prod_done = sem("moe_prod_done")
        hidden_done = sem("moe_hidden_done")
        downs_done = sem("moe_downs_done")
        acc_added = sem("moe_acc_added")
        STEPS = E_ * NG

        def run(eng, step, extra):
            for e in range(2):
                for g in range(NG):
                    step(e * NG + g, g, e, e)
            with eng.Fori(1, E_ // 2 - 1) as i:
                for j in range(2):
                    for g in range(NG):
                        step(i * 8 + 4 * j + g, g, i * 2 + j, j)
            for e in range(E_ - 2, E_):
                for g in range(NG):
                    step(e * NG + g, g, e, e % 2)
            for g in range(extra):
                step(STEPS + g, g, E_, 0)

        with nc.Block() as block:
            @block.sync
            def _(sp):
                with sp.Fori(1, E_ // 2) as i:
                    for j in range(2):
                        sp.wait_ge(we_split, i * 2 + (j - 1))
                        load_expert(sp, i * 2 + j, j)

            @block.scalar
            def _(act):
                def round_weights(e, j, n):
                    act.wait_ge(we_loaded[j], n)
                    wait(act, ups_done, 4 * (e - 1))
                    nc.scalar.activation(we_hi[:, j], we_in[:, j], ACT.Copy).then_inc(we_rounded, 1)

                round_weights(0, 0, 64)

                def step(t, g, e, j):
                    if live(t, STEPS):
                        act.wait_ge(ups_done, t + 1)
                        wait(act, hidden_done, t - 3)
                        nc.scalar.activation(relu[:, g, :], bank[2 + g % 2][:], ACT.Relu).then_inc(relu_done, 1)
                    if g == 0 and live(e + 1, E_):
                        round_weights(e + 1, 1 - j, 64 * ((e + 1) // 2 + 1) if isinstance(e, int) else pair_count(e, j, 1 - j, 1) * 4)
                run(act, step, 0)

            @block.gpsimd
            def _(pool):
                def step(t, g, e, j):
                    pool.wait_ge(prod_done, t + 1)
                    wait(pool, downs_done, t - 3)
                    nc.gpsimd.tensor_tensor(hidden[:, g, :], prod[:, g, :], relu[:, g, :], ALU.mult).then_inc(hidden_done, 1)
                run(pool, step, 0)

            @block.vector
            def _(dve):
                def split_weights(e, j):
                    dve.wait_ge(we_rounded, e + 1)
                    wait(dve, ups_done, 4 * (e - 1))
                    nc.vector.tensor_tensor(we_lo[:, j], we_in[:, j], we_hi[:, j].bitcast(F32), ALU.subtract).then_inc(we_split, 1)

                def copy_gates(e, j):
                    src = gates[:, :, e:e + 1] if isinstance(e, int) else gates[:, :, bass.ds(e, 1)]
                    wait(dve, acc_added, 4 * (e - 1))
                    nc.vector.tensor_scalar(gate_of[:, j, :], src.rearrange("p b a -> p (b a)"), 1.0, None, ALU.mult).then_inc(gate_copied, 1)

                split_weights(0, 0)
                copy_gates(0, 0)

                def step(t, g, e, j):
                    if live(t, STEPS):
                        dve.wait_ge(relu_done, t + 1)
                        wait(dve, hidden_done, t - 3)
                        nc.vector.tensor_tensor(prod[:, g, :], bank[g % 2][:], relu[:, g, :], ALU.mult).then_inc(prod_done, 1)
                    u, ug = t - 3, (g + 1) % 4
                    if live(u, STEPS):
                        uj = j if g >= 3 else 1 - j
                        dve.wait_ge(downs_done, u + 1)
                        if ug == 0:
                            dve.wait_ge(gate_copied, e + 1)
                        wait(dve, acc_added, u - 3)
                        for i in range(GROUP):
                            b = ug * GROUP + i
                            ins = nc.vector.scalar_tensor_tensor(acc[:, b, :], bank[4 + ug][:, i * LAT:(i + 1) * LAT], gate_of[:, uj, b:b + 1], acc[:, b, :],
                                                                 ALU.mult, ALU.add)
                        ins.then_inc(acc_added, 1)
                    if g == 1 and live(e + 1, E_):
                        split_weights(e + 1, 1 - j)
                    if g == 2 and live(e + 1, E_):
                        copy_gates(e + 1, 1 - j)
                run(dve, step, 3)

            @block.tensor
            def _(pe):
                def step(t, g, e, j):
                    if live(t, STEPS):
                        if g == 0:
                            pe.wait_ge(we_split, e + 1)
                        wait(pe, prod_done, t - 1)
                        wait(pe, relu_done, t - 1)
                        toks = XL[:, g * GW:(g + 1) * GW]
                        for w in (1, 0):
                            nc.tensor.matmul(bank[2 * w + g % 2][:], we_hi[:, j, w, :], toks, start=True, stop=False)
                            ins = nc.tensor.matmul(bank[2 * w + g % 2][:], we_lo[:, j, w, :], toks, start=False, stop=True)
                        ins.then_inc(ups_done, 1)
                    u, ug = t - 2, (g + 2) % 4
                    if live(u, STEPS):
                        ue = e if g >= 2 else e - 1
                        w2 = we2[:, ue, :] if isinstance(ue, int) else we2[:, bass.ds(ue, 1), :].rearrange("p a l -> p (a l)")
                        pe.wait_ge(hidden_done, u + 1)
                        wait(pe, acc_added, u - 3)
                        for i in range(GROUP):
                            ins = nc.tensor.matmul(bank[4 + ug][:, i * LAT:(i + 1) * LAT], hidden[:, ug, i * S:(i + 1) * S], w2, start=True, stop=True)
                        ins.then_inc(downs_done, 1)
                run(pe, step, 2)

        accT = sb("moe_accT", [128, 2, 128])
        acc_transposed = sem("moe_acc_transposed")
        accT_ready = sem("moe_accT_ready")
        upped = sem("moe_upped")
        result_ready = sem("moe_result_ready")
        stored = sem("moe_stored")
        PAIRS = B // 2
        with nc.Block() as block:
            @block.tensor
            def _(pe):
                for p in range(PAIRS + 1):
                    if p < PAIRS:
                        wait(pe, accT_ready, p - 1)
                        nc.tensor.transpose(bank[p % 2][:, 0:128], acc[:, 2 * p:2 * p + 2, :].rearrange("p b n -> p (b n)"), ident[:]).then_inc(acc_transposed, 1)
                    u = p - 1
                    if u >= 0:
                        pe.wait_ge(accT_ready, u + 1)
                        wait(pe, result_ready, 2 * (u - 1))
                        for i in range(2):
                            rows = slice(i * LAT, (i + 1) * LAT)
                            nc.tensor.matmul(bank[2 + 2 * (u % 2) + i][:, 0:D], accT[rows, u % 2, :], wup[rows, :], start=True, stop=True).then_inc(upped, 1)

            @block.scalar
            def _(act):
                for p in range(PAIRS):
                    act.wait_ge(acc_transposed, p + 1)
                    wait(act, upped, 2 * (p - 1))
                    nc.scalar.activation(accT[:, p % 2, :], bank[p % 2][:, 0:128], ACT.Copy).then_inc(accT_ready, 1)

            @block.vector
            def _(dve):
                for b in range(B):
                    dve.wait_ge(upped, b + 1)
                    nc.vector.tensor_tensor(X[:, b, :], bank[2 + b % 4][:, 0:D], X[:, b, :], ALU.add).then_inc(result_ready, 1)

            @block.sync
            def _(sp):
                for g in range(NG):
                    done = slice(g * GROUP, (g + 1) * GROUP)
                    sp.wait_ge(result_ready, (g + 1) * GROUP)
                    sp.dma_start(out[done].rearrange("b p d -> p b d"), X[:, done, :]).then_inc(stored, 16)
                sp.wait_ge(stored, 16 * NG)


def weights_ahead(a, sb):
    chunks = lambda name: a[name].rearrange("(k p) n -> p k n", p=128)
    w = {name: sb(name, shape) for name, shape in (
        ("sp_gb", [128, 2, D]), ("sp_slopes", [128, D, 16]), ("sp_rank", [128, 89]), ("sp_table", [64, 129]),
        ("win_wqk", [128, KD, 2 * D]), ("win_w_in", [128, 2, KD, D]), ("win_band_in", [128, 128]), ("win_parity", [128, 2]),
        ("cr_wqk", [128, 2, KD, D]), ("cr_w_in", [128, 2, KD, D]),
        ("moe_wg", [128, KD, 16]), ("moe_w_in", [128, 3, KD, 128]), ("moe_sw2", [128, D]), ("moe_wup", [128, D]),
        ("moe_we2", [128, 16, 64]), ("moe_route_bias", [128, 16]), ("moe_low_rows", [128, 1]))}
    qkv = chunks("w_qkvT")
    row = lambda name: a[name].rearrange("(a n) -> a n", a=1).broadcast_to([128, D])
    transfers = [
        (w["sp_gb"][:, 0, :], row("L0_ffn_ln_gamma")), (w["sp_gb"][:, 1, :], row("L0_ffn_ln_beta")),
        (w["sp_slopes"][:].rearrange("p d g -> p (d g)"), a["L0_ffn_spline_slopes"].rearrange("(a t) j g -> a (t j g)", a=1).broadcast_to([128, D * 16])),
        (w["sp_rank"][:], a["rank"]),
        (w["sp_table"][:, 0:64], a["L0_ffn_spline_bases"].rearrange("t j g -> t (j g)")),
        (w["sp_table"][:, 64:128], a["L0_ffn_spline_slopes"].rearrange("t j g -> t (j g)")),
        (w["sp_table"][:, 128:129], a["L0_ffn_output_scale"].rearrange("(t a) -> t a", a=1)),
        (w["win_wqk"][:], qkv[:, :, 0:2 * D]), (w["win_w_in"][:, 0], qkv[:, :, 2 * D:3 * D]), (w["win_w_in"][:, 1], chunks("w_outT")),
        (w["win_band_in"][:], a["band"]), (w["win_parity"][:], a["parity"]),
        (w["cr_wqk"][:, 0], chunks("x_wqT")), (w["cr_wqk"][:, 1], chunks("x_wkT")),
        (w["cr_w_in"][:, 0], chunks("x_wvT")), (w["cr_w_in"][:, 1], chunks("x_woT")),
        (w["moe_wg"][:], chunks("WgT")), (w["moe_w_in"][:, 0, :, 0:64], chunks("WdownT")), (w["moe_w_in"][:, 0, :, 64:], chunks("WdownT")),
        (w["moe_w_in"][:, 1], chunks("sw1T")), (w["moe_w_in"][:, 2], chunks("swgT")), (w["moe_sw2"][:], a["sw2T"]), (w["moe_wup"][0:64], a["WupT"]), (w["moe_wup"][64:128], a["WupT"]),
        (w["moe_we2"][:], a["rw2T"].rearrange("e h l -> h e l")),
        (w["moe_route_bias"][:], a["L1_ffn_biases"].rearrange("(a n) -> a n", a=1).broadcast_to([128, 16])),
        (w["moe_low_rows"][:], a["low_rows"])]
    return w, transfers


def phase_rest(nc, a, sem, sb, bank, X, ident, mean, var_eps, rstd, minus_half, stats, ln_tmp, out, clear_semaphores):
    t = (nc, a, sem, sb, bank, X, ident, mean, var_eps, rstd, minus_half, stats, ln_tmp)
    w, transfers = weights_ahead(a, sb)
    ahead_loaded = sem("ahead_loaded")
    phase_retention(*t, transfers, ahead_loaded)
    phase_spline(*t, w, ahead_loaded, 16 * len(transfers))
    phase_window(*t, w, ahead_loaded, 16 * len(transfers))
    phase_cross(*t, w)
    clear_semaphores()
    phase_moe(*t, w, out)


INPUTS = ["x", "L0_attn_bo", "L0_xattn_Wh", "L0_xattn_wg_w", "L0_xattn_wo_w",
          "L0_xattn_gn_gamma", "L0_xattn_gn_beta", "L0_ffn_ln_gamma", "L0_ffn_ln_beta", "L0_ffn_spline_bases",
          "L0_ffn_spline_slopes", "L0_ffn_output_scale", "ctx_2048", "L1_ffn_biases"]


def kernel(**inputs):
    import concourse.bacc as bacc
    from concourse.bass_utils import run_bass_kernel_spmd

    f32 = np.float32
    arrays = {n: np.ascontiguousarray(inputs[n]) for n in INPUTS}
    for name, src in (("wqT", "L0_attn_wq"), ("wkT", "L0_attn_wk"), ("wvT", "L0_attn_wv"), ("woT", "L0_attn_wo")):
        arrays[name] = np.ascontiguousarray(np.asarray(inputs[src]).T)
    for name, src in (("ln_gT", "L0_attn_ln_g"), ("ln_bT", "L0_attn_ln_b"), ("bvT", "L0_attn_bv"),
                      ("bqT", "L0_attn_bq"), ("bkT", "L0_attn_bk")):
        arrays[name] = np.ascontiguousarray(np.asarray(inputs[src]).reshape(-1, 128).T)
    for name in ("bqT", "bkT"):
        arrays[name + "_rot"] = np.roll(arrays[name], 64, axis=0)
    arrays["ctxT"] = np.ascontiguousarray(np.asarray(inputs["ctx_2048"]).reshape(B * S, D).T)
    arrays["w_qkvT"] = np.ascontiguousarray(np.asarray(inputs["L1_attn_w_qkv"]).T)
    arrays["w_outT"] = np.ascontiguousarray(np.asarray(inputs["L1_attn_w_out"]).T)
    for name, src in (("x_wqT", "L1_xattn_wq"), ("x_wkT", "L1_xattn_wk"), ("x_wvT", "L1_xattn_wv"), ("x_woT", "L1_xattn_wo"),
                      ("WgT", "L1_ffn_Wg"), ("WdownT", "L1_ffn_Wdown"), ("sw1T", "L1_ffn_sw1"), ("swgT", "L1_ffn_swg"),
                      ("sw2T", "L1_ffn_sw2"), ("WupT", "L1_ffn_Wup")):
        arrays[name] = np.ascontiguousarray(np.asarray(inputs[src]).T)
    for name, src in (("rw1T", "L1_ffn_rw1"), ("rwgT", "L1_ffn_rwg"), ("rw2T", "L1_ffn_rw2")):
        arrays[name] = np.ascontiguousarray(np.asarray(inputs[src]).transpose(0, 2, 1))
    arrays["WhT"] = np.ascontiguousarray(np.asarray(inputs["L0_xattn_Wh"]).transpose(2, 0, 1))
    theta = (f32(1.0) / np.power(f32(10000.0), np.arange(0, DK0, 2, dtype=f32) / f32(DK0))).astype(f32)
    freqs = np.arange(S, dtype=f32)[:, None] * theta[None, :]
    cos, sin = np.cos(freqs).astype(f32), np.sin(freqs).astype(f32)
    cosT = np.ascontiguousarray(np.concatenate([cos, cos], axis=1).T)
    sinT = np.ascontiguousarray(np.concatenate([-sin, sin], axis=1).T)
    scale = f32(1.0 / np.sqrt(DK0))
    arrays.update(cosT_k=cosT, sinT_k=sinT, cosT_q=cosT * scale, sinT_q=sinT * scale)
    arrays["ident"] = np.eye(128, dtype=f32)
    row, col = np.arange(128)[:, None], np.arange(128)[None, :]
    arrays["causal"] = np.where(col <= row, f32(0), f32(MASKED)).astype(f32)
    gamma = (f32(1.0) - f32(2.0) ** (f32(-5.0) - np.arange(2, dtype=f32))).astype(f32)
    expo = np.arange(S, dtype=f32)[None, :] - np.arange(S, dtype=f32)[:, None]
    with np.errstate(over="ignore"):
        dec = np.where(expo[None] <= 0, gamma[:, None, None] ** expo[None], f32(0)).astype(f32)
    dec = dec / np.sqrt(dec.sum(axis=-1, dtype=f32))[:, None, :]
    arrays["decayT"] = np.ascontiguousarray((dec / np.sqrt(f32(128.0))).astype(f32).transpose(2, 0, 1))
    arrays["band"] = np.where((col <= row) & (col >= row - 64), f32(0), f32(MASKED)).astype(f32)
    head = np.arange(128) // 16
    arrays["parity"] = np.stack([head % 2 == 0, head % 2 == 1], axis=1).astype(f32)
    arrays["low_rows"] = np.where(np.arange(128)[:, None] < 64, f32(0), f32(-1)).astype(f32)
    ranks = np.concatenate([np.arange(63, -1, -1), np.arange(7, -1, -1), np.arange(17)]).astype(f32)
    arrays["rank"] = np.tile(ranks, (128, 1))
    nc = bacc.Bacc("TRN2", target_bir_lowering=False, num_devices=1)
    aps = {n: nc.dram_tensor(f"in_{n}", v.shape, mybir.dt.from_np(v.dtype), kind="ExternalInput").ap() for n, v in arrays.items()}
    out = nc.dram_tensor("out", (B, S, D), F32, kind="ExternalOutput").ap()
    decoder_kernel(nc, aps, out)
    result = run_bass_kernel_spmd(nc, [{f"in_{n}": v for n, v in arrays.items()}], core_ids=[0])
    return result.results[0]["out"]
```
